# Optimizing a Trainium2 kernel written in Bass

```python
import numpy as np
import jax
import jax.numpy as jnp

def _softmax(x, axis=-1):
    return jax.nn.softmax(x, axis=axis)

def _gelu(x):
    return jax.nn.gelu(x, approximate=True)

def _silu(x):
    return jax.nn.silu(x)

def _sigmoid(x):
    return jax.nn.sigmoid(x)

def _layernorm(x, axis=-1, eps=1e-05):
    m = jnp.mean(x, axis=axis, keepdims=True)
    v = jnp.var(x, axis=axis, keepdims=True)
    return (x - m) / jnp.sqrt(v + eps)

def _scatter_add(tgt, idx, src, axis=0):
    return tgt.at[idx].add(src)

def _segment_sum(src, seg, n):
    return jax.ops.segment_sum(src, seg, n)
kernel_name = 'mk_gnn_resnorm_d2_gnn_r32_8f750e'

def setup_inputs(seed: int=0):
    np.random.seed(seed)
    _w = jnp.asarray

    def _rec_inputs():
        import jax
        import jax.numpy as jnp
        _gk = jax.random.key(seed)
        x = -0.000202 + 1 * jax.random.normal(jax.random.fold_in(_gk, 1), (3125, 64), jnp.float32)
        _s = jax.random.randint(jax.random.fold_in(_gk, 2), (50000,), 0, 3125, jnp.int32)
        _d = jax.random.randint(jax.random.fold_in(_gk, 3), (50000,), 0, 3125, jnp.int32)
        _loop = jnp.arange(3125, dtype=jnp.int32)
        src = jnp.concatenate([_s, _d, _loop])
        dst = jnp.concatenate([_d, _s, _loop])
        _o = jnp.argsort(dst, stable=True)
        src = src[_o]
        dst = dst[_o]
        return (x, src, dst)
    x, src, dst = _rec_inputs()

    def _L0_gnn_setup():
        import jax, jax.numpy as jnp
        import numpy as np
        N_NODES = 3125
        N_EDGES = 50000
        D = 64
        N_LAYERS = 3

        def _sage_conv(x, src, dst, Wl, Wr, b, n_nodes):
            msgs = x[src]
            summed = jax.ops.segment_sum(msgs, dst, num_segments=n_nodes)
            cnt = jax.ops.segment_sum(jnp.ones(src.shape[0], x.dtype), dst, num_segments=n_nodes)
            agg = summed / jnp.maximum(cnt, 1.0)[:, None]
            return agg @ Wl + x @ Wr + b
        key = jax.random.key(seed)
        k1, k2, k3, k4 = jax.random.split(key, 4)
        x = jax.random.normal(k1, (N_NODES, D), dtype=jnp.float32)
        edge_index = jax.random.randint(k2, (2, N_EDGES), 0, N_NODES, dtype=jnp.int64)
        scale = 1.0 / np.sqrt(D)
        Wl = jax.random.normal(k3, (N_LAYERS, D, D), dtype=jnp.float32) * scale
        Wr = jax.random.normal(k4, (N_LAYERS, D, D), dtype=jnp.float32) * scale
        b = jnp.zeros((N_LAYERS, D), dtype=jnp.float32)
        return {'x': x, 'edge_index': edge_index, 'Wl': Wl, 'Wr': Wr, 'b': b}
    _L0_gnn_all = _L0_gnn_setup()
    _L0_gnn_in = {k: v for k, v in _L0_gnn_all.items() if k in ('Wl', 'Wr', 'b')}
    del _L0_gnn_all

    def _L1_gnn_setup():
        import jax, jax.numpy as jnp
        import numpy as np
        N, E, L, HEADS, HID = (50000, 18750, 4, 8, 128)
        IN_C, OUT_C = (64, 64)
        D_HEAD = HID // HEADS

        def _layer_norm(x, g, b, eps=1e-05):
            m = jnp.mean(x, axis=-1, keepdims=True)
            v = jnp.mean((x - m) ** 2, axis=-1, keepdims=True)
            return (x - m) * jax.lax.rsqrt(v + eps) * g + b

        def _transformer_conv(h, src, dst, Wq, bq, Wk, bk, Wv, bv, Ws, bs, Wbeta):
            n, f = h.shape
            q = (h @ Wq.T + bq)[dst].reshape(-1, HEADS, D_HEAD)
            k = (h @ Wk.T + bk)[src].reshape(-1, HEADS, D_HEAD)
            v = (h @ Wv.T + bv)[src].reshape(-1, HEADS, D_HEAD)
            alpha = jnp.sum(q * k, axis=-1) / float(np.sqrt(D_HEAD))
            amax = jax.ops.segment_max(alpha, dst, num_segments=n)
            ex = jnp.exp(alpha - amax[dst])
            denom = jax.ops.segment_sum(ex, dst, num_segments=n)
            a = ex / (denom[dst] + 1e-16)
            out = jax.ops.segment_sum((a[:, :, None] * v).reshape(-1, f), dst, num_segments=n)
            x_r = h @ Ws.T + bs
            beta = jax.nn.sigmoid(jnp.concatenate([out, x_r, out - x_r], axis=-1) @ Wbeta.T)
            return beta * x_r + (1.0 - beta) * out

        def _forward(x, src, dst, Wi, bi, Wq, bq, Wk, bk, Wv, bv, Ws, bs, Wbeta, ln_g, ln_b, W1, b1, W2, b2, Wo, bo):
            h = jax.nn.gelu(x @ Wi.T + bi, approximate=False)
            for i in range(L):
                res = h
                h = _transformer_conv(h, src, dst, Wq[i], bq[i], Wk[i], bk[i], Wv[i], bv[i], Ws[i], bs[i], Wbeta[i])
                h = _layer_norm(h + res, ln_g[i], ln_b[i])
                res = h
                f = jax.nn.gelu(h @ W1[i].T + b1[i], approximate=False) @ W2[i].T + b2[i]
                h = f + res
            return h @ Wo.T + bo
        key = jax.random.key(seed)
        ks = jax.random.split(key, 24)
        rn = lambda k, shp, s=0.05: jax.random.normal(k, shp, jnp.float32) * s
        x = jax.random.normal(ks[0], (N, IN_C), jnp.float32)
        edge_index = jax.random.randint(ks[1], (2, E), 0, N, dtype=jnp.int64)
        return {'x': x, 'edge_index': edge_index, 'Wi': rn(ks[2], (HID, IN_C)), 'bi': jnp.zeros((HID,), jnp.float32), 'Wq': rn(ks[3], (L, HID, HID)), 'bq': jnp.zeros((L, HID), jnp.float32), 'Wk': rn(ks[4], (L, HID, HID)), 'bk': jnp.zeros((L, HID), jnp.float32), 'Wv': rn(ks[5], (L, HID, HID)), 'bv': jnp.zeros((L, HID), jnp.float32), 'Ws': rn(ks[6], (L, HID, HID)), 'bs': jnp.zeros((L, HID), jnp.float32), 'Wbeta': rn(ks[7], (L, 1, 3 * HID)), 'ln_g': jnp.ones((L, HID), jnp.float32), 'ln_b': jnp.zeros((L, HID), jnp.float32), 'W1': rn(ks[8], (L, 4 * HID, HID)), 'b1': jnp.zeros((L, 4 * HID), jnp.float32), 'W2': rn(ks[9], (L, HID, 4 * HID)), 'b2': jnp.zeros((L, HID), jnp.float32), 'Wo': rn(ks[10], (OUT_C, HID)), 'bo': jnp.zeros((OUT_C,), jnp.float32)}
    _L1_gnn_all = _L1_gnn_setup()
    _L1_gnn_in = {k: v for k, v in _L1_gnn_all.items() if k in ('Wi', 'bi', 'Wq', 'bq', 'Wk', 'bk', 'Wv', 'bv', 'Ws', 'bs', 'Wbeta', 'ln_g', 'ln_b', 'W1', 'b1', 'W2', 'b2', 'Wo', 'bo')}
    del _L1_gnn_all
    return {'x': x, 'src': src, 'dst': dst, 'L0_gnn_Wl': _L0_gnn_in['Wl'], 'L0_gnn_Wr': _L0_gnn_in['Wr'], 'L0_gnn_b': _L0_gnn_in['b'], 'L1_gnn_Wi': _L1_gnn_in['Wi'], 'L1_gnn_bi': _L1_gnn_in['bi'], 'L1_gnn_Wq': _L1_gnn_in['Wq'], 'L1_gnn_bq': _L1_gnn_in['bq'], 'L1_gnn_Wk': _L1_gnn_in['Wk'], 'L1_gnn_bk': _L1_gnn_in['bk'], 'L1_gnn_Wv': _L1_gnn_in['Wv'], 'L1_gnn_bv': _L1_gnn_in['bv'], 'L1_gnn_Ws': _L1_gnn_in['Ws'], 'L1_gnn_bs': _L1_gnn_in['bs'], 'L1_gnn_Wbeta': _L1_gnn_in['Wbeta'], 'L1_gnn_ln_g': _L1_gnn_in['ln_g'], 'L1_gnn_ln_b': _L1_gnn_in['ln_b'], 'L1_gnn_W1': _L1_gnn_in['W1'], 'L1_gnn_b1': _L1_gnn_in['b1'], 'L1_gnn_W2': _L1_gnn_in['W2'], 'L1_gnn_b2': _L1_gnn_in['b2'], 'L1_gnn_Wo': _L1_gnn_in['Wo'], 'L1_gnn_bo': _L1_gnn_in['bo']}

def reference(x, src, dst, L0_gnn_Wl, L0_gnn_Wr, L0_gnn_b, L1_gnn_Wi, L1_gnn_bi, L1_gnn_Wq, L1_gnn_bq, L1_gnn_Wk, L1_gnn_bk, L1_gnn_Wv, L1_gnn_bv, L1_gnn_Ws, L1_gnn_bs, L1_gnn_Wbeta, L1_gnn_ln_g, L1_gnn_ln_b, L1_gnn_W1, L1_gnn_b1, L1_gnn_W2, L1_gnn_b2, L1_gnn_Wo, L1_gnn_bo):
    import jax
    import jax.numpy as jnp

    def _L0_gnn_ref(x, edge_index, Wl, Wr, b):
        import jax, jax.numpy as jnp
        import numpy as np
        N_NODES = 3125
        N_EDGES = 50000
        D = 64
        N_LAYERS = 3

        def _sage_conv(x, src, dst, Wl, Wr, b, n_nodes):
            msgs = x[src]
            summed = jax.ops.segment_sum(msgs, dst, num_segments=n_nodes)
            cnt = jax.ops.segment_sum(jnp.ones(src.shape[0], x.dtype), dst, num_segments=n_nodes)
            agg = summed / jnp.maximum(cnt, 1.0)[:, None]
            return agg @ Wl + x @ Wr + b
        src, dst = (edge_index[0], edge_index[1])
        n = x.shape[0]
        h = x
        for i in range(N_LAYERS - 1):
            h = _sage_conv(h, src, dst, Wl[i], Wr[i], b[i], n)
            h = jax.nn.relu(h)
        h = _sage_conv(h, src, dst, Wl[-1], Wr[-1], b[-1], n)
        return h

    def _L1_gnn_ref(x, edge_index, Wi, bi, Wq, bq, Wk, bk, Wv, bv, Ws, bs, Wbeta, ln_g, ln_b, W1, b1, W2, b2, Wo, bo):
        import jax, jax.numpy as jnp
        import numpy as np
        N, E, L, HEADS, HID = (50000, 18750, 4, 8, 128)
        IN_C, OUT_C = (64, 64)
        D_HEAD = HID // HEADS

        def _layer_norm(x, g, b, eps=1e-05):
            m = jnp.mean(x, axis=-1, keepdims=True)
            v = jnp.mean((x - m) ** 2, axis=-1, keepdims=True)
            return (x - m) * jax.lax.rsqrt(v + eps) * g + b

        def _transformer_conv(h, src, dst, Wq, bq, Wk, bk, Wv, bv, Ws, bs, Wbeta):
            n, f = h.shape
            q = (h @ Wq.T + bq)[dst].reshape(-1, HEADS, D_HEAD)
            k = (h @ Wk.T + bk)[src].reshape(-1, HEADS, D_HEAD)
            v = (h @ Wv.T + bv)[src].reshape(-1, HEADS, D_HEAD)
            alpha = jnp.sum(q * k, axis=-1) / float(np.sqrt(D_HEAD))
            amax = jax.ops.segment_max(alpha, dst, num_segments=n)
            ex = jnp.exp(alpha - amax[dst])
            denom = jax.ops.segment_sum(ex, dst, num_segments=n)
            a = ex / (denom[dst] + 1e-16)
            out = jax.ops.segment_sum((a[:, :, None] * v).reshape(-1, f), dst, num_segments=n)
            x_r = h @ Ws.T + bs
            beta = jax.nn.sigmoid(jnp.concatenate([out, x_r, out - x_r], axis=-1) @ Wbeta.T)
            return beta * x_r + (1.0 - beta) * out

        def _forward(x, src, dst, Wi, bi, Wq, bq, Wk, bk, Wv, bv, Ws, bs, Wbeta, ln_g, ln_b, W1, b1, W2, b2, Wo, bo):
            h = jax.nn.gelu(x @ Wi.T + bi, approximate=False)
            for i in range(L):
                res = h
                h = _transformer_conv(h, src, dst, Wq[i], bq[i], Wk[i], bk[i], Wv[i], bv[i], Ws[i], bs[i], Wbeta[i])
                h = _layer_norm(h + res, ln_g[i], ln_b[i])
                res = h
                f = jax.nn.gelu(h @ W1[i].T + b1[i], approximate=False) @ W2[i].T + b2[i]
                h = f + res
            return h @ Wo.T + bo
        src, dst = (edge_index[0], edge_index[1])
        return _forward(x, src, dst, Wi, bi, Wq, bq, Wk, bk, Wv, bv, Ws, bs, Wbeta, ln_g, ln_b, W1, b1, W2, b2, Wo, bo)
    edge_index = jnp.stack([src, dst])
    x = _layernorm(x + _L0_gnn_ref(x, edge_index, L0_gnn_Wl, L0_gnn_Wr, L0_gnn_b), axis=-1)
    x = _layernorm(x + _L1_gnn_ref(x, edge_index, L1_gnn_Wi, L1_gnn_bi, L1_gnn_Wq, L1_gnn_bq, L1_gnn_Wk, L1_gnn_bk, L1_gnn_Wv, L1_gnn_bv, L1_gnn_Ws, L1_gnn_bs, L1_gnn_Wbeta, L1_gnn_ln_g, L1_gnn_ln_b, L1_gnn_W1, L1_gnn_b1, L1_gnn_W2, L1_gnn_b2, L1_gnn_Wo, L1_gnn_bo), axis=-1)
    return x

_drawn_inputs = setup_inputs


def setup_inputs(seed=0):
    import zlib

    import numpy as np

    out = dict(_drawn_inputs(seed))
    spreads = {'L0_gnn_b': (0.0, 0.1),
     'L1_gnn_bi': (0.0, 0.1),
     'L1_gnn_bq': (0.0, 0.8),
     'L1_gnn_bk': (0.0, 0.8),
     'L1_gnn_bv': (0.0, 0.1),
     'L1_gnn_bs': (0.0, 0.1),
     'L1_gnn_ln_g': (1.0, 0.2),
     'L1_gnn_ln_b': (0.0, 0.1),
     'L1_gnn_b1': (0.0, 0.1),
     'L1_gnn_b2': (0.0, 0.1),
     'L1_gnn_bo': (0.0, 0.1)}
    factors = {'L1_gnn_Wk': 2.859}
    for name, (base, spread) in spreads.items():
        noise = np.random.default_rng([zlib.crc32(name.encode()), seed]).standard_normal(out[name].shape)
        drawn = base * np.exp(spread * noise) if base else spread * noise
        out[name] = jnp.asarray(drawn.astype(out[name].dtype))
    for name, factor in factors.items():
        out[name] = (out[name] * factor).astype(out[name].dtype)
    return out
```

```python
from contextlib import ExitStack

import concourse.bass as bass
from concourse import mybir

ALU = mybir.AluOpType
ACT = mybir.ActivationFunctionType
AX = mybir.AxisListType
F32 = mybir.dt.float32
BF16 = mybir.dt.bfloat16
I32 = mybir.dt.int32

P = 128
DEBUG = False


def build(nc, t_in, out, dbg=None):
    N, D = t_in["x"].shape
    E = t_in["src"].shape[0]
    HID = t_in["wqkvs"].shape[1]
    LS, LT = t_in["wlr"].shape[0], t_in["wqkvs"].shape[0]
    FF = t_in["w1t"].shape[2]
    HEADS = 8
    DH = HID // HEADS
    VW = DH + 1
    KV = HID + HEADS * VW
    FC = FF // P
    T = -(-N // P)
    NP = T * P
    LAST = N - (T - 1) * P
    DUMMY = NP
    CH = 8
    CH_LOG = 3
    NB = 4
    GMAX = T + E // CH + NB
    EJ = -(-E // P)
    EL = E - (P - 1) * EJ
    JB = next(j for j in range(32, 0, -1) if EJ % (2 * j) == 0)
    DEG_CLAMP = 4095.0
    NEG = -1.0e30
    W_LOADS = 16 * (2 + LT + 2 + 1 + 6 + 2)

    ctx = ExitStack()
    with ctx:
        def sb(name, shape, dt=F32):
            return ctx.enter_context(nc.sbuf_tensor(name, shape, dt))

        def ps(name):
            return ctx.enter_context(nc.psum_tensor(name, [P, 512], F32))

        def sem(name):
            return ctx.enter_context(nc.semaphore(name))

        def dram(name, shape, dt=F32):
            return nc.dram_tensor(name, shape, dt, kind="Internal").ap()

        src_run = dram("src_run", (2 * E + CH,), I32)
        natural = dram("natural", (3, 64 * 64))
        posrec = dram("posrec", (NP, 4), I32)
        slot_ids = dram("slot_ids", (GMAX + NB, P, CH), I32)
        xtab = dram("xtab", (NP + 1, D))
        kvtab = dram("kvtab", (NP + 1, KV))

        diff_i = sb("diff_i", [P, P], I32)
        ident = sb("ident", [P, P])
        upper = sb("upper", [P, P])
        iota64_i = sb("iota64_i", [P, 64], I32)
        iota64 = sb("iota64", [P, 64], BF16)
        iota8 = sb("iota8", [P, CH])
        node_i = sb("node_i", [P, T], I32)
        nodekey_i = sb("nodekey_i", [64, 64], I32)
        nodekey = sb("nodekey", [64, 64])
        zeros = sb("zeros", [P, 1024])
        posn = sb("posn", [P, T, 4], I32)
        deg_pos = sb("deg_pos", [P, T])
        off_pos = sb("off_pos", [P, T])
        inv_cnt = sb("inv_cnt", [P, T])
        chunks_f = sb("chunks_f", [32, 4])
        chunks_i = sb("chunks_i", [32, 4], I32)
        meta = sb("meta", [1, 32], I32)
        meta_f = sb("meta_f", [1, 4])
        meta_i = sb("meta_i", [1, 4], I32)

        pool_a = sb("pool_a", [P, NB * CH * KV])
        pool_b = sb("pool_b", [P, T * KV])
        dst_i = pool_b[:, 0:EJ].bitcast(I32)
        dhi_i = pool_b[:, EJ:2 * EJ].bitcast(I32)
        dhi = pool_b[:, 2 * EJ:3 * EJ]
        dlo = pool_b[:, 3 * EJ:4 * EJ]
        hot_hi = [pool_a[:, JB * 32 * u:JB * 32 * (u + 1)].bitcast(BF16).rearrange("p (j c) -> p j c", c=64) for u in range(2)]
        hot_lo = [pool_a[:, JB * 32 * (2 + u):JB * 32 * (3 + u)].bitcast(BF16).rearrange("p (j c) -> p j c", c=64) for u in range(2)]
        keys_bc = pool_a[:, 0:NP]
        greater = pool_a[:, NP:2 * NP]
        deg_nat = sb("deg_nat", [64, 64])
        off_nat = sb("off_nat", [64, 64])
        key_nat = sb("key_nat", [64, 64])
        rowsum = sb("rowsum", [64, 2])
        nat_row = sb("nat_row", [T, 3, P])
        nat_col = sb("nat_col", [P, 3, T])
        rank_f = sb("rank_f", [P, T])
        rank_i = sb("rank_i", [P, T], I32)
        rec = sb("rec", [P, T, 4], I32)

        run_at = sb("run_at", [P, 1])
        run_i = sb("run_i", [P, NB, 1], I32)
        raw = sb("raw", [P, NB, CH], I32)
        left = sb("left", [P, 1])
        valid = sb("valid", [P, CH])
        rawf = sb("rawf", [P, CH])
        ids_out = sb("ids_out", [P, NB, CH], I32)

        ids = sb("ids", [P, NB, CH], I32)
        xs = pool_a[:, 0:NB * CH * D].rearrange("p (u s d) -> p u s d", u=NB, s=CH)
        kv = pool_a[:, :].rearrange("p (u s d) -> p u s d", u=NB, s=CH)
        xp = pool_b[:, 0:T * D].rearrange("p (t d) -> p t d", d=D)
        kvn = pool_b[:, :].rearrange("p (t d) -> p t d", d=KV)

        x0 = sb("x0", [P, T, D])
        agg = sb("agg", [P, D])
        part = sb("part", [P, D])
        cat = sb("cat", [P, P])
        catT = sb("catT", [P, P])
        wlr = sb("wlr", [P, LS, D])
        bl_bc = sb("bl_bc", [P, LS, D])
        floors = sb("floors", [P, LS])

        wi = sb("wi", [D, HID])
        wqkvs = sb("wqkvs", [P, LT, 4 * HID])
        w1 = sb("w1", [P, FF])
        w2 = sb("w2", [P, LT, FC, HID])
        wo = sb("wo", [P, D])
        bi_bc = sb("bi_bc", [P, HID])
        bqkvs_bc = sb("bqkvs_bc", [P, LT, 4 * HID])
        wbeta_bc = sb("wbeta_bc", [P, LT, 3 * HID])
        lng_bc = sb("lng_bc", [P, LT, HID])
        lnb_bc = sb("lnb_bc", [P, LT, HID])
        b2_bc = sb("b2_bc", [P, LT, HID])
        bo_bc = sb("bo_bc", [P, D])
        b1_row = sb("b1_row", [LT * FC, P])
        b1_all = sb("b1_all", [P, LT * FC])
        b1 = sb("b1", [P, FC])
        h_all = sb("h_all", [P, T, HID])
        q_all = sb("q_all", [P, T, HID])
        r_all = sb("r_all", [P, T, HID])
        y_all = sb("y_all", [P, T, D])
        q_t = sb("q_t", [P, HID])
        prod = sb("prod", [P, CH, HID])
        empty = sb("empty", [P, CH])
        score = sb("score", [P, HEADS, CH + 1])
        top = sb("top", [P, HEADS])
        delta = sb("delta", [P, HEADS, CH + 1])
        expo = sb("expo", [P, HEADS, CH + 1])
        wv = sb("wv", [P, CH + 1, HEADS * VW])
        acc = sb("acc", [P, HEADS * VW])
        rden = sb("rden", [P, HEADS])
        tri = sb("tri", [P, 3 * HID])
        triw = sb("triw", [P, 3 * HID])
        gate = sb("gate", [P, 4])
        y = sb("y", [P, HID])
        stats = sb("stats", [P, 6])
        mv = sb("mv", [P, T, 2])
        std = sb("std", [P, T])
        rstd = sb("rstd", [P, T])
        h1 = sb("h1", [P, HID])
        h1T = sb("h1T", [P, P])
        gT = sb("gT", [P, FC, P])
        hs = sb("hs", [P, HID])
        hT = sb("hT", [P, P])
        xs1 = sb("xs1", [P, D])
        xT = sb("xT", [D, P])
        tmp = sb("tmp", [P, HID])

        psum = [ps(f"psum{i}") for i in range(8)]
        p_hist, p_t, p_y, p_q, p_f1, p_f2, p_t2 = psum[0:7]

        names = """const_pool const_dve dst_free dst_ld src_ld zero_st hot_ready hot_used hist_done
            pre_ready pre_done nat_ready nat_st nat_ld nat_ldb nat_turned rec_ready rec_st pos_ld deg_ready degT_done
            cnt_ready base_done meta_ready run_ready raw_in ids_ready ids_stored xgath xgot
            chunk_done gathered x_ready x_st w_ld w_free catp catt catc mm_done y_free
            out_ready out_st past_wait ones_ready b1_done b1_used w1_ld kv_ready kv_st d_ready e_done z_ready z_done var_ready std_done h1_ready h1_turned h1T_ready f1_done g_done f2_done hs_ready hs_turned hT_ready proj_done x1_ready x1_turned xT_ready hi_done hi_ready gelu_done fvar_ready fstd_done dbg_s""".split()
        S = {n: sem(n) for n in names}
        raw_ld = [sem(f"raw_ld{u}") for u in range(NB)]
        ids_st = [sem(f"ids_st{u}") for u in range(NB)]
        ids_ld = [sem(f"ids_ld{u}") for u in range(NB)]
        rows_ld = [sem(f"rows_ld{u}") for u in range(NB)]

        def base(eng, t):
            return eng.value_load(meta[0:1, bass.ds(t, 1)], min_val=0, max_val=GMAX)

        def chunk_total(eng):
            return eng.value_load(meta[0:1, T:T + 1], min_val=NB, max_val=GMAX)

        def wait_count(eng, semaphore, count):
            eng.wait_ge(semaphore, count)
            eng.sem_inc(S["past_wait"], 1)

        block = ctx.enter_context(nc.Block())

        @block.sync
        def _(sp):
            sp.dma_start(src_run[0:E].rearrange("(a b) -> a b", a=625),
                         t_in["src"].rearrange("(a b) -> a b", a=625)).then_inc(S["src_ld"], 16)
            sp.dma_start(xtab[0:N, :], t_in["x"]).then_inc(S["src_ld"], 16)
            sp.wait_ge(S["dst_free"], 1)
            sp.dma_start(dst_i[0:P - 1, :], t_in["dst"][0:(P - 1) * EJ].rearrange("(p j) -> p j", j=EJ)).then_inc(S["dst_ld"], 16)
            sp.dma_start(dst_i[P - 1:P, 0:EL], t_in["dst"][(P - 1) * EJ:E].rearrange("(p j) -> p j", p=1)).then_inc(S["dst_ld"], 16)
            sp.wait_ge(S["const_dve"], 1)
            zi = zeros[:, :].bitcast(I32)
            n_tail = E + CH
            rows = n_tail // 1024
            sp.dma_start(src_run[E:E + rows * 1024].rearrange("(p j) -> p j", j=1024), zi[0:rows, :]).then_inc(S["zero_st"], 16)
            sp.dma_start(src_run[E + rows * 1024:2 * E + CH].rearrange("(p j) -> p j", p=1), zi[0:1, 0:n_tail - rows * 1024]).then_inc(S["zero_st"], 16)
            sp.dma_start(xtab[N:NP + 1, :], zeros[0:NP + 1 - N, 0:D]).then_inc(S["zero_st"], 16)
            sp.dma_start(kvtab[DUMMY:DUMMY + 1, :], zeros[0:1, 0:KV]).then_inc(S["zero_st"], 16)
            for tile, name in ((wlr, "wlr"), (wqkvs, "wqkvs")):
                sp.dma_start(tile[:, :, :], t_in[name].rearrange("l k n -> k l n")).then_inc(S["w_ld"], 16)
            for layer in range(LT):
                sp.dma_start(w2[:, layer, :, :], t_in["w2t"][layer].rearrange("(c k) n -> k c n", k=P)).then_inc(S["w_ld"], 16)
            for tile, name in ((wi, "wi"), (wo, "wo")):
                sp.dma_start(tile[:, :], t_in[name]).then_inc(S["w_ld"], 16)
            sp.dma_start(b1_row[:, :], t_in["b1"].rearrange("l (c k) -> (l c) k", k=P)).then_inc(S["w_ld"], 16)
            for tile, name in ((bl_bc, "bl"), (bqkvs_bc, "bqkvs"), (wbeta_bc, "wbeta"), (lng_bc, "lng"), (lnb_bc, "lnb"), (b2_bc, "b2")):
                flat = t_in[name].rearrange("(a l) n -> a (l n)", a=1)
                sp.dma_start(tile[:, :, :].rearrange("p l n -> p (l n)"), flat.partition_broadcast(P)).then_inc(S["w_ld"], 16)
            for tile, name in ((bi_bc, "bi"), (bo_bc, "bo")):
                sp.dma_start(tile[:, :], t_in[name].partition_broadcast(P)).then_inc(S["w_ld"], 16)
            sp.wait_ge(S["nat_ready"], 1)
            for i, t in enumerate((key_nat, off_nat, deg_nat)):
                sp.dma_start(natural[i, :].rearrange("(a b) -> a b", b=64), t[:, :]).then_inc(S["nat_st"], 16)
            sp.wait_ge(S["nat_st"], 48)
            sp.dma_start(keys_bc, natural[0:1, 0:NP].partition_broadcast(P)).then_inc(S["nat_ldb"], 16)
            for i in range(3):
                sp.dma_start(nat_row[:, i, :], natural[i, 0:NP].rearrange("(t p) -> t p", p=P)).then_inc(S["nat_ld"], 16)
            sp.wait_ge(S["rec_st"], 16 * T)
            sp.dma_start(posn[:, :, :], posrec.rearrange("(t p) c -> p t c", p=P)).then_inc(S["pos_ld"], 16)

            sp.wait_ge(S["meta_ready"], 1)
            total = chunk_total(sp)
            with sp.Fori(0, total, NB) as g:
                k = g // NB
                for u in range(NB):
                    wait_count(sp, raw_ld[u], 16 * k + 16)
                    sp.sem_inc(S["raw_in"], 1)
                    wait_count(sp, S["ids_ready"], g + (u + 1))
                    sp.dma_start(slot_ids[bass.ds(g + u, 1), :, :].rearrange("a p s -> (a p) s"), ids_out[:, u, :]).then_inc(ids_st[u], 16)
                for u in range(NB):
                    wait_count(sp, ids_st[u], 16 * k + 16)
                sp.sem_inc(S["ids_stored"], NB)
            if DEBUG:
                sp.dma_start(dbg[0:96, :, :], slot_ids[0:96, :, :]).then_inc(S["dbg_s"], 16)
                sp.wait_ge(S["dbg_s"], 16)

            def feed(first, last):
                with sp.Fori(first, last) as layer:
                    if first == LS:
                        wait_count(sp, S["f1_done"], (layer - LS) * T + 1)
                        sp.dma_start(w1[:, :], t_in["w1t"][bass.ds(layer - LS, 1), :, :].rearrange("a k n -> (a k) n")).then_inc(S["w1_ld"], 16)
                    with sp.Fori(0, total, NB) as g:
                        q = layer * total + g
                        k = q // NB
                        for u in range(NB):
                            wait_count(sp, S["chunk_done"], q + (u + 1))
                            sp.dma_start(ids[:, u, :], slot_ids[bass.ds(g + u, 1), :, :].rearrange("a p s -> (a p) s")).then_inc(ids_ld[u], 16)
                            if u >= 2:
                                wait_count(sp, rows_ld[u - 2], 16 * CH * k + 16 * CH)
                                sp.sem_inc(S["gathered"], 1)
                            else:
                                with sp.If(g > 0):
                                    wait_count(sp, rows_ld[u + NB - 2], 16 * CH * k)
                                    sp.sem_inc(S["gathered"], 1)
                    kl = (layer + 1) * total // NB
                    for u in range(NB - 2, NB):
                        wait_count(sp, rows_ld[u], 16 * CH * kl)
                        sp.sem_inc(S["gathered"], 1)

            sp.sem_inc(S["chunk_done"], NB)
            feed(0, LS)
            sp.sem_inc(S["f1_done"], 1)
            feed(LS, LS + LT)
            sp.wait_ge(S["out_ready"], T)
            sp.wait_ge(S["out_st"], 16 * T)

        @block.gpsimd
        def _(pool):
            nc.gpsimd.iota(diff_i[:, :], pattern=[[1, P]], base=0, channel_multiplier=-1).then_inc(S["const_pool"], 1)
            nc.gpsimd.iota(iota64_i[:, :], pattern=[[1, 64]], base=0, channel_multiplier=0).then_inc(S["const_pool"], 1)
            nc.gpsimd.iota(node_i[:, :], pattern=[[P, T]], base=0, channel_multiplier=1).then_inc(S["const_pool"], 1)
            nc.gpsimd.iota(nodekey_i[:, :], pattern=[[-1, 64]], base=4095, channel_multiplier=-64).then_inc(S["const_pool"], 1)
            pool.wait_ge(S["rec_ready"], 1)
            for t in range(T):
                pool.indirect_dma_start(posrec, bass.IndirectOffsetOnAxis(ap=rank_i[:, t:t + 1], axis=0),
                                        rec[:, t, :], None).then_inc(S["rec_st"], 16)
            pool.wait_ge(S["pos_ld"], 16)
            pool.wait_ge(S["src_ld"], 32)
            pool.wait_ge(S["zero_st"], 64)
            for t in range(T):
                pool.indirect_dma_start(x0[:, t, :], None, xtab,
                                        bass.IndirectOffsetOnAxis(ap=posn[:, t, 0:1], axis=0)).then_inc(S["xgath"], 16)
            pool.wait_ge(S["meta_ready"], 1)
            total = chunk_total(pool)
            runs = src_run.rearrange("(n a) -> n a", a=1)
            with pool.Fori(0, total, NB) as g:
                for u in range(NB):
                    wait_count(pool, S["run_ready"], g + (u + 1))
                    pool.indirect_dma_start(raw[:, u, :], None, runs,
                                            bass.IndirectOffsetOnAxis(ap=run_i[:, u, :], axis=0)).then_inc(raw_ld[u], 16)

            def gather(layer, table, rows):
                with pool.Fori(0, total, NB) as g:
                    k = (layer * total + g) // NB
                    for u in range(NB):
                        wait_count(pool, ids_ld[u], 16 * k + 16)
                        for s in range(CH):
                            pool.indirect_dma_start(rows[:, u, s, :], None, table,
                                                    bass.IndirectOffsetOnAxis(ap=ids[:, u, s:s + 1], axis=0)).then_inc(rows_ld[u], 16)

            def scatter(layer, table, rows, ready, stored, count):
                for u in range(NB):
                    wait_count(pool, rows_ld[u], 16 * CH * ((layer + 1) * total // NB))
                store(table, rows, ready, stored, count)

            def store(table, rows, ready, stored, count):
                for t in range(T):
                    wait_count(pool, ready, count * T + (t + 1))
                    pool.indirect_dma_start(table, bass.IndirectOffsetOnAxis(ap=posn[:, t, 0:1], axis=0),
                                            rows[:, t, :], None).then_inc(stored, 16)
                wait_count(pool, stored, count * (16 * T) + 16 * T)

            with pool.Fori(0, LS - 1) as layer:
                gather(layer, xtab, xs)
                scatter(layer, xtab, xp, S["x_ready"], S["x_st"], layer)
            gather(LS - 1, xtab, xs)
            store(kvtab, kvn, S["kv_ready"], S["kv_st"], 0)
            with pool.Fori(LS, LS + LT - 1) as layer:
                gather(layer, kvtab, kv)
                scatter(layer, kvtab, kvn, S["kv_ready"], S["kv_st"], layer - (LS - 1))
            gather(LS + LT - 1, kvtab, kv)
            for t in range(T):
                pool.wait_ge(S["out_ready"], t + 1)
                m = P if t < T - 1 else LAST
                pool.indirect_dma_start(out, bass.IndirectOffsetOnAxis(ap=posn[0:m, t, 0:1], axis=0),
                                        y_all[0:m, t, :], None).then_inc(S["out_st"], 16)

        @block.vector
        def _(dve):
            nc.vector.memset(dst_i, -1).then_inc(S["dst_free"], 1)
            nc.vector.memset(zeros[:, :], 0.0).then_inc(S["const_dve"], 1)
            nc.vector.memset(floors[:, 0:LS - 1], 0.0)
            nc.vector.memset(floors[:, LS - 1:LS], -3.0e38)
            dve.wait_ge(S["const_pool"], 4)
            nc.vector.tensor_scalar(ident[:, :], diff_i[:, :], 0.0, None, ALU.is_equal)
            nc.vector.tensor_scalar(upper[:, :], diff_i[:, :], 0.0, None, ALU.is_gt)
            nc.vector.tensor_copy(iota64[:, :], iota64_i[:, :])
            nc.vector.tensor_copy(iota8[:, :], iota64_i[:, 0:CH])
            nc.vector.tensor_copy(nodekey[:, :], nodekey_i[:, :])

            dve.wait_ge(S["dst_ld"], 32)
            nc.vector.tensor_scalar(dhi_i, dst_i, 6, None, ALU.arith_shift_right)
            dve.drain()
            nc.vector.tensor_copy(dhi, dhi_i)
            nc.vector.tensor_scalar(dst_i, dst_i, 63, None, ALU.bitwise_and)
            dve.drain()
            nc.vector.tensor_copy(dlo, dst_i)
            dve.drain().then_inc(S["const_dve"], 1)
            with dve.Fori(0, EJ // (2 * JB)) as i:
                for u in range(2):
                    wait_count(dve, S["hot_used"], 2 * i + (u + 1))
                    grid = iota64[:, :].unsqueeze(1).to_broadcast((P, JB, 64))
                    for hot, half in ((hot_hi, dhi), (hot_lo, dlo)):
                        ins = nc.vector.tensor_tensor(
                            hot[u], grid,
                            half[:, bass.ds(i * (2 * JB) + u * JB, JB)].unsqueeze(2).to_broadcast((P, JB, 64)),
                            ALU.is_equal)
                    ins.then_inc(S["hot_ready"], 1)
            dve.wait_ge(S["hist_done"], 1)
            nc.vector.tensor_copy(deg_nat[:, :], p_hist[0:64, 0:64])
            nc.vector.tensor_reduce(rowsum[:, 0:1], p_hist[0:64, 0:64], AX.X, ALU.add).then_inc(S["pre_ready"], 1)
            dve.drain()
            nc.vector.tensor_scalar(key_nat[:, :], deg_nat[:, :], DEG_CLAMP, 4096.0, ALU.min, ALU.mult)
            dve.drain()
            nc.vector.tensor_tensor(key_nat[:, :], key_nat[:, :], nodekey[:, :], ALU.add)
            dve.wait_ge(S["pre_done"], 1)
            nc.vector.tensor_copy(rowsum[:, 1:2], p_y[0:64, 0:1])
            dve.drain()
            nc.vector.tensor_tensor_scan(off_nat[:, :], deg_nat[:, :], zeros[0:64, 0:64], rowsum[:, 1:2], ALU.add, ALU.add)
            dve.drain()
            nc.vector.tensor_tensor(off_nat[:, :], off_nat[:, :], deg_nat[:, :], ALU.subtract).then_inc(S["nat_ready"], 1)
            dve.wait_ge(S["nat_ldb"], 16)
            dve.wait_ge(S["nat_turned"], 3)
            nc.vector.tensor_copy(nat_col[:, :, :].rearrange("p c t -> p (c t)"), p_t[:, 0:3 * T])
            dve.drain()
            for t in range(T):
                if t:
                    dve.drain()
                nc.vector.tensor_scalar(greater, keys_bc, nat_col[:, 0, t:t + 1], 0.0, ALU.is_gt, ALU.add,
                                        accum_out=rank_f[:, t:t + 1])
            nc.vector.tensor_copy(rec[:, :, 0], node_i[:, :])
            nc.vector.tensor_copy(rec[:, :, 1], nat_col[:, 1, :])
            nc.vector.tensor_copy(rec[:, :, 2], nat_col[:, 2, :])
            nc.vector.tensor_copy(rec[:, :, 3], node_i[:, :])
            dve.drain()
            nc.vector.tensor_copy(rank_i[:, :], rank_f[:, :])
            dve.drain().then_inc(S["rec_ready"], 1)
            dve.wait_ge(S["pos_ld"], 16)
            nc.vector.tensor_copy(off_pos[:, :], posn[:, :, 1])
            nc.vector.tensor_copy(deg_pos[:, :], posn[:, :, 2])
            dve.drain().then_inc(S["deg_ready"], 1)
            nc.vector.tensor_scalar(inv_cnt[:, :], deg_pos[:, :], 1.0, None, ALU.max)
            dve.drain()
            nc.vector.reciprocal(inv_cnt[:, :], inv_cnt[:, :])
            dve.wait_ge(S["degT_done"], 1)
            nc.vector.tensor_reduce(chunks_f[0:T, 0:1], p_t[0:T, 0:P], AX.X, ALU.max)
            dve.drain()
            nc.vector.tensor_scalar(chunks_i[0:T, 0:1], chunks_f[0:T, 0:1], float(CH - 1), float(CH), ALU.add, ALU.max)
            dve.drain()
            nc.vector.tensor_scalar(chunks_i[0:T, 1:2], chunks_i[0:T, 0:1], CH_LOG, None, ALU.arith_shift_right)
            dve.drain()
            nc.vector.tensor_copy(chunks_f[0:T, 1:2], chunks_i[0:T, 1:2])
            dve.drain().then_inc(S["cnt_ready"], 1)
            dve.wait_ge(S["base_done"], 1)
            nc.vector.tensor_copy(meta[0:1, 0:T + 1], p_y[0:1, 0:T + 1])
            nc.vector.tensor_scalar(meta_i[0:1, 0:1], p_y[0:1, T:T + 1], float(NB - 1), None, ALU.add)
            dve.drain()
            nc.vector.tensor_scalar(meta[0:1, T:T + 1], meta_i[0:1, 0:1], -NB, None, ALU.bitwise_and)
            dve.drain().then_inc(S["meta_ready"], 1)

            dve.wait_ge(S["meta_ready"], 1)
            with dve.Fori(0, T) as t:
                dve.drain()
                nc.vector.tensor_copy(left[:, :], deg_pos[:, bass.ds(t, 1)])
                with dve.Fori(base(dve, t), base(dve, t + 1)) as g:
                    u = g % NB
                    wait_count(dve, S["raw_in"], g + 1)
                    dve.drain()
                    nc.vector.tensor_scalar(valid[:, :], iota8[:, :], left[:, 0:1], None, ALU.is_lt)
                    nc.vector.tensor_scalar(rawf[:, :], raw[:, bass.ds(u, 1), :], -float(DUMMY), None, ALU.add)
                    dve.drain()
                    nc.vector.tensor_scalar(left[:, :], left[:, :], -float(CH), None, ALU.add)
                    nc.vector.tensor_tensor(rawf[:, :], rawf[:, :], valid[:, :], ALU.mult)
                    wait_count(dve, S["ids_stored"], g + 1)
                    dve.drain()
                    nc.vector.tensor_scalar(ids_out[:, bass.ds(u, 1), :], rawf[:, :], float(DUMMY), None, ALU.add).then_inc(S["ids_ready"], 1)

            dve.wait_ge(S["xgath"], 16 * T)
            nc.vector.tensor_copy(xp.rearrange("p t d -> p (t d)"), x0[:, :, :].rearrange("p t d -> p (t d)"))
            total = chunk_total(dve)
            with dve.Fori(0, LS) as layer:
                with dve.Fori(0, T) as t:
                    dve.drain()
                    nc.vector.memset(agg[:, :], 0.0)
                    with dve.Fori(base(dve, t), base(dve, t + 1)) as g:
                        wait_count(dve, S["gathered"], layer * total + g + 1)
                        dve.drain()
                        nc.vector.tensor_reduce(part[:, :], xs[:, bass.ds(g % NB, 1), :, :].rearrange("p u s d -> p d (u s)"),
                                                AX.X, ALU.add).then_inc(S["chunk_done"], 1)
                        dve.drain()
                        nc.vector.tensor_tensor(agg[:, :], agg[:, :], part[:, :], ALU.add)
                    n = layer * T + t
                    dve.drain()
                    nc.vector.tensor_scalar(cat[:, 0:D], agg[:, :], inv_cnt[:, bass.ds(t, 1)], None, ALU.mult)
                    nc.vector.tensor_copy(cat[:, D:2 * D], xp[:, bass.ds(t, 1), :])
                    dve.drain().then_inc(S["catp"], 1)
                    wait_count(dve, S["mm_done"], n + 1)
                    nc.vector.tensor_tensor(part[:, :], p_y[:, 0:D], bl_bc[:, bass.ds(layer, 1), :], ALU.add)
                    dve.drain()
                    nc.vector.tensor_scalar(xp[:, bass.ds(t, 1), :], part[:, :], floors[:, bass.ds(layer, 1)], None, ALU.max)
                    dve.drain().then_inc(S["x_ready"], 1)

            dve.drain()
            flat = x0[:, :, :].rearrange("p t d -> p (t d)")
            nc.vector.tensor_tensor(flat, flat, xp.rearrange("p t d -> p (t d)"), ALU.add)
            dve.drain()
            for t in range(T):
                nc.vector.bn_stats(stats[:, :], x0[:, t, :])
                dve.drain()
                nc.vector.bn_aggr(mv[:, t, :], stats[:, :])
                dve.drain()
            nc.vector.tensor_scalar(std[:, :], mv[:, :, 1], 1e-5, None, ALU.add)
            dve.drain().then_inc(S["var_ready"], 1)
            dve.wait_ge(S["std_done"], 1)
            nc.vector.reciprocal(rstd[:, :], std[:, :])
            dve.drain()
            for t in range(T):
                nc.vector.tensor_scalar(x0[:, t, :], x0[:, t, :], mv[:, t, 0:1], rstd[:, t:t + 1], ALU.subtract, ALU.mult)
            dve.drain()
            nc.vector.memset(kvn[:, :, :], 1.0)
            dve.wait_ge(S["b1_done"], 1)
            nc.vector.tensor_copy(b1_all[:, :], p_t2[:, 0:LT * FC]).then_inc(S["b1_used"], 1)

            def project(t, layer, n):
                def add(dst, c, src=None):
                    bias = bqkvs_bc[:, bass.ds(layer, 1), c * HID:(c + 1) * HID]
                    return nc.vector.tensor_tensor(dst, p_q[:, c * HID:(c + 1) * HID], bias, ALU.add)
                wait_count(dve, S["proj_done"], n + 1)
                add(tmp[:, :], 0)
                add(kvn[:, bass.ds(t, 1), 0:HID], 1)
                vals = kvn[:, bass.ds(t, 1), HID:KV].rearrange("p a (h w) -> p (a h) w", w=VW)[:, :, 0:DH]
                nc.vector.tensor_tensor(vals, p_q[:, 2 * HID:3 * HID].rearrange("p (h w) -> p h w", w=DH),
                                        bqkvs_bc[:, bass.ds(layer, 1), 2 * HID:3 * HID].rearrange("p a (h w) -> p (a h) w", w=DH), ALU.add)
                add(r_all[:, bass.ds(t, 1), :], 3)
                dve.drain()
                nc.vector.tensor_scalar(q_all[:, bass.ds(t, 1), :], tmp[:, :], float(DH) ** -0.5, None, ALU.mult)
                dve.drain().then_inc(S["kv_ready"], 1)

            with dve.Fori(0, T) as t:
                dve.drain()
                nc.vector.tensor_copy(xs1[:, :], x0[:, bass.ds(t, 1), :]).then_inc(S["x1_ready"], 1)
                wait_count(dve, S["hi_done"], t + 1)
                nc.vector.tensor_tensor(y[:, :], p_y[:, 0:HID], bi_bc[:, :], ALU.add).then_inc(S["hi_ready"], 1)
                wait_count(dve, S["gelu_done"], t + 1)
                nc.vector.tensor_copy(h_all[:, bass.ds(t, 1), :], hs[:, :])
                project(t, 0, t)

            def attend(t, layer):
                dve.drain()
                nc.vector.tensor_copy(q_t[:, :], q_all[:, bass.ds(t, 1), :])
                nc.vector.memset(score[:, :, CH], NEG)
                nc.vector.memset(acc[:, :], 0.0)
                with dve.Fori(base(dve, t), base(dve, t + 1)) as g:
                    q = (layer + LS) * total + g
                    ql = layer * total + g
                    u = g % NB
                    wait_count(dve, S["gathered"], q + 1)
                    dve.drain()
                    nc.vector.tensor_tensor(prod[:, :, :], kv[:, bass.ds(u, 1), :, 0:HID].rearrange("p u s d -> p (u s) d"),
                                            q_t[:, :].unsqueeze(1).to_broadcast((P, CH, HID)), ALU.mult)
                    nc.vector.tensor_scalar(empty[:, :], ids[:, bass.ds(u, 1), :], float(DUMMY), NEG, ALU.is_equal, ALU.mult)
                    dve.drain()
                    nc.vector.tensor_reduce(score[:, :, 0:CH].rearrange("p h s -> p s h"),
                                            prod[:, :, :].rearrange("p s (h d) -> p s h d", d=DH), AX.X, ALU.add)
                    dve.drain()
                    nc.vector.tensor_tensor(score[:, :, 0:CH], score[:, :, 0:CH],
                                            empty[:, :].unsqueeze(1).to_broadcast((P, HEADS, CH)), ALU.add)
                    dve.drain()
                    nc.vector.tensor_reduce(top[:, :], score[:, :, :], AX.X, ALU.max)
                    dve.drain()
                    nc.vector.tensor_tensor(delta[:, :, :], score[:, :, :],
                                            top[:, :].unsqueeze(2).to_broadcast((P, HEADS, CH + 1)), ALU.subtract).then_inc(S["d_ready"], 1)
                    wait_count(dve, S["e_done"], ql + 1)
                    nc.vector.tensor_copy(score[:, :, CH], top[:, :])
                    nc.vector.tensor_tensor(wv[:, 0:CH, :].rearrange("p s (h w) -> p s h w", w=VW),
                                            kv[:, bass.ds(u, 1), :, HID:KV].rearrange("p u s (h w) -> p (u s) h w", w=VW),
                                            expo[:, :, 0:CH].rearrange("p h s -> p s h").unsqueeze(3).to_broadcast((P, CH, HEADS, VW)),
                                            ALU.mult).then_inc(S["chunk_done"], 1)
                    nc.vector.tensor_tensor(wv[:, CH, :].rearrange("p (h w) -> p h w", w=VW),
                                            acc[:, :].rearrange("p (h w) -> p h w", w=VW),
                                            expo[:, :, CH:CH + 1].to_broadcast((P, HEADS, VW)), ALU.mult)
                    dve.drain()
                    nc.vector.tensor_reduce(acc[:, :], wv[:, :, :].rearrange("p s f -> p f s"), AX.X, ALU.add)
                dve.drain()

            def finish(t, layer, n):
                accw = acc[:, :].rearrange("p (h w) -> p h w", w=VW)
                nc.vector.tensor_scalar(rden[:, :], accw[:, :, DH], 1e-16, None, ALU.add)
                nc.vector.tensor_copy(tri[:, HID:2 * HID], r_all[:, bass.ds(t, 1), :])
                dve.drain()
                nc.vector.reciprocal(rden[:, :], rden[:, :])
                dve.drain()
                nc.vector.tensor_tensor(tri[:, 0:HID].rearrange("p (h w) -> p h w", w=DH), accw[:, :, 0:DH],
                                        rden[:, :].unsqueeze(2).to_broadcast((P, HEADS, DH)), ALU.mult)
                dve.drain()
                nc.vector.tensor_tensor(tri[:, 2 * HID:3 * HID], tri[:, 0:HID], tri[:, HID:2 * HID], ALU.subtract)
                dve.drain()
                nc.vector.tensor_tensor(triw[:, :], tri[:, :], wbeta_bc[:, bass.ds(layer, 1), :], ALU.mult)
                dve.drain()
                nc.vector.tensor_reduce(gate[:, 0:1], triw[:, :], AX.X, ALU.add)
                dve.drain().then_inc(S["z_ready"], 1)
                wait_count(dve, S["z_done"], n + 1)
                nc.vector.tensor_scalar(gate[:, 2:3], gate[:, 1:2], 1.0, None, ALU.add)
                dve.drain()
                nc.vector.reciprocal(gate[:, 2:3], gate[:, 2:3])
                dve.drain()
                nc.vector.tensor_scalar(gate[:, 3:4], gate[:, 2:3], -1.0, None, ALU.mult)
                dve.drain()
                nc.vector.scalar_tensor_tensor(out=y[:, :], in0=tri[:, 2 * HID:3 * HID], scalar=gate[:, 3:4], in1=tri[:, 0:HID],
                                               op0=ALU.mult, op1=ALU.add)
                dve.drain()
                nc.vector.tensor_tensor(y[:, :], y[:, :], h_all[:, bass.ds(t, 1), :], ALU.add)
                dve.drain()
                norm(y, n + 1)
                nc.vector.tensor_scalar(tmp[:, :], y[:, :], mv[:, 0, 0:1], rstd[:, 0:1], ALU.subtract, ALU.mult)
                dve.drain()
                nc.vector.tensor_tensor(tmp[:, :], tmp[:, :], lng_bc[:, bass.ds(layer, 1), :], ALU.mult)
                dve.drain()
                nc.vector.tensor_tensor(h1[:, :], tmp[:, :], lnb_bc[:, bass.ds(layer, 1), :], ALU.add)
                dve.drain().then_inc(S["h1_ready"], 1)
                wait_count(dve, S["f2_done"], n + 1)
                nc.vector.tensor_tensor(tmp[:, :], p_f2[:, 0:HID], b2_bc[:, bass.ds(layer, 1), :], ALU.add)
                dve.drain()
                nc.vector.tensor_tensor(hs[:, :], tmp[:, :], h1[:, :], ALU.add)
                dve.drain().then_inc(S["hs_ready"], 1)

            def norm(v, count):
                nc.vector.bn_stats(stats[:, :], v[:, :])
                dve.drain()
                nc.vector.bn_aggr(mv[:, 0, :], stats[:, :])
                dve.drain()
                nc.vector.tensor_scalar(std[:, 0:1], mv[:, 0, 1:2], 1e-5, None, ALU.add)
                dve.drain().then_inc(S["var_ready"], 1)
                wait_count(dve, S["std_done"], count + 1)
                nc.vector.reciprocal(rstd[:, 0:1], std[:, 0:1])
                dve.drain()

            with dve.Fori(0, LT - 1) as layer:
                with dve.Fori(0, T) as t:
                    n = layer * T + t
                    attend(t, layer)
                    finish(t, layer, n)
                    nc.vector.tensor_copy(h_all[:, bass.ds(t, 1), :], hs[:, :])
                    project(t, layer + 1, n + T)
            with dve.Fori(0, T) as t:
                n = (LT - 1) * T + t
                attend(t, LT - 1)
                finish(t, LT - 1, n)
                wait_count(dve, S["proj_done"], n + T + 1)
                nc.vector.tensor_tensor(xs1[:, :], p_q[:, 0:D], bo_bc[:, :], ALU.add)
                dve.drain()
                nc.vector.tensor_tensor(xs1[:, :], xs1[:, :], x0[:, bass.ds(t, 1), :], ALU.add)
                dve.drain()
                nc.vector.bn_stats(stats[:, :], xs1[:, :])
                dve.drain()
                nc.vector.bn_aggr(mv[:, 0, :], stats[:, :])
                dve.drain()
                nc.vector.tensor_scalar(std[:, 0:1], mv[:, 0, 1:2], 1e-5, None, ALU.add)
                dve.drain().then_inc(S["fvar_ready"], 1)
                wait_count(dve, S["fstd_done"], t + 1)
                nc.vector.reciprocal(rstd[:, 0:1], std[:, 0:1])
                dve.drain()
                nc.vector.tensor_scalar(y_all[:, bass.ds(t, 1), :], xs1[:, :], mv[:, 0, 0:1], rstd[:, 0:1], ALU.subtract, ALU.mult)
                dve.drain().then_inc(S["out_ready"], 1)

        @block.scalar
        def _(act):
            act.wait_ge(S["meta_ready"], 1)
            act.sem_inc(S["ids_stored"], NB)
            with act.Fori(0, T) as t:
                act.drain()
                nc.scalar.activation(run_at[:, :], off_pos[:, bass.ds(t, 1)], ACT.Copy)
                with act.Fori(base(act, t), base(act, t + 1)) as g:
                    wait_count(act, S["ids_stored"], g + 1)
                    act.drain()
                    nc.scalar.activation(run_i[:, bass.ds(g % NB, 1), :], run_at[:, :], ACT.Copy).then_inc(S["run_ready"], 1)
                    nc.scalar.activation(run_at[:, :], run_at[:, :], ACT.Copy, bias=float(CH))
            with act.Fori(0, LS) as layer:
                with act.Fori(0, T) as t:
                    n = layer * T + t
                    wait_count(act, S["catt"], n + 1)
                    nc.scalar.copy(catT[:, :], p_t[:, 0:P]).then_inc(S["catc"], 1)
            act.wait_ge(S["var_ready"], 1)
            nc.scalar.activation(std[:, :], std[:, :], ACT.Sqrt)
            act.drain().then_inc(S["std_done"], 1)

            def copy_state(n):
                wait_count(act, S["hs_turned"], n + 1)
                nc.scalar.copy(hT[:, :], p_t[:, 0:P])
                act.drain().then_inc(S["hT_ready"], 1)

            with act.Fori(0, T) as t:
                wait_count(act, S["x1_turned"], t + 1)
                nc.scalar.copy(xT[:, :], p_t[0:D, 0:P]).then_inc(S["xT_ready"], 1)
                wait_count(act, S["hi_ready"], t + 1)
                nc.scalar.activation(hs[:, :], y[:, :], ACT.Gelu)
                act.drain()
                act.sem_inc(S["gelu_done"], 1)
                act.sem_inc(S["hs_ready"], 1)
                copy_state(t)
            act.wait_ge(S["b1_used"], 1)
            total = chunk_total(act)
            with act.Fori(0, LT) as layer:
                act.drain()
                nc.scalar.copy(b1[:, :], b1_all[:, bass.ds(layer * FC, FC)])
                with act.Fori(0, T) as t:
                    n = layer * T + t
                    with act.Fori(base(act, t), base(act, t + 1)) as g:
                        wait_count(act, S["d_ready"], layer * total + g + 1)
                        nc.scalar.activation(expo[:, :, :], delta[:, :, :], ACT.Exp)
                        act.drain().then_inc(S["e_done"], 1)
                    wait_count(act, S["z_ready"], n + 1)
                    nc.scalar.activation(gate[:, 1:2], gate[:, 0:1], ACT.Exp, scale=-1.0)
                    act.drain().then_inc(S["z_done"], 1)
                    wait_count(act, S["var_ready"], n + 2)
                    nc.scalar.activation(std[:, 0:1], std[:, 0:1], ACT.Sqrt)
                    act.drain().then_inc(S["std_done"], 1)
                    wait_count(act, S["h1_turned"], n + 1)
                    nc.scalar.copy(h1T[:, :], p_t2[:, 0:P])
                    act.drain().then_inc(S["h1T_ready"], 1)
                    wait_count(act, S["f1_done"], n + 2)
                    for c in range(FC):
                        nc.scalar.activation(gT[:, c, :], p_f1[:, c * P:(c + 1) * P], ACT.Gelu, bias=b1[:, c:c + 1])
                    act.drain().then_inc(S["g_done"], 1)
                    copy_state(n + T)
                    with act.If(layer == LT - 1):
                        wait_count(act, S["fvar_ready"], t + 1)
                        nc.scalar.activation(std[:, 0:1], std[:, 0:1], ACT.Sqrt)
                        act.drain().then_inc(S["fstd_done"], 1)

        @block.tensor
        def _(pe):
            pe.wait_ge(S["const_dve"], 2)
            zb = zeros[:, 0:32].bitcast(BF16)
            pe.sem_inc(S["hot_used"], 2)
            nc.tensor.matmul(p_hist[0:64, 0:64], zb, zb, start=True, stop=False)
            with pe.Fori(0, EJ // (2 * JB)) as i:
                for u in range(2):
                    wait_count(pe, S["hot_ready"], 2 * i + (u + 1))
                    for j in range(JB):
                        mm = nc.tensor.matmul(p_hist[0:64, 0:64], hot_hi[u][:, j, :], hot_lo[u][:, j, :], start=False, stop=False)
                    mm.then_inc(S["hot_used"], 1)
            nc.tensor.matmul(p_hist[0:64, 0:64], zb, zb, start=False, stop=True).then_inc(S["hist_done"], 1)
            pe.wait_ge(S["pre_ready"], 1)
            nc.tensor.matmul(p_y[0:64, 0:1], upper[0:64, 0:64], rowsum[:, 0:1], start=True, stop=True).then_inc(S["pre_done"], 1)
            pe.wait_ge(S["nat_ld"], 48)
            for i in range(3):
                nc.tensor.transpose(p_t[:, i * T:(i + 1) * T], nat_row[:, i, :], ident[0:T, 0:T]).then_inc(S["nat_turned"], 1)
            pe.wait_ge(S["deg_ready"], 1)
            nc.tensor.transpose(p_t[0:T, 0:P], deg_pos[:, :], ident[:, :]).then_inc(S["degT_done"], 1)
            pe.wait_ge(S["cnt_ready"], 1)
            nc.tensor.matmul(p_y[0:1, 0:T + 1], chunks_f[0:T, 1:2], upper[0:T, 0:T + 1], start=True, stop=True).then_inc(S["base_done"], 1)
            pe.wait_ge(S["w_ld"], W_LOADS)
            with pe.Fori(0, LS) as layer:
                with pe.Fori(0, T) as t:
                    n = layer * T + t
                    wait_count(pe, S["catp"], n + 1)
                    nc.tensor.transpose(p_t[:, 0:P], cat[:, :], ident[:, :]).then_inc(S["catt"], 1)
                    wait_count(pe, S["catc"], n + 1)
                    nc.tensor.matmul(p_y[:, 0:D], catT[:, :], wlr[:, bass.ds(layer, 1), :], start=True, stop=True).then_inc(S["mm_done"], 1)
            nc.tensor.transpose(p_t2[:, 0:LT * FC], b1_row[:, :], ident[0:LT * FC, 0:LT * FC]).then_inc(S["b1_done"], 1)

            def state_out(layer, n):
                wait_count(pe, S["hs_ready"], n + 1)
                nc.tensor.transpose(p_t[:, 0:P], hs[:, :], ident[:, :]).then_inc(S["hs_turned"], 1)
                wait_count(pe, S["hT_ready"], n + 1)
                nc.tensor.matmul(p_q[:, :], hT[:, :], wqkvs[:, bass.ds(layer, 1), :], start=True, stop=True).then_inc(S["proj_done"], 1)

            with pe.Fori(0, T) as t:
                wait_count(pe, S["x1_ready"], t + 1)
                nc.tensor.transpose(p_t[0:D, 0:P], xs1[:, :], ident[:, :]).then_inc(S["x1_turned"], 1)
                wait_count(pe, S["xT_ready"], t + 1)
                nc.tensor.matmul(p_y[:, 0:HID], xT[:, :], wi[:, :], start=True, stop=True).then_inc(S["hi_done"], 1)
                state_out(0, t)

            def feed_forward(n):
                wait_count(pe, S["h1_ready"], n + 1)
                nc.tensor.transpose(p_t2[:, 0:P], h1[:, :], ident[:, :]).then_inc(S["h1_turned"], 1)
                wait_count(pe, S["h1T_ready"], n + 1)
                for c in range(FC):
                    mm = nc.tensor.matmul(p_f1[:, c * P:(c + 1) * P], w1[:, c * P:(c + 1) * P], h1T[:, :], start=True, stop=True)
                mm.then_inc(S["f1_done"], 1)
                wait_count(pe, S["g_done"], n + 1)

            def feed_forward_out(layer):
                for c in range(FC):
                    mm = nc.tensor.matmul(p_f2[:, 0:HID], gT[:, c, :], w2[:, bass.ds(layer, 1), c, :], start=(c == 0), stop=(c == FC - 1))
                mm.then_inc(S["f2_done"], 1)

            with pe.Fori(0, LT - 1) as layer:
                wait_count(pe, S["w1_ld"], 16 * layer + 16)
                with pe.Fori(0, T) as t:
                    n = layer * T + t
                    feed_forward(n)
                    feed_forward_out(layer)
                    state_out(layer + 1, n + T)
            pe.wait_ge(S["w1_ld"], 16 * LT)
            with pe.Fori(0, T) as t:
                n = (LT - 1) * T + t
                feed_forward(n)
                feed_forward_out(LT - 1)
                wait_count(pe, S["hs_ready"], n + T + 1)
                nc.tensor.transpose(p_t[:, 0:P], hs[:, :], ident[:, :]).then_inc(S["hs_turned"], 1)
                wait_count(pe, S["hT_ready"], n + T + 1)
                nc.tensor.matmul(p_q[:, 0:D], hT[:, :], wo[:, :], start=True, stop=True).then_inc(S["proj_done"], 1)


def kernel(**inputs):
    import numpy as np
    import concourse.bacc as bacc
    from concourse import mybir as mb
    from concourse.bass_utils import run_bass_kernel_spmd as run

    a = {k: np.asarray(v) for k, v in inputs.items()}
    turned = lambda w: np.swapaxes(w, -1, -2)
    given = {
        "x": a["x"], "src": a["src"], "dst": a["dst"],
        "wlr": np.concatenate([a["L0_gnn_Wl"], a["L0_gnn_Wr"]], axis=1),
        "bl": a["L0_gnn_b"],
        "wi": a["L1_gnn_Wi"].T, "bi": a["L1_gnn_bi"][None],
        "wqkvs": np.concatenate([turned(a["L1_gnn_W" + c]) for c in "qkvs"], axis=2),
        "bqkvs": np.concatenate([a["L1_gnn_b" + c] for c in "qkvs"], axis=1),
        "wbeta": a["L1_gnn_Wbeta"][:, 0],
        "lng": a["L1_gnn_ln_g"], "lnb": a["L1_gnn_ln_b"],
        "w1t": turned(a["L1_gnn_W1"]), "b1": a["L1_gnn_b1"],
        "w2t": turned(a["L1_gnn_W2"]), "b2": a["L1_gnn_b2"],
        "wo": a["L1_gnn_Wo"].T, "bo": a["L1_gnn_bo"][None],
    }
    nc = bacc.Bacc("TRN2", target_bir_lowering=False, num_devices=1)
    arrays, t_in = {}, {}
    for name, v in given.items():
        v = np.ascontiguousarray(v)
        arrays["in_" + name] = v
        t_in[name] = nc.dram_tensor("in_" + name, v.shape, mb.dt.from_np(v.dtype), kind="ExternalInput").ap()
    out = nc.dram_tensor("out_0", a["x"].shape, mb.dt.float32, kind="ExternalOutput").ap()
    dbg = nc.dram_tensor("dbg", (256, 128, 8), mb.dt.int32, kind="ExternalOutput").ap() if DEBUG else None
    build(nc, t_in, out, dbg)
    r = run(nc, [arrays], core_ids=[0])
    return r.results[0]["out_0"]
```

```python
from contextlib import ExitStack

import concourse.bass as bass
from concourse import mybir

ALU = mybir.AluOpType
ACT = mybir.ActivationFunctionType
AX = mybir.AxisListType
F32 = mybir.dt.float32
BF16 = mybir.dt.bfloat16
I32 = mybir.dt.int32

P = 128
DEBUG = False


def build(nc, t_in, out, dbg=None):
    N, D = t_in["x"].shape
    E = t_in["src"].shape[0]
    HID = t_in["wqkvs"].shape[1]
    LS, LT = t_in["wlr"].shape[0], t_in["wqkvs"].shape[0]
    FF = t_in["w1t"].shape[2]
    HEADS = 8
    DH = HID // HEADS
    VW = DH + 1
    KV = HID + HEADS * VW
    FC = FF // P
    T = -(-N // P)
    NP = T * P
    LAST = N - (T - 1) * P
    DUMMY = NP
    CH = 8
    CH_LOG = 3
    NB = 4
    GMAX = T + E // CH + NB
    EJ = -(-E // P)
    EL = E - (P - 1) * EJ
    JB = next(j for j in range(32, 0, -1) if EJ % (2 * j) == 0)
    DEG_CLAMP = 4095.0
    NEG = -1.0e30
    ZW = 512
    Z_STORES = 16 * (3 + -(-((E + CH) // ZW) // P))
    G = next(g for g in (5, 4, 3, 2, 1) if T % g == 0)
    SS = 64
    SC = SS // CH
    LO = 32
    HI = NP // LO
    PAIRS = -(-T // 2)
    Q = 32
    W_LOADS = 16 * (2 + LT + 2 + 1 + 6 + 2)

    ctx = ExitStack()
    with ctx:
        def sb(name, shape, dt=F32):
            return ctx.enter_context(nc.sbuf_tensor(name, shape, dt))

        def ps(name):
            return ctx.enter_context(nc.psum_tensor(name, [P, 512], F32))

        def sem(name):
            return ctx.enter_context(nc.semaphore(name))

        def dram(name, shape, dt=F32):
            return nc.dram_tensor(name, shape, dt, kind="Internal").ap()

        src_run = dram("src_run", (2 * E + CH + P,), I32)
        natural = dram("natural", (3, 64 * 64))
        posrec = dram("posrec", (NP, 4), I32)
        slot_ids = dram("slot_ids", (GMAX + NB, P, CH), I32)
        xtab = dram("xtab", (NP + 1, D))
        kvtab = dram("kvtab", (NP + 1, KV))
        counts = dram("counts", (2 * PAIRS, HI, P * LO), BF16)

        diff_i = sb("diff_i", [P, P], I32)
        ident = sb("ident", [P, P])
        upper = sb("upper", [P, P])
        iota64_i = sb("iota64_i", [P, P], I32)
        iota64 = sb("iota64", [P, P], BF16)
        iota8 = sb("iota8", [P, CH])
        node_i = sb("node_i", [P, T], I32)
        nodekey_i = sb("nodekey_i", [64, 64], I32)
        nodekey = sb("nodekey", [64, 64])
        zeros = sb("zeros", [P, ZW])
        posn = sb("posn", [P, T, 4], I32)
        deg_pos = sb("deg_pos", [P, T])
        off_pos = sb("off_pos", [P, T])
        inv_cnt = sb("inv_cnt", [P, T])
        chunks_f = sb("chunks_f", [32, 4])
        chunks_i = sb("chunks_i", [32, 4], I32)
        meta = sb("meta", [1, 32], I32)
        meta_f = sb("meta_f", [1, 4])
        meta_i = sb("meta_i", [1, 4], I32)

        pool_a = sb("pool_a", [P, NB * CH * KV])
        pool_b = sb("pool_b", [P, T * KV])
        dst_i = pool_b[:, 0:EJ].bitcast(I32)
        dhi_i = pool_b[:, EJ:2 * EJ].bitcast(I32)
        dhi = pool_b[:, 2 * EJ:3 * EJ]
        dlo = pool_b[:, 3 * EJ:4 * EJ]
        dnext = pool_b[:, 4 * EJ:5 * EJ].bitcast(I32)
        src_i = pool_b[:, 5 * EJ:6 * EJ].bitcast(I32)
        s_a, s_b, s_m, s_n = (pool_a[:, P * i:P * i + P] for i in range(4))
        s_at, s_bt = (pool_a[0:64, P * i:P * i + P] for i in (4, 5))
        s_next = pool_a[0:64, 6 * P:6 * P + 64]
        s_before = pool_a[:, 7 * P:8 * P]
        s_col = pool_a[:, 8 * P:8 * P + 8]
        s_place = pool_a[:, 8 * P + 8:8 * P + 9].bitcast(I32)
        s_src = pool_a[:, 8 * P + 9:8 * P + 10].bitcast(I32)
        disorder = sb("disorder", [P, 2])
        hot_hi = [pool_a[:, JB * 32 * u:JB * 32 * (u + 1)].bitcast(BF16).rearrange("p (j c) -> p j c", c=64) for u in range(2)]
        hot_lo = [pool_a[:, JB * 32 * (2 + u):JB * 32 * (3 + u)].bitcast(BF16).rearrange("p (j c) -> p j c", c=64) for u in range(2)]
        keys_bc = pool_a[:, 0:NP]
        greater = pool_a[:, NP:2 * NP]
        deg_nat = sb("deg_nat", [64, 64])
        off_nat = sb("off_nat", [64, 64])
        key_nat = sb("key_nat", [64, 64])
        rowsum = sb("rowsum", [64, 2])
        nat_row = sb("nat_row", [T, 3, P])
        nat_col = sb("nat_col", [P, 3, T])
        rank_f = sb("rank_f", [P, T])
        rank_i = sb("rank_i", [P, T], I32)
        rec = sb("rec", [P, T, 4], I32)

        run_at = sb("run_at", [P, 1])
        run_i = sb("run_i", [P, NB, 1], I32)
        raw = sb("raw", [P, NB, CH], I32)
        left = sb("left", [P, 1])
        valid = sb("valid", [P, CH])
        rawf = sb("rawf", [P, CH])
        ids_out = sb("ids_out", [P, NB, CH], I32)

        ids = sb("ids", [P, NB, CH], I32)
        xs = pool_a[:, 0:NB * CH * D].rearrange("p (u s d) -> p u s d", u=NB, s=CH)
        kv = pool_a[:, :].rearrange("p (u s d) -> p u s d", u=NB, s=CH)
        xp = pool_b[:, 0:T * D].rearrange("p (t d) -> p t d", d=D)
        kvn = pool_b[:, :].rearrange("p (t d) -> p t d", d=KV)

        x0 = sb("x0", [P, T, D])
        agg = sb("agg", [P, D])
        part = sb("part", [P, D])
        cat = sb("cat", [P, P])
        catT = sb("catT", [P, P])
        wlr = sb("wlr", [P, LS, D])
        bl_bc = sb("bl_bc", [P, LS, D])
        floors = sb("floors", [P, LS])

        wi = sb("wi", [D, HID])
        wqkvs = sb("wqkvs", [P, LT, 4 * HID])
        w1 = sb("w1", [P, FF])
        w2 = sb("w2", [P, LT, FC, HID])
        wo = sb("wo", [P, D])
        bi_bc = sb("bi_bc", [P, HID])
        ones_row = sb("ones_row", [1, P])
        bqkvs_row = sb("bqkvs_row", [1, LT, 4 * HID])
        b2_row = sb("b2_row", [1, LT, HID])
        wbeta_bc = sb("wbeta_bc", [P, LT, 3 * HID])
        lng_bc = sb("lng_bc", [P, LT, HID])
        lnb_bc = sb("lnb_bc", [P, LT, HID])
        bo_bc = sb("bo_bc", [P, D])
        b1_row = sb("b1_row", [LT * FC, P])
        b1_all = sb("b1_all", [P, LT * FC])
        b1 = sb("b1", [P, FC])
        arena = sb("arena", [P, 3, T, HID])
        h_all = arena[:, 0, :, :]
        q_all = arena[:, 1, :, :]
        r_all = arena[:, 2, :, :]
        y_all = sb("y_all", [P, T, D])
        q_t = sb("q_t", [P, HID])
        prod = sb("prod", [P, CH, HID])
        empty = sb("empty", [P, CH])
        score = sb("score", [P, HEADS, CH + 1])
        top = sb("top", [P, HEADS])
        delta = sb("delta", [P, 2, HEADS, CH + 1])
        expo = sb("expo", [P, 2, HEADS, CH + 1])
        wv = sb("wv", [P, 2, CH + 1, HEADS * VW])
        acc = sb("acc", [P, G, HEADS * VW])
        rden = sb("rden", [P, G, HEADS])
        tri = sb("tri", [P, G, 3, HID])
        gate = sb("gate", [P, 4, G])
        y = sb("y", [P, G, HID])
        stats = sb("stats", [P, T, 6])
        mv = sb("mv", [P, T, 2])
        std = sb("std", [P, T])
        rstd = sb("rstd", [P, T])
        h1 = sb("h1", [P, G, HID])
        hs = sb("hs", [P, G, HID])
        turned_work = sb("turned_work", [P, 2 * G * P + 2 * FC * P])
        h1T = turned_work[:, 0:G * P]
        hT = turned_work[:, G * P:2 * G * P]
        gT = turned_work[:, 2 * G * P:].rearrange("p (u c k) -> p u c k", u=2, c=FC)
        triw = turned_work[:, 0:G * 3 * HID].rearrange("p (i f) -> p i f", i=G)

        NC = G
        free_a = arena[:, :, :, :].rearrange("p a t d -> p (a t d)")
        def half(base, at, n):
            return base[:, at:at + n // 2].bitcast(BF16)
        cw = P * LO // 2
        in_a = 3 * T * HID // cw
        where = [(free_a, i * cw) for i in range(in_a)] + [(pool_a, 5 * LO * D // 2 + i * cw) for i in range(NC - in_a)]
        cnt = [half(space, at, P * LO)[0:HI, :].rearrange("a (d b) -> a d b", b=LO) for space, at in where[:NC]]
        xnat = pool_a[0:HI, 0:LO * D].rearrange("a (b f) -> a b f", b=LO)
        x3 = half(pool_a, LO * D, LO * 3 * D)[0:HI, :].rearrange("a (b c f) -> a b c f", b=LO, c=3)
        slot_f = pool_a[:, 0:T * SS].rearrange("p (t s) -> p t s", s=SS)
        slot_v = pool_a[:, T * SS:2 * T * SS].rearrange("p (t s) -> p t s", s=SS)
        raw64 = pool_a[:, 2 * T * SS:3 * T * SS].bitcast(I32).rearrange("p (t s) -> p t s", s=SS)
        slot_i = pool_a[:, 3 * T * SS:4 * T * SS].bitcast(I32).rearrange("p (t s) -> p t s", s=SS)
        a_at = 0
        halves = free_a[:, a_at:a_at + 2 * 2 * PAIRS * SS].rearrange("p (c t s) -> p c t s", c=2, s=SS)
        a_at += 2 * 2 * PAIRS * SS
        halvesT = half(free_a, a_at, PAIRS * 2 * P).rearrange("p (k c d) -> p k c d", k=PAIRS, c=2)
        a_at += PAIRS * P
        hots = []
        for _ in range(2):
            hots.append((half(free_a, a_at, Q * HI).rearrange("p (d a) -> p d a", a=HI),
                         half(free_a, a_at + Q * HI // 2, Q * LO).rearrange("p (d b) -> p d b", b=LO)))
            a_at += Q * (HI + LO) // 2
        assert a_at <= 3 * T * HID
        SL = (T * SS + (NB - 1) * CH)
        slot_list = pool_b[:, T * D:T * D + SL].bitcast(I32)
        cq = half(pool_b, T * D + SL, 4 * Q * LO)[0:HI, :].rearrange("a (v c f) -> a v c f", v=2, c=2)

        psum = [ps(f"psum{i}") for i in range(8)]
        p_hist, p_t, p_y = psum[0:3]
        p_big = psum[4:6]
        p_turn = psum[0:2]
        p_wide = psum[2:4]
        p_f2 = psum[4:6]
        p_acc = psum[6]
        p_t2 = psum[7]

        names = """const_pool const_dve dst_free dst_ld src_ld zero_st hot_ready hot_used hist_done
            pre_ready pre_done nat_ready nat_st nat_ld nat_ldb nat_turned rec_ready rec_st pos_ld deg_ready degT_done
            cnt_ready base_done meta_ready run_ready raw_in ids_ready ids_stored xgath
            x_ready x_st w_ld w_free catp catt catc mm_done y_free
            out_ready out_st past_wait ones_ready b1_done b1_used w1_ld kv_ready kv_st d_ready e_done z_ready z_done var_ready std_done h1_ready h1_turned h1T_ready f1_done g_done f2_done hs_ready hs_turned hT_ready proj_done x1_ready x1_turned xT_ready hi_done hi_ready gelu_done fvar_ready fstd_done h_saved w_ready sum_done acc_saved o_done
            raw64_ld lists_ready lists_st halves_ready halves_turned halvesT_ready halvesT_saved hot2_ready hot2_used
            next_ld src_i_ld disorder_ready disorder_done s_hot s_turned s_copied s_product s_placed s_stored
            cq_ready counts_st xnat_ld x3_ready big_done dbg_s""".split()
        S = {n: sem(n) for n in names}
        raw_ld = [sem(f"raw_ld{u}") for u in range(NB)]
        ids_st = [sem(f"ids_st{u}") for u in range(NB)]
        SG, TR = [([sem(f"{w}_ids_ld{u}") for u in range(NB)], [sem(f"{w}_rows_ld{u}") for u in range(NB)],
                   sem(f"{w}_chunk_done"), sem(f"{w}_gathered")) for w in ("sage", "tran")]
        cq_st = [sem(f"cq_st{v}") for v in range(2)]
        cnt_ld = [sem(f"cnt_ld{i}") for i in range(NC)]

        def base(eng, t):
            return eng.value_load(meta[0:1, bass.ds(t, 1)], min_val=0, max_val=GMAX)

        def disordered(eng):
            return eng.value_load(meta[0:1, 30:31], min_val=0, max_val=E)

        def chunk_total(eng):
            return eng.value_load(meta[0:1, T:T + 1], min_val=NB, max_val=GMAX)

        def wait_count(eng, semaphore, count):
            eng.wait_ge(semaphore, count)
            eng.sem_inc(S["past_wait"], 1)

        block = ctx.enter_context(nc.Block())

        @block.sync
        def _(sp):
            sp.dma_start(src_run[0:E].rearrange("(a b) -> a b", a=625),
                         t_in["src"].rearrange("(a b) -> a b", a=625)).then_inc(S["src_ld"], 16)
            sp.dma_start(xtab[0:N, :], t_in["x"]).then_inc(S["src_ld"], 16)
            sp.wait_ge(S["dst_free"], 1)
            sp.dma_start(dst_i[0:P - 1, :], t_in["dst"][0:(P - 1) * EJ].rearrange("(p j) -> p j", j=EJ)).then_inc(S["dst_ld"], 16)
            sp.dma_start(dst_i[P - 1:P, 0:EL], t_in["dst"][(P - 1) * EJ:E].rearrange("(p j) -> p j", p=1)).then_inc(S["dst_ld"], 16)
            sp.dma_start(dnext[0:P - 1, :], t_in["dst"][1:(P - 1) * EJ + 1].rearrange("(p j) -> p j", j=EJ)).then_inc(S["next_ld"], 16)
            sp.dma_start(dnext[P - 1:P, 0:EL - 1], t_in["dst"][(P - 1) * EJ + 1:E].rearrange("(p j) -> p j", p=1)).then_inc(S["next_ld"], 16)
            sp.dma_start(src_i[0:P - 1, :], t_in["src"][0:(P - 1) * EJ].rearrange("(p j) -> p j", j=EJ)).then_inc(S["src_i_ld"], 16)
            sp.dma_start(src_i[P - 1:P, 0:EL], t_in["src"][(P - 1) * EJ:E].rearrange("(p j) -> p j", p=1)).then_inc(S["src_i_ld"], 16)
            sp.wait_ge(S["const_dve"], 1)
            zi = zeros[:, :].bitcast(I32)
            n_tail = E + CH
            rows = n_tail // ZW
            for r in range(0, rows, P):
                m = min(P, rows - r)
                sp.dma_start(src_run[E + r * ZW:E + (r + m) * ZW].rearrange("(p j) -> p j", j=ZW), zi[0:m, :]).then_inc(S["zero_st"], 16)
            sp.dma_start(src_run[E + rows * ZW:2 * E + CH].rearrange("(p j) -> p j", p=1), zi[0:1, 0:n_tail - rows * ZW]).then_inc(S["zero_st"], 16)
            sp.dma_start(xtab[N:NP + 1, :], zeros[0:NP + 1 - N, 0:D]).then_inc(S["zero_st"], 16)
            sp.dma_start(kvtab[DUMMY:DUMMY + 1, :], zeros[0:1, 0:KV]).then_inc(S["zero_st"], 16)
            for tile, name in ((wlr, "wlr"), (wqkvs, "wqkvs")):
                sp.dma_start(tile[:, :, :], t_in[name].rearrange("l k n -> k l n")).then_inc(S["w_ld"], 16)
            for layer in range(LT):
                sp.dma_start(w2[:, layer, :, :], t_in["w2t"][layer].rearrange("(c k) n -> k c n", k=P)).then_inc(S["w_ld"], 16)
            for tile, name in ((wi, "wi"), (wo, "wo")):
                sp.dma_start(tile[:, :], t_in[name]).then_inc(S["w_ld"], 16)
            sp.dma_start(b1_row[:, :], t_in["b1"].rearrange("l (c k) -> (l c) k", k=P)).then_inc(S["w_ld"], 16)
            for tile, name in ((bl_bc, "bl"), (wbeta_bc, "wbeta"), (lng_bc, "lng"), (lnb_bc, "lnb")):
                flat = t_in[name].rearrange("(a l) n -> a (l n)", a=1)
                sp.dma_start(tile[:, :, :].rearrange("p l n -> p (l n)"), flat.partition_broadcast(P)).then_inc(S["w_ld"], 16)
            for tile, name in ((bqkvs_row, "bqkvs"), (b2_row, "b2")):
                sp.dma_start(tile[:, :, :], t_in[name].rearrange("(a l) n -> a l n", a=1)).then_inc(S["w_ld"], 16)
            for tile, name in ((bi_bc, "bi"), (bo_bc, "bo")):
                sp.dma_start(tile[:, :], t_in[name].partition_broadcast(P)).then_inc(S["w_ld"], 16)
            sp.wait_ge(S["nat_ready"], 1)
            for i, t in enumerate((key_nat, off_nat, deg_nat)):
                sp.dma_start(natural[i, :].rearrange("(a b) -> a b", b=64), t[:, :]).then_inc(S["nat_st"], 16)
            sp.wait_ge(S["nat_st"], 48)
            sp.dma_start(keys_bc, natural[0:1, 0:NP].partition_broadcast(P)).then_inc(S["nat_ldb"], 16)
            for i in range(3):
                sp.dma_start(nat_row[:, i, :], natural[i, 0:NP].rearrange("(t p) -> t p", p=P)).then_inc(S["nat_ld"], 16)
            sp.wait_ge(S["rec_st"], 16 * T)
            sp.dma_start(posn[:, :, :], posrec.rearrange("(t p) c -> p t c", p=P)).then_inc(S["pos_ld"], 16)

            sp.wait_ge(S["meta_ready"], 1)
            total = chunk_total(sp)
            def feed(sems, layers, before=None):
                ids_ld, rows_ld, chunk_done, gathered = sems
                sp.sem_inc(chunk_done, NB)
                with sp.Fori(0, layers) as layer:
                    if before:
                        before(layer)
                    with sp.Fori(0, total, NB) as g:
                        q = layer * total + g
                        k = q // NB
                        for u in range(NB):
                            wait_count(sp, chunk_done, q + (u + 1))
                            sp.dma_start(ids[:, u, :], slot_ids[bass.ds(g + u, 1), :, :].rearrange("a p s -> (a p) s")).then_inc(ids_ld[u], 16)
                            if u >= 2:
                                wait_count(sp, rows_ld[u - 2], 16 * CH * k + 16 * CH)
                                sp.sem_inc(gathered, 1)
                            else:
                                with sp.If(g > 0):
                                    wait_count(sp, rows_ld[u + NB - 2], 16 * CH * k)
                                    sp.sem_inc(gathered, 1)
                    kl = (layer + 1) * total // NB
                    for u in range(NB - 2, NB):
                        wait_count(sp, rows_ld[u], 16 * CH * kl)
                        sp.sem_inc(gathered, 1)

            def lists_by_chunk():
                with sp.Fori(0, total, NB) as g:
                    k = g // NB
                    for u in range(NB):
                        wait_count(sp, raw_ld[u], 16 * k + 16)
                        sp.sem_inc(S["raw_in"], 1)
                        wait_count(sp, S["ids_ready"], g + (u + 1))
                        sp.dma_start(slot_ids[bass.ds(g + u, 1), :, :].rearrange("a p s -> (a p) s"), ids_out[:, u, :]).then_inc(ids_st[u], 16)
                    for u in range(NB):
                        wait_count(sp, ids_st[u], 16 * k + 16)
                    sp.sem_inc(S["ids_stored"], NB)

            def lists_and_counts():
                sp.wait_ge(S["lists_ready"], 1)
                with sp.Fori(0, T) as t:
                    lo = base(sp, t)
                    with sp.Fori(lo, base(sp, t + 1)) as g:
                        at = (t * SS + (g - lo) * CH).with_bounds(min_val=0, max_val=SL - CH)
                        sp.dma_start(slot_ids[bass.ds(g, 1), :, :].rearrange("a p s -> (a p) s"), slot_list[:, bass.ds(at, CH)]).then_inc(S["lists_st"], 16)
                with sp.Fori(0, PAIRS) as k:
                    for v in range(4):
                        wait_count(sp, S["cq_ready"], 4 * k + (v + 3))
                        sp.dma_start(counts[bass.ds(2 * k, 2), :, v * Q * LO:(v + 1) * Q * LO].rearrange("c a f -> a c f"), cq[:, v % 2, :, :]).then_inc(cq_st[v % 2], 16)
                for v in range(2):
                    sp.wait_ge(cq_st[v], 16 * 2 * PAIRS)
                wait_count(sp, S["lists_st"], total * 16)

            def counts_in():
                with sp.Fori(0, LS) as layer:
                    with sp.If(layer > 0):
                        wait_count(sp, S["x_st"], layer * (16 * T))
                        wait_count(sp, S["mm_done"], layer * T)
                    sp.dma_start(xnat.rearrange("a b f -> a (b f)"), xtab[0:NP, :].rearrange("(a b) f -> a (b f)", b=LO)).then_inc(S["xnat_ld"], 16)
                    load_counts(layer)

            def load_counts(layer):
                with sp.Fori(0, T // G) as j:
                    for i in range(G):
                        n = layer * T + j * G + i
                        wait_count(sp, S["big_done"], n + 1)
                        sp.dma_start(cnt[i].rearrange("a d b -> a (d b)"), counts[bass.ds(j * G + i, 1), :, :].rearrange("c a f -> (c a) f")).then_inc(cnt_ld[i], 16)

            with sp.If(base(sp, 1) > SC):
                lists_by_chunk()
                feed(SG, LS)
            with sp.Else():
                lists_and_counts()
                counts_in()
            sp.sem_inc(S["f1_done"], 1)

            def load_w1(layer):
                wait_count(sp, S["f1_done"], layer * T + 1)
                sp.dma_start(w1[:, :], t_in["w1t"][bass.ds(layer, 1), :, :].rearrange("a k n -> (a k) n")).then_inc(S["w1_ld"], 16)

            feed(TR, LT, load_w1)
            sp.wait_ge(S["out_st"], 16 * T)

        @block.gpsimd
        def _(pool):
            nc.gpsimd.iota(diff_i[:, :], pattern=[[1, P]], base=0, channel_multiplier=-1).then_inc(S["const_pool"], 1)
            nc.gpsimd.iota(iota64_i[:, :], pattern=[[1, P]], base=0, channel_multiplier=0).then_inc(S["const_pool"], 1)
            nc.gpsimd.iota(node_i[:, :], pattern=[[P, T]], base=0, channel_multiplier=1).then_inc(S["const_pool"], 1)
            nc.gpsimd.iota(nodekey_i[:, :], pattern=[[-1, 64]], base=4095, channel_multiplier=-64).then_inc(S["const_pool"], 1)
            pool.wait_ge(S["rec_ready"], 1)
            for t in range(T):
                pool.indirect_dma_start(posrec, bass.IndirectOffsetOnAxis(ap=rank_i[:, t:t + 1], axis=0),
                                        rec[:, t, :], None).then_inc(S["rec_st"], 16)
            pool.wait_ge(S["pos_ld"], 16)
            pool.wait_ge(S["src_ld"], 32)
            pool.wait_ge(S["zero_st"], Z_STORES)
            for t in range(T):
                pool.indirect_dma_start(x0[:, t, :], None, xtab,
                                        bass.IndirectOffsetOnAxis(ap=posn[:, t, 0:1], axis=0)).then_inc(S["xgath"], 16)
            pool.wait_ge(S["meta_ready"], 1)
            total = chunk_total(pool)
            runs = src_run.rearrange("(n a) -> n a", a=1)

            def run_by_chunk():
                with pool.Fori(0, total, NB) as g:
                    for u in range(NB):
                        wait_count(pool, S["run_ready"], g + (u + 1))
                        pool.indirect_dma_start(raw[:, u, :], None, runs,
                                                bass.IndirectOffsetOnAxis(ap=run_i[:, u, :], axis=0)).then_inc(raw_ld[u], 16)

            def gather(sems, layer, table, rows):
                ids_ld, rows_ld = sems[0:2]
                with pool.Fori(0, total, NB) as g:
                    k = (layer * total + g) // NB
                    for u in range(NB):
                        wait_count(pool, ids_ld[u], 16 * k + 16)
                        for s in range(CH):
                            pool.indirect_dma_start(rows[:, u, s, :], None, table,
                                                    bass.IndirectOffsetOnAxis(ap=ids[:, u, s:s + 1], axis=0)).then_inc(rows_ld[u], 16)

            def all_read(sems, layer):
                for u in range(NB):
                    wait_count(pool, sems[1][u], 16 * CH * ((layer + 1) * total // NB))

            def store(table, rows, ready, stored, count):
                for t in range(T):
                    wait_count(pool, ready, count * T + (t + 1))
                    pool.indirect_dma_start(table, bass.IndirectOffsetOnAxis(ap=posn[:, t, 0:1], axis=0),
                                            rows[:, t, :], None).then_inc(stored, 16)
                wait_count(pool, stored, count * (16 * T) + 16 * T)

            with pool.If(disordered(pool) > 0):
                with pool.Fori(0, EJ) as j:
                    wait_count(pool, S["s_placed"], j + 1)
                    pool.indirect_dma_start(runs, bass.IndirectOffsetOnAxis(ap=s_place, axis=0), s_src, None).then_inc(S["s_stored"], 16)
                    wait_count(pool, S["s_stored"], 16 * j + 16)
            with pool.If(base(pool, 1) > SC):
                run_by_chunk()
                with pool.Fori(0, LS - 1) as layer:
                    gather(SG, layer, xtab, xs)
                    all_read(SG, layer)
                    store(xtab, xp, S["x_ready"], S["x_st"], layer)
                gather(SG, LS - 1, xtab, xs)
            with pool.Else():
                for t in range(T):
                    pool.indirect_dma_start(raw64[:, t, :], None, runs,
                                            bass.IndirectOffsetOnAxis(ap=posn[:, t, 1:2], axis=0)).then_inc(S["raw64_ld"], 16)
                with pool.Fori(0, LS - 1) as layer:
                    wait_count(pool, S["xnat_ld"], 16 * layer + 16)
                    store(xtab, xp, S["x_ready"], S["x_st"], layer)
            pool.wait_ge(S["x_ready"], LS * T)
            store(kvtab, kvn, S["kv_ready"], S["kv_st"], 0)
            with pool.Fori(0, LT - 1) as layer:
                gather(TR, layer, kvtab, kv)
                all_read(TR, layer)
                store(kvtab, kvn, S["kv_ready"], S["kv_st"], layer + 1)
            gather(TR, LT - 1, kvtab, kv)
            for t in range(T):
                pool.wait_ge(S["out_ready"], t // G + 1)
                m = P if t < T - 1 else LAST
                pool.indirect_dma_start(out, bass.IndirectOffsetOnAxis(ap=posn[0:m, t, 0:1], axis=0),
                                        y_all[0:m, t, :], None).then_inc(S["out_st"], 16)

        @block.vector
        def _(dve):
            nc.vector.memset(dst_i, -1)
            nc.vector.memset(src_i, 0)
            nc.vector.memset(dnext, 1 << 20).then_inc(S["dst_free"], 1)
            nc.vector.memset(zeros[:, :], 0.0).then_inc(S["const_dve"], 1)
            nc.vector.memset(floors[:, 0:LS - 1], 0.0)
            nc.vector.memset(floors[:, LS - 1:LS], -3.0e38)
            dve.wait_ge(S["const_pool"], 4)
            nc.vector.tensor_scalar(ident[:, :], diff_i[:, :], 0.0, None, ALU.is_equal)
            nc.vector.tensor_scalar(upper[:, :], diff_i[:, :], 0.0, None, ALU.is_gt)
            nc.vector.tensor_copy(iota64[:, :], iota64_i[:, :])
            nc.vector.tensor_copy(iota8[:, :], iota64_i[:, 0:CH])
            nc.vector.tensor_copy(nodekey[:, :], nodekey_i[:, :])

            dve.wait_ge(S["dst_ld"], 32)
            dve.wait_ge(S["next_ld"], 32)
            nc.vector.memset(disorder[:, 1:2], 1.0)
            nc.vector.tensor_tensor(dhi, dst_i, dnext, ALU.is_gt)
            dve.drain()
            nc.vector.tensor_reduce(disorder[:, 0:1], dhi, AX.X, ALU.add)
            dve.drain().then_inc(S["disorder_ready"], 1)
            nc.vector.tensor_scalar(dhi_i, dst_i, 6, None, ALU.arith_shift_right)
            dve.drain()
            nc.vector.tensor_copy(dhi, dhi_i)
            nc.vector.tensor_scalar(dst_i, dst_i, 63, None, ALU.bitwise_and)
            dve.drain()
            nc.vector.tensor_copy(dlo, dst_i)
            dve.drain().then_inc(S["const_dve"], 1)
            with dve.Fori(0, EJ // (2 * JB)) as i:
                for u in range(2):
                    wait_count(dve, S["hot_used"], 2 * i + (u + 1))
                    grid = iota64[:, 0:64].unsqueeze(1).to_broadcast((P, JB, 64))
                    for hot, half in ((hot_hi, dhi), (hot_lo, dlo)):
                        ins = nc.vector.tensor_tensor(
                            hot[u], grid,
                            half[:, bass.ds(i * (2 * JB) + u * JB, JB)].unsqueeze(2).to_broadcast((P, JB, 64)),
                            ALU.is_equal)
                    ins.then_inc(S["hot_ready"], 1)
            dve.wait_ge(S["hist_done"], 1)
            nc.vector.tensor_copy(deg_nat[:, :], p_hist[0:64, 0:64])
            nc.vector.tensor_reduce(rowsum[:, 0:1], p_hist[0:64, 0:64], AX.X, ALU.add).then_inc(S["pre_ready"], 1)
            dve.drain()
            nc.vector.tensor_scalar(key_nat[:, :], deg_nat[:, :], DEG_CLAMP, 4096.0, ALU.min, ALU.mult)
            dve.drain()
            nc.vector.tensor_tensor(key_nat[:, :], key_nat[:, :], nodekey[:, :], ALU.add)
            dve.wait_ge(S["pre_done"], 1)
            nc.vector.tensor_copy(rowsum[:, 1:2], p_y[0:64, 0:1])
            dve.drain()
            nc.vector.tensor_tensor_scan(off_nat[:, :], deg_nat[:, :], zeros[0:64, 0:64], rowsum[:, 1:2], ALU.add, ALU.add)
            dve.drain()
            nc.vector.tensor_tensor(off_nat[:, :], off_nat[:, :], deg_nat[:, :], ALU.subtract).then_inc(S["nat_ready"], 1)
            dve.wait_ge(S["nat_ldb"], 16)
            dve.wait_ge(S["nat_turned"], 3)
            nc.vector.tensor_copy(nat_col[:, :, :].rearrange("p c t -> p (c t)"), p_t[:, 0:3 * T])
            dve.drain()
            for t in range(T):
                if t:
                    dve.drain()
                nc.vector.tensor_scalar(greater, keys_bc, nat_col[:, 0, t:t + 1], 0.0, ALU.is_gt, ALU.add,
                                        accum_out=rank_f[:, t:t + 1])
            nc.vector.tensor_copy(rec[:, :, 0], node_i[:, :])
            nc.vector.tensor_copy(rec[:, :, 1], nat_col[:, 1, :])
            nc.vector.tensor_copy(rec[:, :, 2], nat_col[:, 2, :])
            nc.vector.tensor_copy(rec[:, :, 3], node_i[:, :])
            dve.drain()
            nc.vector.tensor_copy(rank_i[:, :], rank_f[:, :])
            dve.drain().then_inc(S["rec_ready"], 1)
            dve.wait_ge(S["pos_ld"], 16)
            nc.vector.tensor_copy(off_pos[:, :], posn[:, :, 1])
            nc.vector.tensor_copy(deg_pos[:, :], posn[:, :, 2])
            dve.drain().then_inc(S["deg_ready"], 1)
            nc.vector.tensor_scalar(inv_cnt[:, :], deg_pos[:, :], 1.0, None, ALU.max)
            dve.drain()
            nc.vector.reciprocal(inv_cnt[:, :], inv_cnt[:, :])
            dve.wait_ge(S["degT_done"], 1)
            nc.vector.tensor_reduce(chunks_f[0:T, 0:1], p_t[0:T, 0:P], AX.X, ALU.max)
            dve.drain()
            nc.vector.tensor_scalar(chunks_i[0:T, 0:1], chunks_f[0:T, 0:1], float(CH - 1), float(CH), ALU.add, ALU.max)
            dve.drain()
            nc.vector.tensor_scalar(chunks_i[0:T, 1:2], chunks_i[0:T, 0:1], CH_LOG, None, ALU.arith_shift_right)
            dve.drain()
            nc.vector.tensor_copy(chunks_f[0:T, 1:2], chunks_i[0:T, 1:2])
            dve.drain().then_inc(S["cnt_ready"], 1)
            dve.wait_ge(S["base_done"], 1)
            nc.vector.tensor_copy(meta[0:1, 0:T + 1], p_y[0:1, 0:T + 1])
            nc.vector.tensor_copy(meta[0:1, 30:31], p_y[0:1, 64:65])
            nc.vector.tensor_scalar(meta_i[0:1, 0:1], p_y[0:1, T:T + 1], float(NB - 1), None, ALU.add)
            dve.drain()
            nc.vector.tensor_scalar(meta[0:1, T:T + 1], meta_i[0:1, 0:1], -NB, None, ALU.bitwise_and)
            dve.drain().then_inc(S["meta_ready"], 1)

            def mask_by_chunk():
                with dve.Fori(0, T) as t:
                    dve.drain()
                    nc.vector.tensor_copy(left[:, :], deg_pos[:, bass.ds(t, 1)])
                    with dve.Fori(base(dve, t), base(dve, t + 1)) as g:
                        u = g % NB
                        wait_count(dve, S["raw_in"], g + 1)
                        dve.drain()
                        nc.vector.tensor_scalar(valid[:, :], iota8[:, :], left[:, 0:1], None, ALU.is_lt)
                        nc.vector.tensor_scalar(rawf[:, :], raw[:, bass.ds(u, 1), :], -float(DUMMY), None, ALU.add)
                        dve.drain()
                        nc.vector.tensor_scalar(left[:, :], left[:, :], -float(CH), None, ALU.add)
                        nc.vector.tensor_tensor(rawf[:, :], rawf[:, :], valid[:, :], ALU.mult)
                        wait_count(dve, S["ids_stored"], g + 1)
                        dve.drain()
                        nc.vector.tensor_scalar(ids_out[:, bass.ds(u, 1), :], rawf[:, :], float(DUMMY), None, ALU.add).then_inc(S["ids_ready"], 1)

            def sage_output(t, layer):
                wait_count(dve, S["mm_done"], layer * T + t + 1)
                nc.vector.tensor_tensor(part[:, :], p_y[:, 0:D], bl_bc[:, bass.ds(layer, 1), :], ALU.add)
                dve.drain()
                nc.vector.tensor_scalar(xp[:, bass.ds(t, 1), :], part[:, :], floors[:, bass.ds(layer, 1)], None, ALU.max)
                dve.drain().then_inc(S["x_ready"], 1)

            def sage_by_gather():
                with dve.Fori(0, LS) as layer:
                    with dve.Fori(0, T) as t:
                        dve.drain()
                        nc.vector.memset(agg[:, :], 0.0)
                        with dve.Fori(base(dve, t), base(dve, t + 1)) as g:
                            wait_count(dve, SG[3], layer * total + g + 1)
                            dve.drain()
                            nc.vector.tensor_reduce(part[:, :], xs[:, bass.ds(g % NB, 1), :, :].rearrange("p u s d -> p d (u s)"),
                                                    AX.X, ALU.add).then_inc(SG[2], 1)
                            dve.drain()
                            nc.vector.tensor_tensor(agg[:, :], agg[:, :], part[:, :], ALU.add)
                        dve.drain()
                        nc.vector.tensor_scalar(cat[:, 0:D], agg[:, :], inv_cnt[:, bass.ds(t, 1)], None, ALU.mult)
                        nc.vector.tensor_copy(cat[:, D:2 * D], xp[:, bass.ds(t, 1), :])
                        dve.drain().then_inc(S["catp"], 1)
                        sage_output(t, layer)

            def build_counts():
                dve.wait_ge(S["raw64_ld"], 16 * T)
                nc.vector.tensor_scalar(slot_f, raw64, 1.0, None, ALU.add)
                nc.vector.tensor_tensor(slot_v, iota64[:, 0:SS].unsqueeze(1).to_broadcast((P, T, SS)),
                                        deg_pos[:, :].unsqueeze(2).to_broadcast((P, T, SS)), ALU.is_lt)
                nc.vector.memset(slot_list[:, T * SS:SL], DUMMY)
                nc.vector.memset(halves[:, 0, T:2 * PAIRS, :], -1.0)
                nc.vector.memset(halves[:, 1, T:2 * PAIRS, :], -1.0)
                dve.drain()
                nc.vector.tensor_tensor(slot_f, slot_f, slot_v, ALU.mult)
                dve.drain()
                nc.vector.tensor_scalar(slot_v, slot_v, -float(DUMMY + 1), float(DUMMY), ALU.mult, ALU.add)
                nc.vector.tensor_scalar(slot_i, slot_f, -1.0, None, ALU.add)
                dve.drain()
                nc.vector.tensor_tensor(slot_list[:, 0:T * SS].rearrange("p (t s) -> p t s", s=SS), slot_f, slot_v, ALU.add)
                dve.drain().then_inc(S["lists_ready"], 1)
                nc.vector.tensor_scalar(raw64, slot_i, LO.bit_length() - 1, None, ALU.arith_shift_right)
                dve.drain()
                nc.vector.tensor_copy(halves[:, 0, 0:T, :], raw64)
                nc.vector.tensor_scalar(slot_i, slot_i, LO - 1, None, ALU.bitwise_and)
                dve.drain()
                nc.vector.tensor_copy(halves[:, 1, 0:T, :], slot_i)
                dve.drain().then_inc(S["halves_ready"], 1)
                dve.wait_ge(S["halvesT_ready"], PAIRS)
                with dve.Fori(0, PAIRS) as k:
                    for v in range(4):
                        wait_count(dve, S["hot2_used"], 4 * k + (v + 1))
                        for c, n in ((0, HI), (1, LO)):
                            ins = nc.vector.tensor_tensor(
                                hots[v % 2][c], iota64[:, 0:n].unsqueeze(1).to_broadcast((P, Q, n)),
                                halvesT[:, bass.ds(k, 1), c, v * Q:(v + 1) * Q].rearrange("p a d -> p (a d)").unsqueeze(2).to_broadcast((P, Q, n)),
                                ALU.is_equal)
                        ins.then_inc(S["hot2_ready"], 1)

            def sage_by_counts():
                with dve.Fori(0, LS) as layer:
                    wait_count(dve, S["xnat_ld"], 16 * layer + 16)
                    for c in range(3):
                        nc.vector.tensor_copy(x3[:, :, c, :], xnat)
                        dve.drain()
                        if c < 2:
                            nc.vector.tensor_tensor(xnat, xnat, x3[:, :, c, :], ALU.subtract)
                            dve.drain()
                    dve.drain().then_inc(S["x3_ready"], 1)
                    with dve.Fori(0, T // G) as j:
                        for i in range(G):
                            t = j * G + i
                            wait_count(dve, S["big_done"], layer * T + t + (NC + 1))
                            nc.vector.tensor_reduce(agg[:, :], p_big[i % 2][:, 0:3 * D].rearrange("p (c f) -> p f c", c=3), AX.X, ALU.add)
                            dve.drain()
                            nc.vector.tensor_scalar(cat[:, 0:D], agg[:, :], inv_cnt[:, bass.ds(t, 1)], None, ALU.mult)
                            nc.vector.tensor_copy(cat[:, D:2 * D], xp[:, bass.ds(t, 1), :])
                            dve.drain().then_inc(S["catp"], 1)
                            sage_output(t, layer)

            def place_edges():
                nc.vector.tensor_copy(s_next, off_nat[:, :])
                nc.vector.tensor_scalar(s_before, diff_i[:, :], 0.0, None, ALU.is_lt)
                nc.vector.tensor_scalar(s_col[:, 4:5], diff_i[:, 0:1], -1.0, float(2 * E + CH), ALU.mult, ALU.add)
                with dve.Fori(0, EJ) as j:
                    at = bass.ds(j, 1)
                    dve.drain()
                    nc.vector.tensor_scalar(s_a[:, 0:64], iota64[:, 0:64], dhi[:, at], None, ALU.is_equal)
                    nc.vector.tensor_scalar(s_b[:, 0:64], iota64[:, 0:64], dlo[:, at], None, ALU.is_equal)
                    nc.vector.tensor_copy(s_src, src_i[:, at])
                    nc.vector.tensor_scalar(s_col[:, 2:3], dhi[:, at], 0.0, None, ALU.is_ge)
                    nc.vector.tensor_scalar(s_col[:, 3:4], dhi[:, at], 0.0, s_col[:, 4:5], ALU.is_lt, ALU.mult)
                    dve.drain().then_inc(S["s_hot"], 1)
                    wait_count(dve, S["s_turned"], j + 1)
                    nc.vector.tensor_copy(s_at, psum[1][0:64, 0:P])
                    nc.vector.tensor_copy(s_bt, psum[1][0:64, P:2 * P])
                    dve.drain().then_inc(S["s_copied"], 1)
                    wait_count(dve, S["s_product"], j + 1)
                    nc.vector.tensor_copy(s_n, psum[4][:, 0:P])
                    nc.vector.tensor_tensor(s_b[:, 64:128], psum[2][:, 0:64], s_b[:, 0:64], ALU.mult)
                    dve.drain()
                    nc.vector.tensor_tensor(s_m, psum[3][:, 0:P], s_n, ALU.mult)
                    nc.vector.tensor_reduce(s_col[:, 0:1], s_b[:, 64:128], AX.X, ALU.add)
                    dve.drain()
                    nc.vector.tensor_tensor(s_m, s_m, s_before, ALU.mult)
                    dve.drain()
                    nc.vector.tensor_reduce(s_col[:, 1:2], s_m, AX.X, ALU.add)
                    dve.drain()
                    nc.vector.tensor_tensor(s_col[:, 0:1], s_col[:, 0:1], s_col[:, 1:2], ALU.add)
                    dve.drain()
                    nc.vector.tensor_tensor(s_col[:, 0:1], s_col[:, 0:1], s_col[:, 2:3], ALU.mult)
                    dve.drain()
                    nc.vector.tensor_tensor(s_place, s_col[:, 0:1], s_col[:, 3:4], ALU.add)
                    nc.vector.tensor_tensor(s_next, s_next, psum[5][0:64, 0:64], ALU.add)
                    dve.drain().then_inc(S["s_placed"], 1)
                    wait_count(dve, S["s_stored"], 16 * j + 16)

            dve.wait_ge(S["src_i_ld"], 32)
            with dve.If(disordered(dve) > 0):
                place_edges()
            dve.drain()

            dve.wait_ge(S["xgath"], 16 * T)
            nc.vector.tensor_copy(xp.rearrange("p t d -> p (t d)"), x0[:, :, :].rearrange("p t d -> p (t d)"))
            total = chunk_total(dve)
            dve.drain()
            with dve.If(base(dve, 1) > SC):
                mask_by_chunk()
                sage_by_gather()
            with dve.Else():
                build_counts()
                sage_by_counts()

            dve.drain()
            flat = x0[:, :, :].rearrange("p t d -> p (t d)")
            nc.vector.tensor_tensor(flat, flat, xp.rearrange("p t d -> p (t d)"), ALU.add)
            dve.drain()
            for t in range(T):
                nc.vector.bn_stats(stats[:, t, :], x0[:, t, :])
            dve.drain()
            for t in range(T):
                nc.vector.bn_aggr(mv[:, t, :], stats[:, t, :])
            dve.drain()
            nc.vector.tensor_scalar(std[:, :], mv[:, :, 1], 1e-5, None, ALU.add)
            dve.drain().then_inc(S["var_ready"], 1)
            dve.wait_ge(S["std_done"], 1)
            nc.vector.reciprocal(rstd[:, :], std[:, :])
            dve.drain()
            for t in range(T):
                nc.vector.tensor_scalar(x0[:, t, :], x0[:, t, :], mv[:, t, 0:1], rstd[:, t:t + 1], ALU.subtract, ALU.mult)
            dve.drain()
            nc.vector.memset(kvn[:, :, :], 1.0)
            nc.vector.memset(ones_row[:, :], 1.0)
            dve.drain().then_inc(S["ones_ready"], 1)
            dve.wait_ge(S["b1_done"], 1)
            nc.vector.tensor_copy(b1_all[:, :], p_t2[:, 0:LT * FC])
            dve.drain().then_inc(S["b1_used"], 1)

            with dve.Fori(0, T // G) as j:
                nc.vector.tensor_copy(y[:, :, 0:D], x0[:, bass.ds(j * G, G), :])
                dve.drain().then_inc(S["x1_ready"], 1)
                wait_count(dve, S["hi_done"], j * G + G)
                for i in range(G):
                    nc.vector.tensor_tensor(h1[:, i, :], p_f2[i // 4][:, i % 4 * P:(i % 4 + 1) * P], bi_bc[:, :], ALU.add)
                dve.drain().then_inc(S["hi_ready"], 1)
                wait_count(dve, S["hs_ready"], j + 1)
                nc.vector.tensor_copy(h_all[:, bass.ds(j * G, G), :], hs[:, :, :])
                dve.drain().then_inc(S["h_saved"], 1)

            def scores(g, ql, layer):
                u = g % NB
                wait_count(dve, TR[3], ql + 1)
                dve.drain()
                nc.vector.tensor_tensor(prod[:, :, :], kv[:, bass.ds(u, 1), :, 0:HID].rearrange("p u s d -> p (u s) d"),
                                        q_t[:, :].unsqueeze(1).to_broadcast((P, CH, HID)), ALU.mult)
                nc.vector.tensor_scalar(empty[:, :], ids[:, bass.ds(u, 1), :], float(DUMMY), NEG, ALU.is_equal, ALU.mult)
                dve.drain()
                nc.vector.tensor_reduce(score[:, :, 0:CH].rearrange("p h s -> p s h"),
                                        prod[:, :, :].rearrange("p s (h d) -> p s h d", d=DH), AX.X, ALU.add)
                dve.drain()
                nc.vector.tensor_tensor(score[:, :, 0:CH], score[:, :, 0:CH],
                                        empty[:, :].unsqueeze(1).to_broadcast((P, HEADS, CH)), ALU.add)
                dve.drain()
                nc.vector.tensor_reduce(top[:, :], score[:, :, :], AX.X, ALU.max)
                dve.drain()
                nc.vector.tensor_tensor(delta[:, bass.ds(g % 2, 1), :, :].rearrange("p a h s -> p (a h) s"), score[:, :, :],
                                        top[:, :].unsqueeze(2).to_broadcast((P, HEADS, CH + 1)), ALU.subtract).then_inc(S["d_ready"], 1)
                dve.drain()
                nc.vector.tensor_copy(score[:, :, CH], top[:, :])

            def weigh(g, ql):
                u, v = g % NB, g % 2
                wait_count(dve, S["e_done"], ql + 1)
                nc.vector.tensor_tensor(wv[:, bass.ds(v, 1), 0:CH, :].rearrange("p a s (h w) -> p (a s) h w", w=VW),
                                        kv[:, bass.ds(u, 1), :, HID:KV].rearrange("p u s (h w) -> p (u s) h w", w=VW),
                                        expo[:, bass.ds(v, 1), :, 0:CH].rearrange("p a h s -> p (a s) h").unsqueeze(3).to_broadcast((P, CH, HEADS, VW)),
                                        ALU.mult).then_inc(TR[2], 1)
                wait_count(dve, S["sum_done"], ql + 1)
                nc.vector.tensor_tensor(wv[:, bass.ds(v, 1), CH, :].rearrange("p a (h w) -> p (a h) w", w=VW),
                                        p_acc[:, 0:HEADS * VW].rearrange("p (h w) -> p h w", w=VW),
                                        expo[:, bass.ds(v, 1), :, CH:CH + 1].rearrange("p a h s -> p (a h) s").to_broadcast((P, HEADS, VW)),
                                        ALU.mult).then_inc(S["w_ready"], 1)

            def attend(j, layer):
                first = base(dve, j * G)
                with dve.Fori(j * G, j * G + G) as t:
                    dve.drain()
                    nc.vector.tensor_copy(q_t[:, :], q_all[:, bass.ds(t, 1), :])
                    nc.vector.memset(score[:, :, CH], 2 * NEG)
                    with dve.Fori(base(dve, t), base(dve, t + 1)) as g:
                        ql = layer * total + g
                        scores(g, ql, layer)
                        with dve.If(g > first):
                            weigh(g + (2 * NB - 1), ql - 1)
                last = base(dve, j * G + G)
                weigh(last + (2 * NB - 1), layer * total + last - 1)

            def gate_and_norm(j, layer, m):
                ts = bass.ds(j * G, G)
                wait_count(dve, S["acc_saved"], m * G + (G + 1))
                accw = acc[:, :, :].rearrange("p i (h w) -> p i h w", w=VW)
                nc.vector.tensor_scalar(rden[:, :, :], accw[:, :, :, DH], 1e-16, None, ALU.add)
                nc.vector.tensor_copy(tri[:, :, 1, :], r_all[:, ts, :])
                dve.drain()
                nc.vector.reciprocal(rden[:, :, :], rden[:, :, :])
                dve.drain()
                for i in range(G):
                    nc.vector.tensor_tensor(tri[:, i, 0, :].rearrange("p (h w) -> p h w", w=DH), accw[:, i, :, 0:DH],
                                            rden[:, i, :].unsqueeze(2).to_broadcast((P, HEADS, DH)), ALU.mult)
                dve.drain()
                nc.vector.tensor_tensor(tri[:, :, 2, :], tri[:, :, 0, :], tri[:, :, 1, :], ALU.subtract)
                nc.vector.tensor_tensor(y[:, :, :], tri[:, :, 0, :], h_all[:, ts, :], ALU.add)
                dve.drain()
                nc.vector.tensor_tensor(triw[:, :, :], tri[:, :, :, :].rearrange("p i c f -> p i (c f)"),
                                        wbeta_bc[:, bass.ds(layer, 1), :].to_broadcast((P, G, 3 * HID)), ALU.mult)
                dve.drain()
                nc.vector.tensor_reduce(gate[:, 0, :], triw[:, :, :], AX.X, ALU.add)
                dve.drain().then_inc(S["z_ready"], 1)
                wait_count(dve, S["z_done"], m + 1)
                nc.vector.tensor_scalar(gate[:, 2, :], gate[:, 1, :], -1.0, -1.0, ALU.mult, ALU.add)
                dve.drain()
                nc.vector.reciprocal(gate[:, 3, :], gate[:, 2, :])
                dve.drain()
                for i in range(G):
                    nc.vector.scalar_tensor_tensor(out=y[:, i, :], in0=tri[:, i, 2, :], scalar=gate[:, 3, i:i + 1], in1=y[:, i, :],
                                                   op0=ALU.mult, op1=ALU.add)
                dve.drain()
                for i in range(G):
                    nc.vector.bn_stats(stats[:, i, :], y[:, i, :])
                dve.drain()
                for i in range(G):
                    nc.vector.bn_aggr(mv[:, i, :], stats[:, i, :])
                dve.drain()
                nc.vector.tensor_scalar(std[:, 0:G], mv[:, 0:G, 1], 1e-5, None, ALU.add)
                dve.drain().then_inc(S["var_ready"], 1)
                wait_count(dve, S["std_done"], m + 2)
                nc.vector.reciprocal(rstd[:, 0:G], std[:, 0:G])
                dve.drain()
                for i in range(G):
                    nc.vector.tensor_scalar(y[:, i, :], y[:, i, :], mv[:, i, 0:1], rstd[:, i:i + 1], ALU.subtract, ALU.mult)
                dve.drain()
                nc.vector.tensor_tensor(y[:, :, :], y[:, :, :], lng_bc[:, bass.ds(layer, 1), :].to_broadcast((P, G, HID)), ALU.mult)
                dve.drain()
                nc.vector.tensor_tensor(h1[:, :, :], y[:, :, :], lnb_bc[:, bass.ds(layer, 1), :].to_broadcast((P, G, HID)), ALU.add)
                dve.drain().then_inc(S["h1_ready"], 1)

            def new_states(j, m):
                wait_count(dve, S["f2_done"], m * G + G)
                for i in range(G):
                    nc.vector.tensor_tensor(hs[:, i, :], p_f2[i // 4][:, i % 4 * P:(i % 4 + 1) * P], h1[:, i, :], ALU.add)
                dve.drain().then_inc(S["hs_ready"], 1)
                nc.vector.tensor_copy(h_all[:, bass.ds(j * G, G), :], hs[:, :, :])
                dve.drain().then_inc(S["h_saved"], 1)

            def output(j):
                wait_count(dve, S["o_done"], j * G + G)
                for i in range(G):
                    nc.vector.tensor_tensor(y[:, i, 0:D], p_f2[i // 4][:, i % 4 * P:i % 4 * P + D], bo_bc[:, :], ALU.add)
                dve.drain()
                nc.vector.tensor_tensor(y[:, :, 0:D], y[:, :, 0:D], x0[:, bass.ds(j * G, G), :], ALU.add)
                dve.drain()
                for i in range(G):
                    nc.vector.bn_stats(stats[:, i, :], y[:, i, 0:D])
                dve.drain()
                for i in range(G):
                    nc.vector.bn_aggr(mv[:, i, :], stats[:, i, :])
                dve.drain()
                nc.vector.tensor_scalar(std[:, 0:G], mv[:, 0:G, 1], 1e-5, None, ALU.add)
                dve.drain().then_inc(S["fvar_ready"], 1)
                wait_count(dve, S["fstd_done"], j + 1)
                nc.vector.reciprocal(rstd[:, 0:G], std[:, 0:G])
                dve.drain()
                for i in range(G):
                    nc.vector.tensor_scalar(y_all[:, bass.ds(j * G + i, 1), :], y[:, i, 0:D], mv[:, i, 0:1], rstd[:, i:i + 1], ALU.subtract, ALU.mult)
                dve.drain().then_inc(S["out_ready"], 1)

            with dve.Fori(0, LT) as layer:
                with dve.Fori(0, T // G) as j:
                    m = layer * (T // G) + j
                    attend(j, layer)
                    gate_and_norm(j, layer, m)
                    new_states(j, m)
                    with dve.If(layer == LT - 1):
                        output(j)

        @block.scalar
        def _(act):
            act.wait_ge(S["meta_ready"], 1)

            def run_starts():
                act.sem_inc(S["ids_stored"], NB)
                with act.Fori(0, T) as t:
                    act.drain()
                    nc.scalar.activation(run_at[:, :], off_pos[:, bass.ds(t, 1)], ACT.Copy)
                    with act.Fori(base(act, t), base(act, t + 1)) as g:
                        wait_count(act, S["ids_stored"], g + 1)
                        act.drain()
                        nc.scalar.activation(run_i[:, bass.ds(g % NB, 1), :], run_at[:, :], ACT.Copy).then_inc(S["run_ready"], 1)
                        nc.scalar.activation(run_at[:, :], run_at[:, :], ACT.Copy, bias=float(CH))

            def counts_out():
                for k in range(PAIRS):
                    act.wait_ge(S["halves_turned"], k + 1)
                    nc.scalar.copy(halvesT[:, k, :, :].rearrange("p c d -> p (c d)"), psum[k % 2][:, 0:2 * P]).then_inc(S["halvesT_ready"], 1)
                act.sem_inc(S["cq_ready"], 2)
                with act.Fori(0, PAIRS) as k:
                    for v in range(4):
                        if v < 2:
                            with act.If(k > 0):
                                wait_count(act, cq_st[v], 32 * k)
                        else:
                            wait_count(act, cq_st[v - 2], 32 * k + 16)
                        wait_count(act, S["hot2_used"], 4 * k + (v + 3))
                        for b in range(4):
                            nc.scalar.copy(cq[:, v % 2, b // 2, b % 2 * 512:(b % 2 + 1) * 512], psum[4 * (v % 2) + b][0:HI, :])
                        act.drain().then_inc(S["cq_ready"], 1)

            def turned_cats():
                with act.Fori(0, LS * T) as n:
                    wait_count(act, S["catt"], n + 1)
                    nc.scalar.copy(catT[:, :], p_t[:, 0:P]).then_inc(S["catc"], 1)

            with act.If(base(act, 1) > SC):
                run_starts()
                turned_cats()
            with act.Else():
                counts_out()
                turned_cats()
            act.wait_ge(S["var_ready"], 1)
            nc.scalar.activation(std[:, :], std[:, :], ACT.Sqrt)
            act.drain().then_inc(S["std_done"], 1)

            def turned(src, dst, name_in, name_out, m):
                for i in range(G):
                    wait_count(act, S[name_in], m * G + (i + 1))
                    nc.scalar.copy(dst[:, i * P:(i + 1) * P], src[i % 2][:, 0:P]).then_inc(S[name_out], 1)

            def projections(j, n0):
                for i in range(G):
                    wait_count(act, S["proj_done"], n0 + (i + 1))
                    ts = bass.ds(j * G + i, 1)
                    p = p_wide[i % 2]
                    nc.scalar.activation(q_all[:, ts, :], p[:, 0:HID], ACT.Copy, scale=float(DH) ** -0.5)
                    nc.scalar.activation(kvn[:, ts, 0:HID], p[:, HID:2 * HID], ACT.Copy)
                    nc.scalar.activation(kvn[:, ts, HID:KV].rearrange("p a (h w) -> p (a h) w", w=VW)[:, :, 0:DH],
                                         p[:, 2 * HID:3 * HID].rearrange("p (h w) -> p h w", w=DH), ACT.Copy)
                    nc.scalar.activation(r_all[:, ts, :], p[:, 3 * HID:4 * HID], ACT.Copy)
                    act.drain().then_inc(S["kv_ready"], 1)

            with act.Fori(0, T // G) as j:
                for i in range(G):
                    wait_count(act, S["x1_turned"], j * G + (i + 1))
                    nc.scalar.copy(h1T[0:D, i * P:(i + 1) * P], p_turn[i % 2][0:D, 0:P]).then_inc(S["xT_ready"], 1)
                wait_count(act, S["hi_ready"], j + 1)
                nc.scalar.activation(hs[:, :, :], h1[:, :, :], ACT.Gelu)
                act.drain().then_inc(S["hs_ready"], 1)
                turned(p_turn, hT, "hs_turned", "hT_ready", j)
                projections(j, j * G)
            act.wait_ge(S["b1_used"], 1)
            total = chunk_total(act)

            with act.Fori(0, LT) as layer:
                act.drain()
                nc.scalar.copy(b1[:, :], b1_all[:, bass.ds(layer * FC, FC)])
                with act.Fori(0, T // G) as j:
                    m = layer * (T // G) + j
                    for i in range(G):
                        t = j * G + i
                        with act.Fori(base(act, t), base(act, t + 1)) as g:
                            wait_count(act, S["d_ready"], layer * total + g + 1)
                            v = bass.ds(g % 2, 1)
                            nc.scalar.activation(expo[:, v, :, :].rearrange("p a h s -> p (a h s)"),
                                                 delta[:, v, :, :].rearrange("p a h s -> p (a h s)"), ACT.Exp)
                            act.drain().then_inc(S["e_done"], 1)
                        wait_count(act, S["sum_done"], layer * total + base(act, t + 1) + 1)
                        nc.scalar.copy(acc[:, i, :], p_acc[:, 0:HEADS * VW]).then_inc(S["acc_saved"], 1)
                    wait_count(act, S["z_ready"], m + 1)
                    nc.scalar.activation(gate[:, 1, :], gate[:, 0, :], ACT.Exp, scale=-1.0)
                    act.drain().then_inc(S["z_done"], 1)
                    wait_count(act, S["var_ready"], m + 2)
                    nc.scalar.activation(std[:, 0:G], std[:, 0:G], ACT.Sqrt)
                    act.drain().then_inc(S["std_done"], 1)
                    turned(p_turn, h1T, "h1_turned", "h1T_ready", m)
                    for i in range(G):
                        wait_count(act, S["f1_done"], m * G + (i + 2))
                        if i >= 2:
                            wait_count(act, S["f2_done"], m * G + (i - 1))
                        for c in range(FC):
                            nc.scalar.activation(gT[:, i % 2, c, :], p_wide[i % 2][:, c * P:(c + 1) * P], ACT.Gelu, bias=b1[:, c:c + 1])
                        act.drain().then_inc(S["g_done"], 1)
                    turned(p_turn, hT, "hs_turned", "hT_ready", m + T // G)
                    with act.If(layer < LT - 1):
                        projections(j, m * G + T)
                    with act.Else():
                        wait_count(act, S["fvar_ready"], j + 1)
                        nc.scalar.activation(std[:, 0:G], std[:, 0:G], ACT.Sqrt)
                        act.drain().then_inc(S["fstd_done"], 1)

        @block.tensor
        def _(pe):
            pe.wait_ge(S["const_dve"], 2)
            zb = zeros[:, 0:32].bitcast(BF16)
            pe.sem_inc(S["hot_used"], 2)
            nc.tensor.matmul(p_hist[0:64, 0:64], zb, zb, start=True, stop=False)
            with pe.Fori(0, EJ // (2 * JB)) as i:
                for u in range(2):
                    wait_count(pe, S["hot_ready"], 2 * i + (u + 1))
                    for j in range(JB):
                        mm = nc.tensor.matmul(p_hist[0:64, 0:64], hot_hi[u][:, j, :], hot_lo[u][:, j, :], start=False, stop=False)
                    mm.then_inc(S["hot_used"], 1)
            nc.tensor.matmul(p_hist[0:64, 0:64], zb, zb, start=False, stop=True).then_inc(S["hist_done"], 1)
            pe.wait_ge(S["pre_ready"], 1)
            nc.tensor.matmul(p_y[0:64, 0:1], upper[0:64, 0:64], rowsum[:, 0:1], start=True, stop=True).then_inc(S["pre_done"], 1)
            pe.wait_ge(S["nat_ld"], 48)
            for i in range(3):
                nc.tensor.transpose(p_t[:, i * T:(i + 1) * T], nat_row[:, i, :], ident[0:T, 0:T]).then_inc(S["nat_turned"], 1)
            pe.wait_ge(S["deg_ready"], 1)
            nc.tensor.transpose(p_t[0:T, 0:P], deg_pos[:, :], ident[:, :]).then_inc(S["degT_done"], 1)
            pe.wait_ge(S["cnt_ready"], 1)
            pe.wait_ge(S["disorder_ready"], 1)
            nc.tensor.matmul(p_y[0:1, 64:65], disorder[:, 0:1], disorder[:, 1:2], start=True, stop=True)
            nc.tensor.matmul(p_y[0:1, 0:T + 1], chunks_f[0:T, 1:2], upper[0:T, 0:T + 1], start=True, stop=True).then_inc(S["base_done"], 1)
            pe.wait_ge(S["w_ld"], W_LOADS)
            def product(layer, n):
                wait_count(pe, S["catp"], n + 1)
                nc.tensor.transpose(p_t[:, 0:P], cat[:, :], ident[:, :]).then_inc(S["catt"], 1)
                wait_count(pe, S["catc"], n + 1)
                nc.tensor.matmul(p_y[:, 0:D], catT[:, :], wlr[:, bass.ds(layer, 1), :], start=True, stop=True).then_inc(S["mm_done"], 1)

            def count_edges():
                pe.wait_ge(S["halves_ready"], 1)
                for k in range(PAIRS):
                    if k >= 2:
                        pe.wait_ge(S["halvesT_ready"], k - 1)
                    for c in range(2):
                        tr = nc.tensor.transpose(psum[k % 2][:, c * P:(c + 1) * P], halves[:, c, 2 * k:2 * k + 2, :].rearrange("p t s -> p (t s)"), ident[:, :])
                    tr.then_inc(S["halves_turned"], 1)
                pe.sem_inc(S["hot2_used"], 2)
                with pe.Fori(0, PAIRS) as k:
                    for v in range(4):
                        wait_count(pe, S["hot2_ready"], 4 * k + (v + 1))
                        wait_count(pe, S["cq_ready"], 4 * k + (v + 1))
                        for d in range(Q):
                            for c in range(2):
                                rows = slice(SS * c, SS * c + SS)
                                mm = nc.tensor.matmul(psum[4 * (v % 2) + 2 * c + d // 16][0:HI, d % 16 * LO:(d % 16 + 1) * LO],
                                                      hots[v % 2][0][rows, d, :], hots[v % 2][1][rows, d, :], start=True, stop=True)
                        mm.then_inc(S["hot2_used"], 1)

            def aggregate():
                pe.sem_inc(S["big_done"], NC)
                with pe.Fori(0, LS) as layer:
                    wait_count(pe, S["x3_ready"], layer + 1)
                    with pe.Fori(0, T // G) as j:
                        for i in range(G):
                            n = layer * T + j * G + i
                            wait_count(pe, cnt_ld[i], (layer * (T // G) + j) * 16 + 16)
                            for b in range(LO):
                                mm = nc.tensor.matmul(p_big[i % 2][:, 0:3 * D], cnt[i][:, :, b], x3[:, b, :, :].rearrange("a c f -> a (c f)"),
                                                      start=(b == 0), stop=(b == LO - 1))
                            mm.then_inc(S["big_done"], 1)
                            if i:
                                product(layer, n - 1)
                        product(layer, layer * T + j * G + (G - 1))

            pe.wait_ge(S["meta_ready"], 1)
            with pe.If(disordered(pe) > 0):
                with pe.Fori(0, EJ) as j:
                    wait_count(pe, S["s_hot"], j + 1)
                    nc.tensor.transpose(psum[1][0:64, 0:P], s_a[:, 0:64], ident[:, :])
                    nc.tensor.transpose(psum[1][0:64, P:2 * P], s_b[:, 0:64], ident[:, :]).then_inc(S["s_turned"], 1)
                    wait_count(pe, S["s_copied"], j + 1)
                    nc.tensor.matmul(psum[2][:, 0:64], s_at, s_next, start=True, stop=True)
                    nc.tensor.matmul(psum[3][:, 0:P], s_at, s_at, start=True, stop=True)
                    nc.tensor.matmul(psum[4][:, 0:P], s_bt, s_bt, start=True, stop=True)
                    nc.tensor.matmul(psum[5][0:64, 0:64], s_a[:, 0:64], s_b[:, 0:64], start=True, stop=True).then_inc(S["s_product"], 1)
            with pe.If(base(pe, 1) > SC):
                with pe.Fori(0, LS) as layer:
                    with pe.Fori(0, T) as t:
                        product(layer, layer * T + t)
            with pe.Else():
                count_edges()
                aggregate()
            nc.tensor.transpose(p_t2[:, 0:LT * FC], b1_row[:, :], ident[0:LT * FC, 0:LT * FC]).then_inc(S["b1_done"], 1)

            pe.wait_ge(S["ones_ready"], 1)
            pe.sem_inc(S["acc_saved"], 1)
            nc.tensor.matmul(p_acc[:, 0:HEADS * VW], ident[:, :], zeros[:, 0:HEADS * VW], start=True, stop=True).then_inc(S["sum_done"], 1)

            def turn(states, name_in, name_out, copied, m, rows=P):
                wait_count(pe, S[name_in], m + 1)
                for i in range(G):
                    if i >= 2:
                        wait_count(pe, S[copied], m * G + (i - 1))
                    nc.tensor.transpose(p_turn[i % 2][0:rows, 0:P], states[:, i, 0:rows], ident[:, :]).then_inc(S[name_out], 1)

            def project(layer, m):
                turn(hs, "hs_ready", "hs_turned", "hT_ready", m)
                for i in range(G):
                    wait_count(pe, S["hT_ready"], m * G + (i + 1))
                    if i >= 2:
                        wait_count(pe, S["kv_ready"], m * G + (i - 1))
                    nc.tensor.matmul(p_wide[i % 2][:, :], ones_row[:, :], bqkvs_row[:, bass.ds(layer, 1), :], start=True, stop=False)
                    nc.tensor.matmul(p_wide[i % 2][:, :], hT[:, i * P:(i + 1) * P], wqkvs[:, bass.ds(layer, 1), :],
                                     start=False, stop=True).then_inc(S["proj_done"], 1)

            def column(i, width):
                return p_f2[i // 4][:, i % 4 * P:i % 4 * P + width]

            with pe.Fori(0, T // G) as j:
                turn(y, "x1_ready", "x1_turned", "xT_ready", j, rows=D)
                for i in range(G):
                    wait_count(pe, S["xT_ready"], j * G + (i + 1))
                    nc.tensor.matmul(column(i, HID), h1T[0:D, i * P:(i + 1) * P], wi[:, :], start=True, stop=True).then_inc(S["hi_done"], 1)
                project(0, j)

            def outer(i, layer, m):
                wait_count(pe, S["g_done"], m * G + (i + 1))
                nc.tensor.matmul(column(i, HID), ones_row[:, :], b2_row[:, bass.ds(layer, 1), :], start=True, stop=False)
                for c in range(FC):
                    mm = nc.tensor.matmul(column(i, HID), gT[:, i % 2, c, :], w2[:, bass.ds(layer, 1), c, :], start=False, stop=(c == FC - 1))
                mm.then_inc(S["f2_done"], 1)

            total = chunk_total(pe)
            with pe.Fori(0, LT) as layer:
                wait_count(pe, S["w1_ld"], 16 * layer + 16)
                with pe.Fori(0, T // G) as j:
                    m = layer * (T // G) + j
                    with pe.Fori(j * G, j * G + G) as t:
                        wait_count(pe, S["acc_saved"], layer * T + t + 1)
                        with pe.Fori(base(pe, t), base(pe, t + 1)) as g:
                            wait_count(pe, S["w_ready"], layer * total + g + 1)
                            for s in range(CH + 1):
                                mm = nc.tensor.matmul(p_acc[:, 0:HEADS * VW], ident[:, :], wv[:, bass.ds(g % 2, 1), s, :],
                                                      start=(s == 0), stop=(s == CH))
                            mm.then_inc(S["sum_done"], 1)
                    turn(h1, "h1_ready", "h1_turned", "h1T_ready", m)
                    for i in range(G):
                        if i >= 2:
                            wait_count(pe, S["g_done"], m * G + (i - 1))
                        wait_count(pe, S["h1T_ready"], m * G + (i + 1))
                        for c in range(FC):
                            mm = nc.tensor.matmul(p_wide[i % 2][:, c * P:(c + 1) * P], w1[:, c * P:(c + 1) * P], h1T[:, i * P:(i + 1) * P],
                                                  start=True, stop=True)
                        mm.then_inc(S["f1_done"], 1)
                        if i:
                            outer(i - 1, layer, m)
                    outer(G - 1, layer, m)
                    with pe.If(layer < LT - 1):
                        project((layer + 1).with_bounds(min_val=1, max_val=LT - 1), m + T // G)
                    with pe.Else():
                        turn(hs, "hs_ready", "hs_turned", "hT_ready", m + T // G)
                        for i in range(G):
                            wait_count(pe, S["hT_ready"], (m + T // G) * G + (i + 1))
                            nc.tensor.matmul(column(i, D), hT[:, i * P:(i + 1) * P], wo[:, :], start=True, stop=True).then_inc(S["o_done"], 1)


def kernel(**inputs):
    import numpy as np
    import concourse.bacc as bacc
    from concourse import mybir as mb
    from concourse.bass_utils import run_bass_kernel_spmd as run

    a = {k: np.asarray(v) for k, v in inputs.items()}
    turned = lambda w: np.swapaxes(w, -1, -2)
    given = {
        "x": a["x"], "src": a["src"], "dst": a["dst"],
        "wlr": np.concatenate([a["L0_gnn_Wl"], a["L0_gnn_Wr"]], axis=1),
        "bl": a["L0_gnn_b"],
        "wi": a["L1_gnn_Wi"].T, "bi": a["L1_gnn_bi"][None],
        "wqkvs": np.concatenate([turned(a["L1_gnn_W" + c]) for c in "qkvs"], axis=2),
        "bqkvs": np.concatenate([a["L1_gnn_b" + c] for c in "qkvs"], axis=1),
        "wbeta": a["L1_gnn_Wbeta"][:, 0],
        "lng": a["L1_gnn_ln_g"], "lnb": a["L1_gnn_ln_b"],
        "w1t": turned(a["L1_gnn_W1"]), "b1": a["L1_gnn_b1"],
        "w2t": turned(a["L1_gnn_W2"]), "b2": a["L1_gnn_b2"],
        "wo": a["L1_gnn_Wo"].T, "bo": a["L1_gnn_bo"][None],
    }
    nc = bacc.Bacc("TRN2", target_bir_lowering=False, num_devices=1)
    arrays, t_in = {}, {}
    for name, v in given.items():
        v = np.ascontiguousarray(v)
        arrays["in_" + name] = v
        t_in[name] = nc.dram_tensor("in_" + name, v.shape, mb.dt.from_np(v.dtype), kind="ExternalInput").ap()
    out = nc.dram_tensor("out_0", a["x"].shape, mb.dt.float32, kind="ExternalOutput").ap()
    dbg = nc.dram_tensor("dbg", (256, 128, 8), mb.dt.int32, kind="ExternalOutput").ap() if DEBUG else None
    build(nc, t_in, out, dbg)
    r = run(nc, [arrays], core_ids=[0])
    return r.results[0]["out_0"]
```

```python
from contextlib import ExitStack

import concourse.bass as bass
from concourse import mybir

ALU = mybir.AluOpType
ACT = mybir.ActivationFunctionType
AX = mybir.AxisListType
F32 = mybir.dt.float32
BF16 = mybir.dt.bfloat16
I32 = mybir.dt.int32

P = 128


def build(nc, t_in, out):
    N, D = t_in["x"].shape
    E = t_in["src"].shape[0]
    HID = t_in["wqkvs"].shape[1]
    LS, LT = t_in["wlr"].shape[0], t_in["wqkvs"].shape[0]
    FF = t_in["w1t"].shape[2]
    HEADS = 8
    DH = HID // HEADS
    VW = DH + 1
    KV = HID + HEADS * VW
    FC = FF // P
    T = -(-N // P)
    NP = T * P
    LAST = N - (T - 1) * P
    DUMMY = NP
    CH = 8
    CH_LOG = 3
    NB = 4
    GMAX = 2 * T + E // CH + NB
    EJ = -(-E // P)
    EL = E - (P - 1) * EJ
    JB = next(j for j in range(32, 0, -1) if EJ % (2 * j) == 0)
    HN = -(-N // 64)
    DEG_CLAMP = 4095.0
    NEG = -1.0e30
    ZW = 512
    Z_STORES = 16 * (3 + -(-((E + CH) // ZW) // P))
    G = next(g for g in (5, 4, 3, 2, 1) if T % g == 0)
    LAG = G + 2
    RESULTS = ((0, T - G), (T - G, T))
    SS = 64
    SC = SS // CH
    LO = 32
    HI = NP // LO
    PAIRS = -(-T // 2)
    Q = 32
    DB = Q // 4
    W_LOADS = 16 * (2 + LT + 2 + 1 + 6 + 2)

    ctx = ExitStack()
    with ctx:
        def sb(name, shape, dt=F32):
            return ctx.enter_context(nc.sbuf_tensor(name, shape, dt))

        def ps(name):
            return ctx.enter_context(nc.psum_tensor(name, [P, 512], F32))

        def sem(name):
            return ctx.enter_context(nc.semaphore(name))

        def dram(name, shape, dt=F32):
            return nc.dram_tensor(name, shape, dt, kind="Internal").ap()

        src_run = dram("src_run", (2 * E + CH + P,), I32)
        natural = dram("natural", (3, 64 * 64))
        posrec = dram("posrec", (NP, 4), I32)
        slot_ids = dram("slot_ids", (GMAX + NB, P, CH), I32)
        xtab = dram("xtab", (NP + 1, D))
        kvtab = dram("kvtab", (NP + 1, KV))
        counts = dram("counts", (2 * PAIRS, HI, P * LO), BF16)

        diff_i = sb("diff_i", [P, P], I32)
        ident = sb("ident", [P, P])
        upper = sb("upper", [P, P])
        iota64_i = sb("iota64_i", [P, P], I32)
        iota64 = sb("iota64", [P, P], BF16)
        iota8 = sb("iota8", [P, CH])
        node_i = sb("node_i", [P, T], I32)
        nodekey_i = sb("nodekey_i", [64, 64], I32)
        nodekey = sb("nodekey", [64, 64])
        zeros = sb("zeros", [P, ZW])
        posn = sb("posn", [P, T, 4], I32)
        deg_pos = sb("deg_pos", [P, T])
        off_pos = sb("off_pos", [P, T])
        inv_cnt = sb("inv_cnt", [P, T])
        chunks_f = sb("chunks_f", [32, 4])
        chunks_i = sb("chunks_i", [32, 4], I32)
        meta = sb("meta", [1, 32], I32)
        meta_f = sb("meta_f", [1, 4])
        meta_i = sb("meta_i", [1, 4], I32)

        pool_a = sb("pool_a", [P, NB * CH * KV])
        pool_b = sb("pool_b", [P, T * KV])
        dst_i = pool_b[:, 0:EJ].bitcast(I32)
        dhi_i = pool_b[:, EJ:2 * EJ].bitcast(I32)
        dhi = pool_b[:, 2 * EJ:3 * EJ]
        dlo = pool_b[:, 3 * EJ:4 * EJ]
        dnext = pool_b[:, 4 * EJ:5 * EJ].bitcast(I32)
        src_i = pool_b[:, 5 * EJ:6 * EJ].bitcast(I32)
        s_a, s_b, s_m, s_n = (pool_a[:, P * i:P * i + P] for i in range(4))
        s_at, s_bt = (pool_a[0:64, P * i:P * i + P] for i in (4, 5))
        s_next = pool_a[0:64, 6 * P:6 * P + 64]
        s_before = pool_a[:, 7 * P:8 * P]
        s_col = pool_a[:, 8 * P:8 * P + 8]
        s_place = pool_a[:, 8 * P + 8:8 * P + 9].bitcast(I32)
        s_src = pool_a[:, 8 * P + 9:8 * P + 10].bitcast(I32)
        disorder = sb("disorder", [P, 2])
        hot_hi = [pool_a[:, JB * 32 * u:JB * 32 * (u + 1)].bitcast(BF16).rearrange("p (c j) -> p c j", c=64) for u in range(2)]
        hot_lo = [pool_a[:, JB * 32 * (2 + u):JB * 32 * (3 + u)].bitcast(BF16).rearrange("p (c j) -> p c j", c=64) for u in range(2)]
        keys_bc = pool_a[:, 0:NP]
        greater = pool_a[:, NP:2 * NP]
        halves_bf = pool_b[:, EJ:2 * EJ].bitcast(BF16).rearrange("p (c j) -> p c j", c=2)
        grid = pool_b[:, 6 * EJ:6 * EJ + 32 * JB].bitcast(BF16).rearrange("p (c j) -> p c j", c=64)
        assert 6 * EJ + 32 * JB <= T * KV
        deg_nat = sb("deg_nat", [64, 64])
        off_nat = sb("off_nat", [64, 64])
        key_nat = sb("key_nat", [64, 64])
        rowsum = sb("rowsum", [64, 2])
        nat_row = pool_a[0:T, 2 * NP:2 * NP + 3 * P].rearrange("t (c p) -> t c p", c=3)
        nat_col = sb("nat_col", [P, 3, T])
        rank_f = sb("rank_f", [P, T])
        rank_i = sb("rank_i", [P, T], I32)
        rec = sb("rec", [P, T, 4], I32)

        run_at = sb("run_at", [P, 1])
        run_i = sb("run_i", [P, NB, 1], I32)
        raw = sb("raw", [P, NB, CH], I32)
        left = sb("left", [P, 1])
        valid = sb("valid", [P, CH])
        rawf = sb("rawf", [P, CH])
        ids_out = sb("ids_out", [P, NB, CH], I32)

        ids = sb("ids", [P, NB, CH], I32)
        xs = pool_a[:, 0:NB * CH * D].rearrange("p (u s d) -> p u s d", u=NB, s=CH)
        kv = pool_a[:, :].rearrange("p (u s d) -> p u s d", u=NB, s=CH)
        xp = pool_b[:, 0:T * D].rearrange("p (t d) -> p t d", d=D)
        kvn = pool_b[:, :].rearrange("p (t d) -> p t d", d=KV)

        x0 = sb("x0", [P, T, D])
        prod = sb("prod", [P, CH, HEADS, VW])
        sage_work = prod[:, :, :, :].rearrange("p s h w -> p (s h w)")
        cat, catT = sage_work[:, 0:P], sage_work[:, P:2 * P]
        agg, part = (sage_work[:, 2 * P + i * D:2 * P + (i + 1) * D] for i in range(2))
        wlr, bl_bc = (sage_work[:, 2 * P + (2 + i * LS) * D:2 * P + (2 + (i + 1) * LS) * D].rearrange("p (l d) -> p l d", d=D)
                      for i in range(2))
        floors = sb("floors", [P, LS])

        wi = sb("wi", [D, HID])
        wqkvs = sb("wqkvs", [P, LT + 1, 4 * HID])
        w1 = sb("w1", [P, FF])
        w2 = sb("w2", [P, LT, FC, HID])
        bi_bc = sb("bi_bc", [P, HID])
        ones_row = sb("ones_row", [1, P])
        bqkvs_row = sb("bqkvs_row", [1, LT + 1, 4 * HID])
        b2_row = sb("b2_row", [1, LT, HID])
        wbeta_bc = sb("wbeta_bc", [P, LT, 3 * HID])
        lng_bc = sb("lng_bc", [P, LT, HID])
        lnb_bc = sb("lnb_bc", [P, LT, HID])
        b1_row = sb("b1_row", [LT * FC, P])
        b1_all = sb("b1_all", [P, LT * FC])
        b1 = sb("b1", [P, FC])
        arena = sb("arena", [P, 3, T, HID])
        h_all = arena[:, 0, :, :]
        q_all = arena[:, 1, :, :]
        r_all = arena[:, 2, :, :]
        y_all = arena[:, 0, :, 0:D]
        q_t = sb("q_t", [P, HID])
        score = sb("score", [P, 2, HEADS, CH + 1])
        delta = sb("delta", [P, 2, HEADS, CH + 1])
        expo = sb("expo", [P, 2, HEADS, CH + 1])
        wv = sb("wv", [P, 2, CH + 1, HEADS * VW])
        acc = sb("acc", [P, G, HEADS * VW])
        rden = sb("rden", [P, G, HEADS])
        tri = sb("tri", [P, G, 3, HID])
        gate = sb("gate", [P, 4, G])
        y = sb("y", [P, G, HID])
        stats = sb("stats", [P, T, 6])
        mv = sb("mv", [P, T, 2])
        std = sb("std", [P, T])
        rstd = sb("rstd", [P, T])
        h1 = sb("h1", [P, G, HID])
        hs = sb("hs", [P, G, HID])
        turned_work = sb("turned_work", [P, 2 * G * P + 2 * FC * P])
        h1T = turned_work[:, 0:G * P]
        hT = turned_work[:, G * P:2 * G * P]
        gT = turned_work[:, 2 * G * P:].rearrange("p (u c k) -> p u c k", u=2, c=FC)
        triw = sb("triw", [P, G, 3 * HID])

        NC = G
        free_a = arena[:, :, :, :].rearrange("p a t d -> p (a t d)")
        def half(base, at, n):
            return base[:, at:at + n // 2].bitcast(BF16)
        cw = P * LO // 2
        in_a = 3 * T * HID // cw
        where = [(free_a, i * cw) for i in range(in_a)] + [(pool_a, 5 * LO * D // 2 + i * cw) for i in range(NC - in_a)]
        cnt = [half(space, at, P * LO)[0:HI, :].rearrange("a (d b) -> a d b", b=LO) for space, at in where[:NC]]
        xnat = pool_a[0:HI, 0:LO * D].rearrange("a (b f) -> a b f", b=LO)
        x3 = half(pool_a, LO * D, LO * 3 * D)[0:HI, :].rearrange("a (b c f) -> a b c f", b=LO, c=3)
        slot_f = pool_a[:, 0:T * SS].rearrange("p (t s) -> p t s", s=SS)
        slot_v = pool_a[:, T * SS:2 * T * SS].rearrange("p (t s) -> p t s", s=SS)
        raw64 = pool_a[:, 2 * T * SS:3 * T * SS].bitcast(I32).rearrange("p (t s) -> p t s", s=SS)
        slot_i = pool_a[:, 3 * T * SS:4 * T * SS].bitcast(I32).rearrange("p (t s) -> p t s", s=SS)
        a_at = 0
        halves = free_a[:, a_at:a_at + 2 * 2 * PAIRS * SS].rearrange("p (c t s) -> p c t s", c=2, s=SS)
        a_at += 2 * 2 * PAIRS * SS
        halvesT = half(free_a, a_at, PAIRS * 2 * P).rearrange("p (k c d) -> p k c d", k=PAIRS, c=2)
        a_at += PAIRS * P
        hot_w = Q * (HI + 2 * LO) // 2
        hots = [(half(space, at, Q * HI).rearrange("p (a d) -> p a d", d=Q),
                 half(space, at + Q * HI // 2, Q * 2 * LO).rearrange("p (b d) -> p b d", d=Q))
                for space, at in ((free_a, a_at), (pool_a, 0))]
        grid2 = half(pool_a, 4 * T * SS, HI * Q).rearrange("p (a d) -> p a d", d=Q)
        assert a_at + hot_w <= 3 * T * HID and hot_w <= 2 * T * SS and 2 * LO <= HI
        assert 4 * T * SS + HI * Q // 2 <= NB * CH * KV and 2 * SS == P
        SL = (T * SS + (NB - 1) * CH)
        slot_list = pool_b[:, T * D:T * D + SL].bitcast(I32)
        cq = half(pool_b, T * D + SL, 4 * Q * LO)[0:HI, :].rearrange("a (v c f) -> a v c f", v=2, c=2)

        psum = [ps(f"psum{i}") for i in range(8)]
        p_hist, p_t, p_y = psum[0:3]
        p_big = [psum[4 + (2 if i == G - 1 else i % 2)] for i in range(G)]
        p_turn = psum[0:2]
        p_wide = psum[2:4]
        p_f2 = psum[4:6]
        p_acc = psum[6]
        p_t2 = psum[7]

        names = """const_pool const_dve dst_free dst_ld src_ld zero_st hot_ready hot_used hist_done pre_ready pre_done
            nat_ready nat_st nat_ld nat_ldb nat_turned rec_ready rec_st pos_ld deg_ready degT_done cnt_ready base_done
            meta_ready run_ready raw_in ids_ready ids_stored xgath x_ready x_st w_ld catp catt catc mm_done out_ready
            out_st past_wait ones_ready b1_done b1_used w1_ld kv_ready kv_st d_ready e_done z_ready z_done var_ready
            std_done h1_ready h1_turned h1T_ready f1_done g_done f2_done hs_ready hs_turned hT_ready proj_done
            x1_ready x1_turned xT_ready hi_done hi_ready fvar_ready fstd_done w_ready sum_done acc_saved raw64_ld
            lists_ready lists_st halves_ready halves_turned halvesT_ready hot2_ready hot2_used next_ld src_i_ld
            disorder_ready s_hot s_turned s_copied s_product s_placed s_stored cq_ready xnat_ld x3_ready big_done""".split()
        S = {n: sem(n) for n in names}
        raw_ld = [sem(f"raw_ld{u}") for u in range(NB)]
        ids_st = [sem(f"ids_st{u}") for u in range(NB)]
        SG, TR = [([sem(f"{w}_ids_ld{u}") for u in range(NB)], [sem(f"{w}_rows_ld{u}") for u in range(NB)],
                   sem(f"{w}_chunk_done"), sem(f"{w}_gathered")) for w in ("sage", "tran")]
        cq_st = [sem(f"cq_st{v}") for v in range(2)]
        cnt_ld = [sem(f"cnt_ld{i}") for i in range(NC)]

        def base(eng, t):
            return eng.value_load(meta[0:1, bass.ds(t, 1)], min_val=0, max_val=GMAX)

        def disordered(eng):
            return eng.value_load(meta[0:1, 30:31], min_val=0, max_val=E)

        def chunk_total(eng):
            return eng.value_load(meta[0:1, T:T + 1], min_val=NB, max_val=GMAX)

        def wait_count(eng, semaphore, count):
            eng.wait_ge(semaphore, count)
            eng.sem_inc(S["past_wait"], 1)

        def whole_chunks(eng):
            return eng.value_load(meta[0:1, 31:32], min_val=NB, max_val=GMAX)

        def has_upper(eng, g, u, whole):
            middle = eng.value_load(ids[0:1, u, CH // 2:CH // 2 + 1], min_val=0, max_val=DUMMY)
            return (DUMMY - middle) * GMAX + whole > g

        def column(i):
            return p_f2[i % 2][:, i // 2 * P:(i // 2 + 1) * P]

        block = ctx.enter_context(nc.Block())

        @block.sync
        def _(sp):
            sp.dma_start(src_run[0:E].rearrange("(a b) -> a b", a=625),
                         t_in["src"].rearrange("(a b) -> a b", a=625)).then_inc(S["src_ld"], 16)
            sp.dma_start(xtab[0:N, :], t_in["x"]).then_inc(S["src_ld"], 16)
            sp.wait_ge(S["dst_free"], 1)
            sp.dma_start(dst_i[0:P - 1, :], t_in["dst"][0:(P - 1) * EJ].rearrange("(p j) -> p j", j=EJ)).then_inc(S["dst_ld"], 16)
            sp.dma_start(dst_i[P - 1:P, 0:EL], t_in["dst"][(P - 1) * EJ:E].rearrange("(p j) -> p j", p=1)).then_inc(S["dst_ld"], 16)
            sp.dma_start(dnext[0:P - 1, :], t_in["dst"][1:(P - 1) * EJ + 1].rearrange("(p j) -> p j", j=EJ)).then_inc(S["next_ld"], 16)
            sp.dma_start(dnext[P - 1:P, 0:EL - 1], t_in["dst"][(P - 1) * EJ + 1:E].rearrange("(p j) -> p j", p=1)).then_inc(S["next_ld"], 16)
            sp.dma_start(src_i[0:P - 1, :], t_in["src"][0:(P - 1) * EJ].rearrange("(p j) -> p j", j=EJ)).then_inc(S["src_i_ld"], 16)
            sp.dma_start(src_i[P - 1:P, 0:EL], t_in["src"][(P - 1) * EJ:E].rearrange("(p j) -> p j", p=1)).then_inc(S["src_i_ld"], 16)
            sp.wait_ge(S["const_dve"], 1)
            zi = zeros[:, :].bitcast(I32)
            n_tail = E + CH
            rows = n_tail // ZW
            for r in range(0, rows, P):
                m = min(P, rows - r)
                sp.dma_start(src_run[E + r * ZW:E + (r + m) * ZW].rearrange("(p j) -> p j", j=ZW), zi[0:m, :]).then_inc(S["zero_st"], 16)
            sp.dma_start(src_run[E + rows * ZW:2 * E + CH].rearrange("(p j) -> p j", p=1), zi[0:1, 0:n_tail - rows * ZW]).then_inc(S["zero_st"], 16)
            sp.dma_start(xtab[N:NP + 1, :], zeros[0:NP + 1 - N, 0:D]).then_inc(S["zero_st"], 16)
            sp.dma_start(kvtab[DUMMY:DUMMY + 1, :], zeros[0:1, 0:KV]).then_inc(S["zero_st"], 16)
            sp.dma_start(wlr[:, :, :], t_in["wlr"].rearrange("l k n -> k l n")).then_inc(S["w_ld"], 16)
            sp.dma_start(wqkvs[:, 0:LT, :], t_in["wqkvs"].rearrange("l k n -> k l n")).then_inc(S["w_ld"], 16)
            sp.dma_start(wqkvs[:, LT, 0:D], t_in["wo"]).then_inc(S["w_ld"], 16)
            for layer in range(LT):
                sp.dma_start(w2[:, layer, :, :], t_in["w2t"][layer].rearrange("(c k) n -> k c n", k=P)).then_inc(S["w_ld"], 16)
            sp.dma_start(wi[:, :], t_in["wi"]).then_inc(S["w_ld"], 16)
            sp.dma_start(b1_row[:, :], t_in["b1"].rearrange("l (c k) -> (l c) k", k=P)).then_inc(S["w_ld"], 16)
            for tile, name in ((bl_bc, "bl"), (wbeta_bc, "wbeta"), (lng_bc, "lng"), (lnb_bc, "lnb")):
                flat = t_in[name].rearrange("(a l) n -> a (l n)", a=1)
                sp.dma_start(tile[:, :, :].rearrange("p l n -> p (l n)"), flat.partition_broadcast(P)).then_inc(S["w_ld"], 16)
            for tile, name in ((bqkvs_row[:, 0:LT, :], "bqkvs"), (b2_row[:, :, :], "b2")):
                sp.dma_start(tile, t_in[name].rearrange("(a l) n -> a l n", a=1)).then_inc(S["w_ld"], 16)
            sp.dma_start(bqkvs_row[:, LT, 0:D], t_in["bo"]).then_inc(S["w_ld"], 16)
            sp.dma_start(bi_bc[:, :], t_in["bi"].partition_broadcast(P)).then_inc(S["w_ld"], 16)
            sp.wait_ge(S["nat_ready"], 1)
            for i, t in enumerate((key_nat, off_nat, deg_nat)):
                sp.dma_start(natural[i, :].rearrange("(a b) -> a b", b=64), t[:, :]).then_inc(S["nat_st"], 16)
            sp.wait_ge(S["nat_st"], 48)
            sp.dma_start(keys_bc, natural[0:1, 0:NP].partition_broadcast(P)).then_inc(S["nat_ldb"], 16)
            for i in range(3):
                sp.dma_start(nat_row[:, i, :], natural[i, 0:NP].rearrange("(t p) -> t p", p=P)).then_inc(S["nat_ld"], 16)
            sp.wait_ge(S["rec_st"], 16 * T)
            sp.dma_start(posn[:, :, :], posrec.rearrange("(t p) c -> p t c", p=P)).then_inc(S["pos_ld"], 16)

            sp.wait_ge(S["meta_ready"], 1)
            total = chunk_total(sp)
            def feed(sems, layers, before=None, halves=False):
                ids_ld, rows_ld, chunk_done, gathered = sems
                sp.sem_inc(chunk_done, NB)
                whole = whole_chunks(sp)
                landed = [sp.alloc_register(f"landed{u}") for u in range(NB)] if halves else None
                for reg in landed or ():
                    sp.reg_mov(reg, 0)

                def pass_on(g, u, k):
                    if halves:
                        wait_count(sp, ids_ld[u], 16 * k)
                        sp.reg_add(landed[u], landed[u], 16 * (CH // 2))
                        with sp.If(has_upper(sp, g, u, whole)):
                            sp.reg_add(landed[u], landed[u], 16 * (CH // 2))
                        wait_count(sp, rows_ld[u], landed[u])
                    else:
                        wait_count(sp, rows_ld[u], 16 * CH * k)
                    sp.sem_inc(gathered, 1)

                with sp.Fori(0, layers) as layer:
                    if before:
                        before(layer)
                    with sp.Fori(0, total, NB) as g:
                        q = layer * total + g
                        k = q // NB
                        for u in range(NB):
                            if u >= 2:
                                pass_on(g + (u - 2), u - 2, k + 1)
                            else:
                                with sp.If(g > 0):
                                    pass_on(g + (u - 2), u + NB - 2, k)
                            wait_count(sp, chunk_done, q + (u + 1))
                            sp.dma_start(ids[:, u, :], slot_ids[bass.ds(g + u, 1), :, :].rearrange("a p s -> (a p) s")).then_inc(ids_ld[u], 16)
                    for u in range(NB - 2, NB):
                        pass_on(total + (u - NB), u, (layer + 1) * total // NB)

            def lists_by_chunk():
                with sp.Fori(0, total, NB) as g:
                    k = g // NB
                    for u in range(NB):
                        wait_count(sp, raw_ld[u], 16 * k + 16)
                        sp.sem_inc(S["raw_in"], 1)
                        wait_count(sp, S["ids_ready"], g + (u + 1))
                        sp.dma_start(slot_ids[bass.ds(g + u, 1), :, :].rearrange("a p s -> (a p) s"), ids_out[:, u, :]).then_inc(ids_st[u], 16)
                    for u in range(NB):
                        wait_count(sp, ids_st[u], 16 * k + 16)
                    sp.sem_inc(S["ids_stored"], NB)

            def lists_and_counts():
                sp.wait_ge(S["lists_ready"], 1)
                with sp.Fori(0, T) as t:
                    lo = base(sp, t)
                    with sp.Fori(lo, base(sp, t + 1)) as g:
                        at = (t * SS + (g - lo) * CH).with_bounds(min_val=0, max_val=SL - CH)
                        sp.dma_start(slot_ids[bass.ds(g, 1), :, :].rearrange("a p s -> (a p) s"), slot_list[:, bass.ds(at, CH)]).then_inc(S["lists_st"], 16)
                with sp.Fori(0, PAIRS) as k:
                    for v in range(4):
                        wait_count(sp, S["cq_ready"], 4 * k + (v + 3))
                        sp.dma_start(counts[bass.ds(2 * k, 2), :, v * Q * LO:(v + 1) * Q * LO].rearrange("c a f -> a c f"), cq[:, v % 2, :, :]).then_inc(cq_st[v % 2], 16)
                for v in range(2):
                    sp.wait_ge(cq_st[v], 16 * 2 * PAIRS)
                wait_count(sp, S["lists_st"], total * 16)

            def counts_in():
                with sp.Fori(0, LS) as layer:
                    with sp.If(layer > 0):
                        wait_count(sp, S["x_st"], layer * (16 * T))
                        wait_count(sp, S["mm_done"], layer * T)
                    sp.dma_start(xnat.rearrange("a b f -> a (b f)"), xtab[0:NP, :].rearrange("(a b) f -> a (b f)", b=LO)).then_inc(S["xnat_ld"], 16)
                    load_counts(layer)

            def load_counts(layer):
                with sp.Fori(0, T // G) as j:
                    for i in range(G):
                        n = layer * T + j * G + i
                        wait_count(sp, S["big_done"], n + 1)
                        sp.dma_start(cnt[i].rearrange("a d b -> a (d b)"), counts[bass.ds(j * G + i, 1), :, :].rearrange("c a f -> (c a) f")).then_inc(cnt_ld[i], 16)

            with sp.If(base(sp, 1) > SC):
                lists_by_chunk()
                feed(SG, LS)
            with sp.Else():
                lists_and_counts()
                counts_in()
            sp.sem_inc(S["f1_done"], 1)

            def load_w1(layer):
                wait_count(sp, S["f1_done"], layer * T + (LAG + 1))
                sp.dma_start(w1[:, :], t_in["w1t"][bass.ds(layer, 1), :, :].rearrange("a k n -> (a k) n")).then_inc(S["w1_ld"], 16)

            feed(TR, LT, load_w1, halves=True)
            sp.wait_ge(S["out_st"], 16 * T)

        @block.gpsimd
        def _(pool):
            nc.gpsimd.iota(diff_i[:, :], pattern=[[1, P]], base=0, channel_multiplier=-1).then_inc(S["const_pool"], 1)
            nc.gpsimd.iota(iota64_i[:, :], pattern=[[1, P]], base=0, channel_multiplier=0).then_inc(S["const_pool"], 1)
            nc.gpsimd.iota(node_i[:, :], pattern=[[P, T]], base=0, channel_multiplier=1).then_inc(S["const_pool"], 1)
            nc.gpsimd.iota(nodekey_i[:, :], pattern=[[-1, 64]], base=4095, channel_multiplier=-64).then_inc(S["const_pool"], 1)
            pool.wait_ge(S["rec_ready"], 1)
            for t in range(T):
                pool.indirect_dma_start(posrec, bass.IndirectOffsetOnAxis(ap=rank_i[:, t:t + 1], axis=0),
                                        rec[:, t, :], None).then_inc(S["rec_st"], 16)
            pool.wait_ge(S["pos_ld"], 16)
            pool.wait_ge(S["src_ld"], 32)
            pool.wait_ge(S["zero_st"], Z_STORES)
            for t in range(T):
                pool.indirect_dma_start(x0[:, t, :], None, xtab,
                                        bass.IndirectOffsetOnAxis(ap=posn[:, t, 0:1], axis=0)).then_inc(S["xgath"], 16)
            pool.wait_ge(S["meta_ready"], 1)
            total = chunk_total(pool)
            runs = src_run.rearrange("(n a) -> n a", a=1)

            def run_by_chunk():
                with pool.Fori(0, total, NB) as g:
                    for u in range(NB):
                        wait_count(pool, S["run_ready"], g + (u + 1))
                        pool.indirect_dma_start(raw[:, u, :], None, runs,
                                                bass.IndirectOffsetOnAxis(ap=run_i[:, u, :], axis=0)).then_inc(raw_ld[u], 16)

            def gather_all_slots(sems, layer, table, rows):
                ids_ld, rows_ld = sems[0:2]
                with pool.Fori(0, total, NB) as g:
                    k = (layer * total + g) // NB
                    for u in range(NB):
                        wait_count(pool, ids_ld[u], 16 * k + 16)
                        for s in range(CH):
                            pool.indirect_dma_start(rows[:, u, s, :], None, table,
                                                    bass.IndirectOffsetOnAxis(ap=ids[:, u, s:s + 1], axis=0)).then_inc(rows_ld[u], 16)

            landed = [pool.alloc_register(f"landed{u}") for u in range(NB)]
            for reg in landed:
                pool.reg_mov(reg, 0)

            def gather(sems, layer, table, rows):
                ids_ld, rows_ld = sems[0:2]
                whole = whole_chunks(pool)
                with pool.Fori(0, total, NB) as g:
                    k = (layer * total + g) // NB
                    for u in range(NB):
                        wait_count(pool, ids_ld[u], 16 * k + 16)
                        for s in range(CH // 2):
                            pool.indirect_dma_start(rows[:, u, s, :], None, table,
                                                    bass.IndirectOffsetOnAxis(ap=ids[:, u, s:s + 1], axis=0)).then_inc(rows_ld[u], 16)
                        pool.reg_add(landed[u], landed[u], 16 * (CH // 2))
                        with pool.If(has_upper(pool, g + u, u, whole)):
                            for s in range(CH // 2, CH):
                                pool.indirect_dma_start(rows[:, u, s, :], None, table,
                                                        bass.IndirectOffsetOnAxis(ap=ids[:, u, s:s + 1], axis=0)).then_inc(rows_ld[u], 16)
                            pool.reg_add(landed[u], landed[u], 16 * (CH - CH // 2))

            def all_read(sems, layer):
                for u in range(NB):
                    wait_count(pool, sems[1][u], 16 * CH * ((layer + 1) * total // NB))

            def store(table, rows, ready, stored, count):
                for t in range(T):
                    wait_count(pool, ready, count * T + (t + 1))
                    pool.indirect_dma_start(table, bass.IndirectOffsetOnAxis(ap=posn[:, t, 0:1], axis=0),
                                            rows[:, t, :], None).then_inc(stored, 16)
                wait_count(pool, stored, count * (16 * T) + 16 * T)

            with pool.If(disordered(pool) > 0):
                with pool.Fori(0, EJ) as j:
                    wait_count(pool, S["s_placed"], j + 1)
                    pool.indirect_dma_start(runs, bass.IndirectOffsetOnAxis(ap=s_place, axis=0), s_src, None).then_inc(S["s_stored"], 16)
                    wait_count(pool, S["s_stored"], 16 * j + 16)
            with pool.If(base(pool, 1) > SC):
                run_by_chunk()
                with pool.Fori(0, LS - 1) as layer:
                    gather_all_slots(SG, layer, xtab, xs)
                    all_read(SG, layer)
                    store(xtab, xp, S["x_ready"], S["x_st"], layer)
                gather_all_slots(SG, LS - 1, xtab, xs)
            with pool.Else():
                for t in range(T):
                    pool.indirect_dma_start(raw64[:, t, :], None, runs,
                                            bass.IndirectOffsetOnAxis(ap=posn[:, t, 1:2], axis=0)).then_inc(S["raw64_ld"], 16)
                with pool.Fori(0, LS - 1) as layer:
                    wait_count(pool, S["xnat_ld"], 16 * layer + 16)
                    store(xtab, xp, S["x_ready"], S["x_st"], layer)
            pool.wait_ge(S["x_ready"], LS * T)
            store(kvtab, kvn, S["kv_ready"], S["kv_st"], 0)
            with pool.Fori(0, LT - 1) as layer:
                gather(TR, layer, kvtab, kv)
                for u in range(NB):
                    wait_count(pool, TR[1][u], landed[u])
                store(kvtab, kvn, S["kv_ready"], S["kv_st"], layer + 1)
            gather(TR, LT - 1, kvtab, kv)
            for t in range(T):
                pool.wait_ge(S["out_ready"], t + 1)
                m = P if t < T - 1 else LAST
                pool.indirect_dma_start(out, bass.IndirectOffsetOnAxis(ap=posn[0:m, t, 0:1], axis=0),
                                        y_all[0:m, t, :], None).then_inc(S["out_st"], 16)

        @block.vector
        def _(dve):
            nc.vector.memset(dst_i, -1)
            nc.vector.memset(src_i, 0)
            nc.vector.memset(dnext, 1 << 20).then_inc(S["dst_free"], 1)
            nc.vector.memset(zeros[:, :], 0.0).then_inc(S["const_dve"], 1)
            nc.vector.memset(wqkvs[:, LT, D:4 * HID], 0.0)
            nc.vector.memset(bqkvs_row[:, LT, D:4 * HID], 0.0)
            nc.vector.memset(floors[:, 0:LS - 1], 0.0)
            nc.vector.memset(floors[:, LS - 1:LS], -3.0e38)
            dve.wait_ge(S["const_pool"], 4)
            nc.vector.tensor_scalar(ident[:, :], diff_i[:, :], 0.0, None, ALU.is_equal)
            nc.vector.tensor_scalar(upper[:, :], diff_i[:, :], 0.0, None, ALU.is_gt)
            nc.vector.tensor_copy(iota64[:, :], iota64_i[:, :])
            nc.vector.tensor_copy(iota8[:, :], iota64_i[:, 0:CH])
            nc.vector.tensor_copy(nodekey[:, :], nodekey_i[:, :])

            dve.wait_ge(S["dst_ld"], 32)
            dve.wait_ge(S["next_ld"], 32)
            nc.vector.memset(disorder[:, 1:2], 1.0)
            nc.vector.tensor_tensor(dhi, dst_i, dnext, ALU.is_gt)
            dve.drain()
            nc.vector.tensor_reduce(disorder[:, 0:1], dhi, AX.X, ALU.add)
            dve.drain().then_inc(S["disorder_ready"], 1)
            nc.vector.tensor_scalar(dhi_i, dst_i, 6, None, ALU.arith_shift_right)
            dve.drain()
            nc.vector.tensor_copy(dhi, dhi_i)
            nc.vector.tensor_scalar(dst_i, dst_i, 63, None, ALU.bitwise_and)
            dve.drain()
            nc.vector.tensor_copy(dlo, dst_i)
            nc.vector.tensor_copy(halves_bf[:, 0, :], dhi)
            nc.vector.tensor_copy(grid, iota64[:, 0:64].unsqueeze(2).to_broadcast((P, 64, JB)))
            dve.drain()
            nc.vector.tensor_copy(halves_bf[:, 1, :], dlo)
            dve.drain().then_inc(S["const_dve"], 1)
            with dve.Fori(0, EJ // (2 * JB)) as i:
                for u in range(2):
                    wait_count(dve, S["hot_used"], 2 * i + (u + 1))
                    for c, (hot, n) in enumerate(((hot_hi, HN), (hot_lo, 64))):
                        ins = nc.vector.tensor_tensor(
                            hot[u][:, 0:n, :], grid[:, 0:n, :],
                            halves_bf[:, c, bass.ds(i * (2 * JB) + u * JB, JB)].unsqueeze(1).to_broadcast((P, n, JB)),
                            ALU.is_equal)
                    ins.then_inc(S["hot_ready"], 1)
            dve.wait_ge(S["hist_done"], 1)
            nc.vector.tensor_copy(deg_nat[:, :], p_hist[0:64, 0:64])
            nc.vector.tensor_reduce(rowsum[:, 0:1], p_hist[0:64, 0:64], AX.X, ALU.add).then_inc(S["pre_ready"], 1)
            dve.drain()
            nc.vector.tensor_scalar(key_nat[:, :], deg_nat[:, :], DEG_CLAMP, 4096.0, ALU.min, ALU.mult)
            dve.drain()
            nc.vector.tensor_tensor(key_nat[:, :], key_nat[:, :], nodekey[:, :], ALU.add)
            dve.wait_ge(S["pre_done"], 1)
            nc.vector.tensor_copy(rowsum[:, 1:2], p_y[0:64, 0:1])
            dve.drain()
            nc.vector.tensor_tensor_scan(off_nat[:, :], deg_nat[:, :], zeros[0:64, 0:64], rowsum[:, 1:2], ALU.add, ALU.add)
            dve.drain()
            nc.vector.tensor_tensor(off_nat[:, :], off_nat[:, :], deg_nat[:, :], ALU.subtract).then_inc(S["nat_ready"], 1)
            dve.wait_ge(S["nat_ldb"], 16)
            dve.wait_ge(S["nat_turned"], 3)
            nc.vector.tensor_copy(nat_col[:, :, :].rearrange("p c t -> p (c t)"), p_t[:, 0:3 * T])
            dve.drain()
            for t in range(T):
                if t:
                    dve.drain()
                nc.vector.tensor_scalar(greater, keys_bc, nat_col[:, 0, t:t + 1], 0.0, ALU.is_gt, ALU.add,
                                        accum_out=rank_f[:, t:t + 1])
            nc.vector.tensor_copy(rec[:, :, 0], node_i[:, :])
            nc.vector.tensor_copy(rec[:, :, 1], nat_col[:, 1, :])
            nc.vector.tensor_copy(rec[:, :, 2], nat_col[:, 2, :])
            nc.vector.tensor_copy(rec[:, :, 3], node_i[:, :])
            dve.drain()
            nc.vector.tensor_copy(rank_i[:, :], rank_f[:, :])
            dve.drain().then_inc(S["rec_ready"], 1)
            dve.wait_ge(S["pos_ld"], 16)
            nc.vector.tensor_copy(off_pos[:, :], posn[:, :, 1])
            nc.vector.tensor_copy(deg_pos[:, :], posn[:, :, 2])
            dve.drain().then_inc(S["deg_ready"], 1)
            nc.vector.tensor_scalar(inv_cnt[:, :], deg_pos[:, :], 1.0, None, ALU.max)
            dve.drain()
            nc.vector.reciprocal(inv_cnt[:, :], inv_cnt[:, :])
            dve.wait_ge(S["degT_done"], 1)
            nc.vector.tensor_reduce(chunks_f[0:T, 0:1], p_t[0:T, 0:P], AX.X, ALU.max)
            dve.drain()
            nc.vector.tensor_scalar(chunks_i[0:T, 0:1], chunks_f[0:T, 0:1], float(CH - 1), float(2 * CH), ALU.add, ALU.max)
            dve.drain()
            nc.vector.tensor_scalar(chunks_i[0:T, 1:2], chunks_i[0:T, 0:1], CH_LOG, None, ALU.arith_shift_right)
            dve.drain()
            nc.vector.tensor_copy(chunks_f[0:T, 1:2], chunks_i[0:T, 1:2])
            dve.drain().then_inc(S["cnt_ready"], 1)
            dve.wait_ge(S["base_done"], 1)
            nc.vector.tensor_copy(meta[0:1, 0:T + 1], p_y[0:1, 0:T + 1])
            nc.vector.tensor_copy(meta[0:1, 30:31], p_y[0:1, 64:65])
            nc.vector.tensor_scalar(meta[0:1, 31:32], p_y[0:1, 1:2], float(NB), None, ALU.max)
            nc.vector.tensor_scalar(meta_i[0:1, 0:1], p_y[0:1, T:T + 1], float(NB - 1), None, ALU.add)
            dve.drain()
            nc.vector.tensor_scalar(meta[0:1, T:T + 1], meta_i[0:1, 0:1], -NB, None, ALU.bitwise_and)
            dve.drain().then_inc(S["meta_ready"], 1)

            def mask_by_chunk():
                with dve.Fori(0, T) as t:
                    dve.drain()
                    nc.vector.tensor_copy(left[:, :], deg_pos[:, bass.ds(t, 1)])
                    with dve.Fori(base(dve, t), base(dve, t + 1)) as g:
                        u = g % NB
                        wait_count(dve, S["raw_in"], g + 1)
                        dve.drain()
                        nc.vector.tensor_scalar(valid[:, :], iota8[:, :], left[:, 0:1], None, ALU.is_lt)
                        nc.vector.tensor_scalar(rawf[:, :], raw[:, bass.ds(u, 1), :], -float(DUMMY), None, ALU.add)
                        dve.drain()
                        nc.vector.tensor_scalar(left[:, :], left[:, :], -float(CH), None, ALU.add)
                        nc.vector.tensor_tensor(rawf[:, :], rawf[:, :], valid[:, :], ALU.mult)
                        wait_count(dve, S["ids_stored"], g + 1)
                        dve.drain()
                        nc.vector.tensor_scalar(ids_out[:, bass.ds(u, 1), :], rawf[:, :], float(DUMMY), None, ALU.add).then_inc(S["ids_ready"], 1)

            def sage_output(t, layer):
                wait_count(dve, S["mm_done"], layer * T + t + 1)
                nc.vector.tensor_tensor(part[:, :], p_y[:, 0:D], bl_bc[:, bass.ds(layer, 1), :], ALU.add)
                dve.drain()
                nc.vector.tensor_scalar(xp[:, bass.ds(t, 1), :], part[:, :], floors[:, bass.ds(layer, 1)], None, ALU.max)
                dve.drain().then_inc(S["x_ready"], 1)

            def sage_by_gather():
                with dve.Fori(0, LS) as layer:
                    with dve.Fori(0, T) as t:
                        dve.drain()
                        nc.vector.memset(agg[:, :], 0.0)
                        with dve.Fori(base(dve, t), base(dve, t + 1)) as g:
                            wait_count(dve, SG[3], layer * total + g + 1)
                            dve.drain()
                            nc.vector.tensor_reduce(part[:, :], xs[:, bass.ds(g % NB, 1), :, :].rearrange("p u s d -> p d (u s)"),
                                                    AX.X, ALU.add).then_inc(SG[2], 1)
                            dve.drain()
                            nc.vector.tensor_tensor(agg[:, :], agg[:, :], part[:, :], ALU.add)
                        dve.drain()
                        nc.vector.tensor_scalar(cat[:, 0:D], agg[:, :], inv_cnt[:, bass.ds(t, 1)], None, ALU.mult)
                        nc.vector.tensor_copy(cat[:, D:2 * D], xp[:, bass.ds(t, 1), :])
                        dve.drain().then_inc(S["catp"], 1)
                        sage_output(t, layer)

            def build_counts():
                dve.wait_ge(S["raw64_ld"], 16 * T)
                nc.vector.tensor_scalar(slot_f, raw64, 1.0, None, ALU.add)
                nc.vector.tensor_tensor(slot_v, iota64[:, 0:SS].unsqueeze(1).to_broadcast((P, T, SS)),
                                        deg_pos[:, :].unsqueeze(2).to_broadcast((P, T, SS)), ALU.is_lt)
                nc.vector.memset(slot_list[:, T * SS:SL], DUMMY)
                nc.vector.memset(halves[:, 0, T:2 * PAIRS, :], -1.0)
                nc.vector.memset(halves[:, 1, T:2 * PAIRS, :], -1.0)
                dve.drain()
                nc.vector.tensor_tensor(slot_f, slot_f, slot_v, ALU.mult)
                dve.drain()
                nc.vector.tensor_scalar(slot_v, slot_v, -float(DUMMY + 1), float(DUMMY), ALU.mult, ALU.add)
                nc.vector.tensor_scalar(slot_i, slot_f, -1.0, None, ALU.add)
                dve.drain()
                nc.vector.tensor_tensor(slot_list[:, 0:T * SS].rearrange("p (t s) -> p t s", s=SS), slot_f, slot_v, ALU.add)
                dve.drain().then_inc(S["lists_ready"], 1)
                nc.vector.tensor_scalar(raw64, slot_i, LO.bit_length() - 1, None, ALU.arith_shift_right)
                dve.drain()
                nc.vector.tensor_copy(halves[:, 0, 0:T, :], raw64)
                nc.vector.tensor_scalar(slot_i, slot_i, LO - 1, None, ALU.bitwise_and)
                dve.drain()
                nc.vector.tensor_copy(halves[:, 1, 0:T, :], slot_i)
                dve.drain()
                second = halves[:, 1, :, :].rearrange("p (k c) s -> p k c s", c=2)[:, :, 1, :]
                nc.vector.tensor_scalar(second, second, float(LO), None, ALU.add)
                nc.vector.tensor_copy(grid2, iota64[:, 0:HI].unsqueeze(2).to_broadcast((P, HI, Q)))
                dve.drain().then_inc(S["halves_ready"], 1)
                dve.wait_ge(S["halvesT_ready"], PAIRS)
                with dve.Fori(0, PAIRS) as k:
                    for v in range(4):
                        wait_count(dve, S["hot2_used"], 4 * k + (v + 1))
                        for c, n in ((0, HI), (1, 2 * LO)):
                            ins = nc.vector.tensor_tensor(
                                hots[v % 2][c], grid2[:, 0:n, :],
                                halvesT[:, bass.ds(k, 1), c, v * Q:(v + 1) * Q].rearrange("p a d -> p (a d)").unsqueeze(1).to_broadcast((P, n, Q)),
                                ALU.is_equal)
                        ins.then_inc(S["hot2_ready"], 1)

            def sage_by_counts():
                with dve.Fori(0, LS) as layer:
                    wait_count(dve, S["xnat_ld"], 16 * layer + 16)
                    for c in range(3):
                        nc.vector.tensor_copy(x3[:, :, c, :], xnat)
                        dve.drain()
                        if c < 2:
                            nc.vector.tensor_tensor(xnat, xnat, x3[:, :, c, :], ALU.subtract)
                            dve.drain()
                    dve.drain().then_inc(S["x3_ready"], 1)
                    with dve.Fori(0, T // G) as j:
                        for i in range(G):
                            t = j * G + i
                            wait_count(dve, S["big_done"], layer * T + t + (NC + 1))
                            nc.vector.tensor_reduce(agg[:, :], p_big[i][:, 0:3 * D].rearrange("p (c f) -> p f c", c=3), AX.X, ALU.add)
                            dve.drain()
                            nc.vector.tensor_scalar(cat[:, 0:D], agg[:, :], inv_cnt[:, bass.ds(t, 1)], None, ALU.mult)
                            nc.vector.tensor_copy(cat[:, D:2 * D], xp[:, bass.ds(t, 1), :])
                            dve.drain().then_inc(S["catp"], 1)
                            sage_output(t, layer)

            def place_edges():
                nc.vector.tensor_copy(s_next, off_nat[:, :])
                nc.vector.tensor_scalar(s_before, diff_i[:, :], 0.0, None, ALU.is_lt)
                nc.vector.tensor_scalar(s_col[:, 4:5], diff_i[:, 0:1], -1.0, float(2 * E + CH), ALU.mult, ALU.add)
                with dve.Fori(0, EJ) as j:
                    at = bass.ds(j, 1)
                    dve.drain()
                    nc.vector.tensor_scalar(s_a[:, 0:64], iota64[:, 0:64], dhi[:, at], None, ALU.is_equal)
                    nc.vector.tensor_scalar(s_b[:, 0:64], iota64[:, 0:64], dlo[:, at], None, ALU.is_equal)
                    nc.vector.tensor_copy(s_src, src_i[:, at])
                    nc.vector.tensor_scalar(s_col[:, 2:3], dhi[:, at], 0.0, None, ALU.is_ge)
                    nc.vector.tensor_scalar(s_col[:, 3:4], dhi[:, at], 0.0, s_col[:, 4:5], ALU.is_lt, ALU.mult)
                    dve.drain().then_inc(S["s_hot"], 1)
                    wait_count(dve, S["s_turned"], j + 1)
                    nc.vector.tensor_copy(s_at, psum[1][0:64, 0:P])
                    nc.vector.tensor_copy(s_bt, psum[1][0:64, P:2 * P])
                    dve.drain().then_inc(S["s_copied"], 1)
                    wait_count(dve, S["s_product"], j + 1)
                    nc.vector.tensor_copy(s_n, psum[4][:, 0:P])
                    nc.vector.tensor_tensor(s_b[:, 64:128], psum[2][:, 0:64], s_b[:, 0:64], ALU.mult)
                    dve.drain()
                    nc.vector.tensor_tensor(s_m, psum[3][:, 0:P], s_n, ALU.mult)
                    nc.vector.tensor_reduce(s_col[:, 0:1], s_b[:, 64:128], AX.X, ALU.add)
                    dve.drain()
                    nc.vector.tensor_tensor(s_m, s_m, s_before, ALU.mult)
                    dve.drain()
                    nc.vector.tensor_reduce(s_col[:, 1:2], s_m, AX.X, ALU.add)
                    dve.drain()
                    nc.vector.tensor_tensor(s_col[:, 0:1], s_col[:, 0:1], s_col[:, 1:2], ALU.add)
                    dve.drain()
                    nc.vector.tensor_tensor(s_col[:, 0:1], s_col[:, 0:1], s_col[:, 2:3], ALU.mult)
                    dve.drain()
                    nc.vector.tensor_tensor(s_place, s_col[:, 0:1], s_col[:, 3:4], ALU.add)
                    nc.vector.tensor_tensor(s_next, s_next, psum[5][0:64, 0:64], ALU.add)
                    dve.drain().then_inc(S["s_placed"], 1)
                    wait_count(dve, S["s_stored"], 16 * j + 16)

            dve.wait_ge(S["src_i_ld"], 32)
            with dve.If(disordered(dve) > 0):
                place_edges()
            dve.drain()

            dve.wait_ge(S["xgath"], 16 * T)
            nc.vector.tensor_copy(xp.rearrange("p t d -> p (t d)"), x0[:, :, :].rearrange("p t d -> p (t d)"))
            total = chunk_total(dve)
            dve.drain()
            with dve.If(base(dve, 1) > SC):
                mask_by_chunk()
                sage_by_gather()
            with dve.Else():
                build_counts()
                sage_by_counts()

            dve.drain()
            flat = x0[:, :, :].rearrange("p t d -> p (t d)")
            nc.vector.tensor_tensor(flat, flat, xp.rearrange("p t d -> p (t d)"), ALU.add)
            dve.drain()
            for t in range(T):
                nc.vector.bn_stats(stats[:, t, :], x0[:, t, :])
            dve.drain()
            for t in range(T):
                nc.vector.bn_aggr(mv[:, t, :], stats[:, t, :])
            dve.drain()
            nc.vector.tensor_scalar(std[:, :], mv[:, :, 1], 1e-5, None, ALU.add)
            dve.drain().then_inc(S["var_ready"], 1)
            dve.wait_ge(S["std_done"], 1)
            nc.vector.reciprocal(rstd[:, :], std[:, :])
            dve.drain()
            for t in range(T):
                nc.vector.tensor_scalar(x0[:, t, :], x0[:, t, :], mv[:, t, 0:1], rstd[:, t:t + 1], ALU.subtract, ALU.mult)
            dve.drain()
            nc.vector.memset(kvn[:, :, :], 1.0)
            nc.vector.memset(ones_row[:, :], 1.0)
            dve.drain().then_inc(S["ones_ready"], 1)
            dve.wait_ge(S["b1_done"], 1)
            nc.vector.tensor_copy(b1_all[:, :], p_t2[:, 0:LT * FC])
            dve.drain().then_inc(S["b1_used"], 1)

            def first_inputs(j):
                nc.vector.tensor_copy(y[:, :, 0:D], x0[:, bass.ds(j * G, G), :])
                dve.drain().then_inc(S["x1_ready"], 1)

            def first_sums(j):
                wait_count(dve, S["hi_done"], j * G + G)
                for i in range(G):
                    nc.vector.tensor_tensor(h1[:, i, :], column(i), bi_bc[:, :], ALU.add)
                dve.drain().then_inc(S["hi_ready"], 1)

            def first_states(j):
                wait_count(dve, S["hs_ready"], j * G + G)
                nc.vector.tensor_copy(h_all[:, bass.ds(j * G, G), :], hs[:, :, :])
                dve.drain()

            first_inputs(0)
            first_sums(0)
            with dve.Fori(0, T // G - 1) as j:
                first_inputs(j + 1)
                first_states(j)
                first_sums(j + 1)
            first_states(T // G - 1)

            def scores(g, ql, layer):
                u = g % NB
                this, other = bass.ds(g % 2, 1), bass.ds((g + 1) % 2, 1)
                wait_count(dve, TR[3], ql + 1)
                nc.vector.tensor_tensor(prod[:, :, :, 0:DH], kv[:, bass.ds(u, 1), :, 0:HID].rearrange("p u s (h d) -> p (u s) h d", d=DH),
                                        q_t[:, :].rearrange("p (h d) -> p h d", d=DH).unsqueeze(1).to_broadcast((P, CH, HEADS, DH)), ALU.mult)
                nc.vector.tensor_scalar(prod[:, :, :, DH], ids[:, bass.ds(u, 1), :].rearrange("p u s -> p (u s)").unsqueeze(2).to_broadcast((P, CH, HEADS)),
                                        float(DUMMY), NEG, ALU.is_equal, ALU.mult)
                dve.drain()
                nc.vector.tensor_reduce(score[:, this, :, 0:CH].rearrange("p a h s -> p s (a h)"), prod[:, :, :, :], AX.X, ALU.add)
                dve.drain()
                nc.vector.tensor_reduce(score[:, other, :, CH], score[:, this, :, :], AX.X, ALU.max)
                dve.drain()
                nc.vector.tensor_tensor(delta[:, this, :, :].rearrange("p a h s -> p (a h) s"), score[:, this, :, :].rearrange("p a h s -> p (a h) s"),
                                        score[:, other, :, CH:CH + 1].rearrange("p a h s -> p (a h) s").to_broadcast((P, HEADS, CH + 1)), ALU.subtract).then_inc(S["d_ready"], 1)

            def weigh(g, ql, sums):
                u, v = g % NB, g % 2
                wait_count(dve, S["e_done"], ql + 1)
                nc.vector.tensor_tensor(wv[:, bass.ds(v, 1), 0:CH, :].rearrange("p a s (h w) -> p (a s) h w", w=VW),
                                        kv[:, bass.ds(u, 1), :, HID:KV].rearrange("p u s (h w) -> p (u s) h w", w=VW),
                                        expo[:, bass.ds(v, 1), :, 0:CH].rearrange("p a h s -> p (a s) h").unsqueeze(3).to_broadcast((P, CH, HEADS, VW)),
                                        ALU.mult).then_inc(TR[2], 1)
                wait_count(dve, S["sum_done"], sums + 2)
                nc.vector.tensor_tensor(wv[:, bass.ds(v, 1), CH, :].rearrange("p a (h w) -> p (a h) w", w=VW),
                                        p_acc[:, 0:HEADS * VW].rearrange("p (h w) -> p h w", w=VW),
                                        expo[:, bass.ds(v, 1), :, CH:CH + 1].rearrange("p a h s -> p (a h) s").to_broadcast((P, HEADS, VW)),
                                        ALU.mult).then_inc(S["w_ready"], 1)

            def slot(j, i, layer, m):
                t = j * G + i
                k = (i - LAG) % G
                dve.drain()
                nc.vector.tensor_copy(q_t[:, :], q_all[:, bass.ds(t, 1), :])
                nc.vector.memset(score[:, :, :, CH], 2 * NEG)
                dve.drain()
                first = base(dve, t)
                ql = layer * total + first
                scores(first, ql, layer)
                if i:
                    weigh(first + (2 * NB - 1), ql - 1, ql + layer * T + t - 2)
                else:
                    with dve.If(j > 0):
                        weigh(first + (2 * NB - 1), ql - 1, ql + layer * T + t - 2)
                if i == 1:
                    with dve.If(j > 0):
                        gate_logits(layer)
                with dve.Fori(first + 1, base(dve, t + 1)) as g:
                    ql = layer * total + g
                    scores(g, ql, layer)
                    weigh(g + (2 * NB - 1), ql - 1, ql + layer * T + t - 1)
                with dve.If(j > (LAG - 1 - i) // G):
                    new_state((t - LAG).with_bounds(min_val=0, max_val=T - 1), k, layer * T + t)
                if i == 0:
                    with dve.If(j > 0):
                        gated_parts((j - 1).with_bounds(min_val=0, max_val=T // G - 1), m * G)
                if i == 1:
                    with dve.If(j > 0):
                        gated(m)
                        normed(layer)

            def new_state(t, i, n):
                wait_count(dve, S["f2_done"], n + 1)
                nc.vector.tensor_tensor(hs[:, i, :], column(i), h1[:, i, :], ALU.add)
                dve.drain().then_inc(S["hs_ready"], 1)
                nc.vector.tensor_copy(h_all[:, bass.ds(t, 1), :], hs[:, i, :])

            def gated_parts(j, n):
                ts = bass.ds(j * G, G)
                wait_count(dve, S["acc_saved"], n + 1)
                accw = acc[:, :, :].rearrange("p i (h w) -> p i h w", w=VW)
                nc.vector.tensor_scalar(rden[:, :, :], accw[:, :, :, DH], 1e-16, None, ALU.add)
                nc.vector.tensor_copy(tri[:, :, 1, :], r_all[:, ts, :])
                dve.drain()
                nc.vector.reciprocal(rden[:, :, :], rden[:, :, :])
                dve.drain()
                for i in range(G):
                    nc.vector.tensor_tensor(tri[:, i, 0, :].rearrange("p (h w) -> p h w", w=DH), accw[:, i, :, 0:DH],
                                            rden[:, i, :].unsqueeze(2).to_broadcast((P, HEADS, DH)), ALU.mult)
                dve.drain()
                nc.vector.tensor_tensor(tri[:, :, 2, :], tri[:, :, 0, :], tri[:, :, 1, :], ALU.subtract)
                nc.vector.tensor_tensor(y[:, :, :], tri[:, :, 0, :], h_all[:, ts, :], ALU.add)

            def gate_logits(layer):
                dve.drain()
                nc.vector.tensor_tensor(triw[:, :, :], tri[:, :, :, :].rearrange("p i c f -> p i (c f)"),
                                        wbeta_bc[:, bass.ds(layer, 1), :].to_broadcast((P, G, 3 * HID)), ALU.mult)
                dve.drain()
                nc.vector.tensor_reduce(gate[:, 0, :], triw[:, :, :], AX.X, ALU.add)
                dve.drain().then_inc(S["z_ready"], 1)

            def gated(m):
                wait_count(dve, S["z_done"], m)
                nc.vector.tensor_scalar(gate[:, 2, :], gate[:, 1, :], -1.0, -1.0, ALU.mult, ALU.add)
                dve.drain()
                nc.vector.reciprocal(gate[:, 3, :], gate[:, 2, :])
                dve.drain()
                for i in range(G):
                    nc.vector.scalar_tensor_tensor(out=y[:, i, :], in0=tri[:, i, 2, :], scalar=gate[:, 3, i:i + 1], in1=y[:, i, :],
                                                   op0=ALU.mult, op1=ALU.add)
                dve.drain()
                for i in range(G):
                    nc.vector.bn_stats(stats[:, i, :], y[:, i, :])
                dve.drain()
                for i in range(G):
                    nc.vector.bn_aggr(mv[:, i, :], stats[:, i, :])
                dve.drain()
                nc.vector.tensor_scalar(std[:, 0:G], mv[:, 0:G, 1], 1e-5, None, ALU.add)
                dve.drain().then_inc(S["var_ready"], 1)
                wait_count(dve, S["std_done"], m + 1)

            def normed(layer):
                nc.vector.reciprocal(rstd[:, 0:G], std[:, 0:G])
                dve.drain()
                for i in range(G):
                    nc.vector.tensor_scalar(y[:, i, :], y[:, i, :], mv[:, i, 0:1], rstd[:, i:i + 1], ALU.subtract, ALU.mult)
                dve.drain()
                nc.vector.tensor_tensor(y[:, :, :], y[:, :, :], lng_bc[:, bass.ds(layer, 1), :].to_broadcast((P, G, HID)), ALU.mult)
                dve.drain()
                nc.vector.tensor_tensor(h1[:, :, :], y[:, :, :], lnb_bc[:, bass.ds(layer, 1), :].to_broadcast((P, G, HID)), ALU.add)
                dve.drain().then_inc(S["h1_ready"], 1)

            def new_states(n):
                wait_count(dve, S["f2_done"], n + G)
                for i in range(G):
                    nc.vector.tensor_tensor(hs[:, i, :], column(i), h1[:, i, :], ALU.add).then_inc(S["hs_ready"], 1)
                dve.drain()
                nc.vector.tensor_copy(h_all[:, T - G:T, :], hs[:, :, :])

            with dve.Fori(0, LT) as layer:
                with dve.Fori(0, T // G) as j:
                    m = layer * (T // G) + j
                    for i in range(G):
                        slot(j, i, layer, m)
                ql = (layer + 1) * total
                weigh(base(dve, T) + (2 * NB - 1), ql - 1, ql + layer * T + T - 2)
                m = layer * (T // G) + T // G
                gated_parts(T // G - 1, m * G)
                gate_logits(layer)
                for k in range(T - LAG, T - G):
                    new_state(k, k % G, layer * T + k + LAG)
                gated(m)
                normed(layer)
                new_states(layer * T + T - G + LAG)

            for n, (lo, hi) in enumerate(RESULTS):
                wait_count(dve, S["kv_ready"], LT * T + hi)
                dve.drain()
                nc.vector.scalar_tensor_tensor(out=y_all[:, lo:hi, :], in0=q_all[:, lo:hi, 0:D], scalar=float(DH) ** 0.5, in1=x0[:, lo:hi, :],
                                               op0=ALU.mult, op1=ALU.add)
                dve.drain()
                for t in range(lo, hi):
                    nc.vector.bn_stats(stats[:, t, :], y_all[:, t, :])
                dve.drain()
                for t in range(lo, hi):
                    nc.vector.bn_aggr(mv[:, t, :], stats[:, t, :])
                dve.drain()
                nc.vector.tensor_scalar(std[:, lo:hi], mv[:, lo:hi, 1], 1e-5, None, ALU.add)
                dve.drain().then_inc(S["fvar_ready"], 1)
                dve.wait_ge(S["fstd_done"], n + 1)
                nc.vector.reciprocal(rstd[:, lo:hi], std[:, lo:hi])
                dve.drain()
                for t in range(lo, hi):
                    nc.vector.tensor_scalar(y_all[:, t, :], y_all[:, t, :], mv[:, t, 0:1], rstd[:, t:t + 1],
                                            ALU.subtract, ALU.mult).then_inc(S["out_ready"], 1)

        @block.scalar
        def _(act):
            act.wait_ge(S["meta_ready"], 1)

            def run_starts():
                act.sem_inc(S["ids_stored"], NB)
                with act.Fori(0, T) as t:
                    act.drain()
                    nc.scalar.activation(run_at[:, :], off_pos[:, bass.ds(t, 1)], ACT.Copy)
                    with act.Fori(base(act, t), base(act, t + 1)) as g:
                        wait_count(act, S["ids_stored"], g + 1)
                        act.drain()
                        nc.scalar.activation(run_i[:, bass.ds(g % NB, 1), :], run_at[:, :], ACT.Copy).then_inc(S["run_ready"], 1)
                        nc.scalar.activation(run_at[:, :], run_at[:, :], ACT.Copy, bias=float(CH))

            def counts_out():
                for k in range(PAIRS):
                    act.wait_ge(S["halves_turned"], k + 1)
                    nc.scalar.copy(halvesT[:, k, :, :].rearrange("p c d -> p (c d)"), psum[k % 2][:, 0:2 * P]).then_inc(S["halvesT_ready"], 1)
                act.sem_inc(S["cq_ready"], 2)
                with act.Fori(0, PAIRS) as k:
                    for v in range(4):
                        if v < 2:
                            with act.If(k > 0):
                                wait_count(act, cq_st[v], 32 * k)
                        else:
                            wait_count(act, cq_st[v - 2], 32 * k + 16)
                        wait_count(act, S["hot2_used"], 4 * k + (v + 3))
                        for b in range(4):
                            nc.scalar.copy(cq[:, v % 2, :, b * DB * LO:(b + 1) * DB * LO].rearrange("a c (d l) -> a c d l", l=LO),
                                           psum[4 * (v % 2) + b][0:HI, :].rearrange("a (d c l) -> a c d l", c=2, l=LO))
                        act.drain().then_inc(S["cq_ready"], 1)

            def turned_cats():
                with act.Fori(0, LS * T) as n:
                    wait_count(act, S["catt"], n + 1)
                    nc.scalar.copy(catT[:, :], p_t[:, 0:P]).then_inc(S["catc"], 1)

            with act.If(base(act, 1) > SC):
                run_starts()
                turned_cats()
            with act.Else():
                counts_out()
                turned_cats()
            act.wait_ge(S["var_ready"], 1)
            nc.scalar.activation(std[:, :], std[:, :], ACT.Sqrt)
            act.drain().then_inc(S["std_done"], 1)

            def turned(i, src, dst, name_in, name_out, n):
                wait_count(act, S[name_in], n + 1)
                nc.scalar.copy(dst[:, i * P:(i + 1) * P], src[:, 0:P]).then_inc(S[name_out], 1)

            def projections(t, n, bank):
                wait_count(act, S["proj_done"], n + 1)
                ts = bass.ds(t, 1)
                p = p_wide[bank]
                nc.scalar.activation(q_all[:, ts, :], p[:, 0:HID], ACT.Copy, scale=float(DH) ** -0.5)
                nc.scalar.activation(kvn[:, ts, 0:HID], p[:, HID:2 * HID], ACT.Copy)
                nc.scalar.activation(kvn[:, ts, HID:KV].rearrange("p a (h w) -> p (a h) w", w=VW)[:, :, 0:DH],
                                     p[:, 2 * HID:3 * HID].rearrange("p (h w) -> p h w", w=DH), ACT.Copy)
                nc.scalar.activation(r_all[:, ts, :], p[:, 3 * HID:4 * HID], ACT.Copy)
                act.drain().then_inc(S["kv_ready"], 1)

            def gelus(i, n, bank, behind=0):
                wait_count(act, S["f1_done"], n + 2)
                if behind:
                    wait_count(act, S["f2_done"], n - 1)
                for c in range(FC):
                    nc.scalar.activation(gT[:, i % 2, c, :], p_wide[bank][:, c * P:(c + 1) * P], ACT.Gelu, bias=b1[:, c:c + 1])
                act.drain().then_inc(S["g_done"], 1)

            def result_deviations(n):
                act.wait_ge(S["fvar_ready"], n + 1)
                lo, hi = RESULTS[n]
                nc.scalar.activation(std[:, lo:hi], std[:, lo:hi], ACT.Sqrt)
                act.drain().then_inc(S["fstd_done"], 1)

            def states_on(t, n, last=None):
                for i in range(G + 1):
                    if last is not None and i == G:
                        with act.If(last > 0):
                            result_deviations(0)
                    if i < G:
                        turned(i, p_turn[i % 2], hT, "hs_turned", "hT_ready", n + i)
                    if i:
                        projections(t + (i - 1), n + (i - 1), (i - 1) % 2)

            def weights_of(g, ql):
                wait_count(act, S["d_ready"], ql + 1)
                v = bass.ds(g % 2, 1)
                nc.scalar.activation(expo[:, v, :, :].rearrange("p a h s -> p (a h s)"),
                                     delta[:, v, :, :].rearrange("p a h s -> p (a h s)"), ACT.Exp)
                act.drain().then_inc(S["e_done"], 1)

            def save_sum(i, ql, n):
                wait_count(act, S["sum_done"], ql + n + 2)
                nc.scalar.copy(acc[:, i, :], p_acc[:, 0:HEADS * VW]).then_inc(S["acc_saved"], 1)
                act.drain().then_inc(S["sum_done"], 1)

            def gate_exp(m):
                wait_count(act, S["z_ready"], m)
                nc.scalar.activation(gate[:, 1, :], gate[:, 0, :], ACT.Exp, scale=-1.0)
                act.drain().then_inc(S["z_done"], 1)

            def deviations(m):
                wait_count(act, S["var_ready"], m + 1)
                nc.scalar.activation(std[:, 0:G], std[:, 0:G], ACT.Sqrt)
                act.drain().then_inc(S["std_done"], 1)

            def first_turned(j):
                for i in range(G):
                    wait_count(act, S["x1_turned"], j * G + (i + 1))
                    nc.scalar.copy(h1T[0:D, i * P:(i + 1) * P], p_turn[i % 2][0:D, 0:P]).then_inc(S["xT_ready"], 1)

            def first_gelu(j):
                wait_count(act, S["hi_ready"], j + 1)
                nc.scalar.activation(hs[:, :, :], h1[:, :, :], ACT.Gelu)
                act.drain().then_inc(S["hs_ready"], G)

            first_turned(0)
            first_gelu(0)
            with act.Fori(0, T // G - 1) as j:
                first_turned(j + 1)
                states_on(j * G, j * G)
                first_gelu(j + 1)
            states_on(T - G, T - G)
            act.wait_ge(S["b1_used"], 1)
            total = chunk_total(act)

            with act.Fori(0, LT) as layer:
                act.drain()
                nc.scalar.copy(b1[:, :], b1_all[:, bass.ds(layer * FC, FC)])
                with act.Fori(0, T // G) as j:
                    m = layer * (T // G) + j
                    for i in range(G):
                        t = j * G + i
                        first = base(act, t)
                        ql = layer * total + first
                        weights_of(first, ql)
                        if i:
                            save_sum(i - 1, ql, layer * T + t - 1)
                        else:
                            with act.If(j > 0):
                                save_sum(G - 1, ql, layer * T + t - 1)
                        if i == 1:
                            with act.If(j > 0):
                                gate_exp(m)
                        n = layer * T + t
                        with act.If(j > (LAG + 1 - i) // G):
                            projections((t - LAG - 2).with_bounds(min_val=0, max_val=T - 1), n + (T - LAG - 2), 1)
                        with act.If(j > (LAG - i) // G):
                            turned((i - LAG - 1) % G, p_turn[1], hT, "hs_turned", "hT_ready", n + (T - LAG - 1))
                        with act.If(j > (LAG - 1 - i) // G):
                            turned((i - LAG) % G, p_turn[0], h1T, "h1_turned", "h1T_ready", n)
                            gelus((i - LAG) % G, n, 0)
                        with act.Fori(first + 1, base(act, t + 1)) as g:
                            weights_of(g, layer * total + g)
                        if i == 1:
                            with act.If(j > 0):
                                deviations(m)
                save_sum(G - 1, (layer + 1) * total, layer * T + T - 1)
                m = layer * (T // G) + T // G
                on, ff = layer * T + T, layer * T + LAG
                projections(T - LAG - 2, on + (T - LAG - 2), 1)
                turned((T - LAG - 1) % G, p_turn[1], hT, "hs_turned", "hT_ready", on + (T - LAG - 1))
                for k in range(T - LAG, T - G):
                    turned(k % G, p_turn[0], h1T, "h1_turned", "h1T_ready", ff + k)
                    gelus(k % G, ff + k, 0)
                    if k == T - LAG:
                        projections(T - LAG - 1, on + (T - LAG - 1), 1)
                gate_exp(m)
                for k in range(T - LAG, T - G):
                    turned(k % G, p_turn[1], hT, "hs_turned", "hT_ready", on + k)
                    if k == T - LAG:
                        deviations(m)
                    projections(k, on + k, (k - T + LAG) % 2)
                for i in range(G):
                    turned(i, p_turn[i % 2], h1T, "h1_turned", "h1T_ready", ff + (T - G + i))
                for i in range(G):
                    gelus(i, ff + (T - G + i), i % 2, behind=i >= 2)
                states_on(T - G, on + (T - G), last=layer - (LT - 2))
            result_deviations(1)

        @block.tensor
        def _(pe):
            pe.wait_ge(S["const_dve"], 2)
            zb = zeros[:, 0:32].bitcast(BF16)
            pe.sem_inc(S["hot_used"], 2)
            nc.tensor.matmul(p_hist[0:64, 0:64], zb, zb, start=True, stop=False)
            with pe.Fori(0, EJ // (2 * JB)) as i:
                for u in range(2):
                    wait_count(pe, S["hot_ready"], 2 * i + (u + 1))
                    for j in range(JB):
                        mm = nc.tensor.matmul(p_hist[0:HN, 0:64], hot_hi[u][:, 0:HN, j], hot_lo[u][:, :, j], start=False, stop=False)
                    mm.then_inc(S["hot_used"], 1)
            nc.tensor.matmul(p_hist[0:64, 0:64], zb, zb, start=False, stop=True).then_inc(S["hist_done"], 1)
            pe.wait_ge(S["pre_ready"], 1)
            nc.tensor.matmul(p_y[0:64, 0:1], upper[0:64, 0:64], rowsum[:, 0:1], start=True, stop=True).then_inc(S["pre_done"], 1)
            pe.wait_ge(S["nat_ld"], 48)
            for i in range(3):
                nc.tensor.transpose(p_t[:, i * T:(i + 1) * T], nat_row[:, i, :], ident[0:T, 0:T]).then_inc(S["nat_turned"], 1)
            pe.wait_ge(S["deg_ready"], 1)
            nc.tensor.transpose(p_t[0:T, 0:P], deg_pos[:, :], ident[:, :]).then_inc(S["degT_done"], 1)
            pe.wait_ge(S["cnt_ready"], 1)
            pe.wait_ge(S["disorder_ready"], 1)
            nc.tensor.matmul(p_y[0:1, 64:65], disorder[:, 0:1], disorder[:, 1:2], start=True, stop=True)
            nc.tensor.matmul(p_y[0:1, 0:T + 1], chunks_f[0:T, 1:2], upper[0:T, 0:T + 1], start=True, stop=True).then_inc(S["base_done"], 1)
            pe.wait_ge(S["w_ld"], W_LOADS)
            def turn_cat(n):
                wait_count(pe, S["catp"], n)
                nc.tensor.transpose(p_t[:, 0:P], cat[:, :], ident[:, :]).then_inc(S["catt"], 1)

            def times_weights(layer, n):
                wait_count(pe, S["catc"], n)
                nc.tensor.matmul(p_y[:, 0:D], catT[:, :], wlr[:, bass.ds(layer, 1), :], start=True, stop=True).then_inc(S["mm_done"], 1)

            def count_edges():
                pe.wait_ge(S["halves_ready"], 1)
                for k in range(PAIRS):
                    if k >= 2:
                        pe.wait_ge(S["halvesT_ready"], k - 1)
                    for c in range(2):
                        tr = nc.tensor.transpose(psum[k % 2][:, c * P:(c + 1) * P], halves[:, c, 2 * k:2 * k + 2, :].rearrange("p t s -> p (t s)"), ident[:, :])
                    tr.then_inc(S["halves_turned"], 1)
                pe.sem_inc(S["hot2_used"], 2)
                with pe.Fori(0, PAIRS) as k:
                    for v in range(4):
                        wait_count(pe, S["hot2_ready"], 4 * k + (v + 1))
                        wait_count(pe, S["cq_ready"], 4 * k + (v + 1))
                        for d in range(Q):
                            mm = nc.tensor.matmul(psum[4 * (v % 2) + d // DB][0:HI, d % DB * 2 * LO:(d % DB + 1) * 2 * LO],
                                                  hots[v % 2][0][:, :, d], hots[v % 2][1][:, :, d], start=True, stop=True)
                        mm.then_inc(S["hot2_used"], 1)

            def aggregate():
                pe.sem_inc(S["big_done"], NC)
                with pe.Fori(0, LS) as layer:
                    wait_count(pe, S["x3_ready"], layer + 1)
                    with pe.Fori(0, T // G) as j:
                        for i in range(G):
                            n = layer * T + j * G + i
                            wait_count(pe, cnt_ld[i], (layer * (T // G) + j) * 16 + 16)
                            for b in range(LO):
                                if b == LO * 3 // 4:
                                    if i:
                                        turn_cat(n)
                                    else:
                                        with pe.If(j > 0):
                                            turn_cat(n)
                                mm = nc.tensor.matmul(p_big[i][:, 0:3 * D], cnt[i][:, :, b], x3[:, b, :, :].rearrange("a c f -> a (c f)"),
                                                      start=(b == 0), stop=(b == LO - 1))
                            mm.then_inc(S["big_done"], 1)
                            if i:
                                times_weights(layer, n)
                            else:
                                with pe.If(j > 0):
                                    times_weights(layer, n)
                    turn_cat((layer + 1) * T)
                    times_weights(layer, (layer + 1) * T)

            pe.wait_ge(S["meta_ready"], 1)
            with pe.If(disordered(pe) > 0):
                with pe.Fori(0, EJ) as j:
                    wait_count(pe, S["s_hot"], j + 1)
                    nc.tensor.transpose(psum[1][0:64, 0:P], s_a[:, 0:64], ident[:, :])
                    nc.tensor.transpose(psum[1][0:64, P:2 * P], s_b[:, 0:64], ident[:, :]).then_inc(S["s_turned"], 1)
                    wait_count(pe, S["s_copied"], j + 1)
                    nc.tensor.matmul(psum[2][:, 0:64], s_at, s_next, start=True, stop=True)
                    nc.tensor.matmul(psum[3][:, 0:P], s_at, s_at, start=True, stop=True)
                    nc.tensor.matmul(psum[4][:, 0:P], s_bt, s_bt, start=True, stop=True)
                    nc.tensor.matmul(psum[5][0:64, 0:64], s_a[:, 0:64], s_b[:, 0:64], start=True, stop=True).then_inc(S["s_product"], 1)
            with pe.If(base(pe, 1) > SC):
                with pe.Fori(0, LS) as layer:
                    with pe.Fori(0, T) as t:
                        turn_cat(layer * T + t + 1)
                        times_weights(layer, layer * T + t + 1)
            with pe.Else():
                count_edges()
                aggregate()
            nc.tensor.transpose(p_t2[:, 0:LT * FC], b1_row[:, :], ident[0:LT * FC, 0:LT * FC]).then_inc(S["b1_done"], 1)

            pe.wait_ge(S["ones_ready"], 1)
            pe.sem_inc(S["acc_saved"], 1)
            pe.sem_inc(S["sum_done"], 1)
            for name in ("h1_turned", "h1T_ready", "f1_done", "g_done", "f2_done"):
                pe.sem_inc(S[name], LAG)
            nc.tensor.matmul(p_acc[:, 0:HEADS * VW], ident[:, :], zeros[:, 0:HEADS * VW], start=True, stop=True).then_inc(S["sum_done"], 1)

            def turn(i, states, bank, name_in, count, name_out, rows=P):
                if count is not None:
                    wait_count(pe, S[name_in], count)
                nc.tensor.transpose(p_turn[bank][0:rows, 0:P], states[:, i, 0:rows], ident[:, :]).then_inc(S[name_out], 1)

            def project(i, layer, n, bank):
                wait_count(pe, S["hT_ready"], n + 1)
                nc.tensor.matmul(p_wide[bank][:, :], ones_row[:, :], bqkvs_row[:, bass.ds(layer, 1), :], start=True, stop=False)
                nc.tensor.matmul(p_wide[bank][:, :], hT[:, i * P:(i + 1) * P], wqkvs[:, bass.ds(layer, 1), :],
                                 start=False, stop=True).then_inc(S["proj_done"], 1)

            def project_all(layer, n):
                for i in range(G):
                    if i >= 2:
                        wait_count(pe, S["hT_ready"], n + (i - 1))
                    turn(i, hs, i % 2, "hs_ready", n + (i + 1), "hs_turned")
                    if i >= 3:
                        wait_count(pe, S["kv_ready"], n + (i - 2))
                    if i:
                        project(i - 1, layer, n + (i - 1), (i - 1) % 2)
                wait_count(pe, S["kv_ready"], n + (G - 2))
                project(G - 1, layer, n + (G - 1), (G - 1) % 2)

            def inner(i, n, bank):
                wait_count(pe, S["h1T_ready"], n + 1)
                for c in range(FC):
                    mm = nc.tensor.matmul(p_wide[bank][:, c * P:(c + 1) * P], w1[:, c * P:(c + 1) * P], h1T[:, i * P:(i + 1) * P],
                                          start=True, stop=True)
                mm.then_inc(S["f1_done"], 1)

            def outer(i, layer, n):
                wait_count(pe, S["g_done"], n + 1)
                nc.tensor.matmul(column(i), ones_row[:, :], b2_row[:, bass.ds(layer, 1), :], start=True, stop=False)
                for c in range(FC):
                    mm = nc.tensor.matmul(column(i), gT[:, i % 2, c, :], w2[:, bass.ds(layer, 1), c, :], start=False, stop=(c == FC - 1))
                mm.then_inc(S["f2_done"], 1)

            def add_chunk(g, ql):
                wait_count(pe, S["w_ready"], ql + 1)
                for s in range(CH + 1):
                    mm = nc.tensor.matmul(p_acc[:, 0:HEADS * VW], ident[:, :], wv[:, bass.ds(g % 2, 1), s, :],
                                          start=(s == 0), stop=(s == CH))
                mm.then_inc(S["sum_done"], 1)

            def first_products(j):
                for i in range(G):
                    if i >= 2:
                        wait_count(pe, S["xT_ready"], j * G + (i - 1))
                    turn(i, y, i % 2, "x1_ready", j + 1, "x1_turned", rows=D)
                for i in range(G):
                    wait_count(pe, S["xT_ready"], j * G + (i + 1))
                    nc.tensor.matmul(column(i), h1T[0:D, i * P:(i + 1) * P], wi[:, :], start=True, stop=True).then_inc(S["hi_done"], 1)

            first_products(0)
            with pe.Fori(0, T // G - 1) as j:
                first_products(j + 1)
                project_all(0, j * G)
            project_all(0, T - G)

            total = chunk_total(pe)
            with pe.Fori(0, LT) as layer:
                wait_count(pe, S["w1_ld"], 16 * layer + 16)
                with pe.Fori(0, T // G) as j:
                    m = layer * (T // G) + j
                    for i in range(G):
                        t = j * G + i
                        n = layer * T + t
                        now, then = (i - LAG) % G, (i - LAG - 1) % G
                        with pe.If(j > (LAG - i) // G):
                            turn(then, hs, 1, "hs_ready", n + (T - LAG), "hs_turned")
                        with pe.If(j > (LAG - 1 - i) // G):
                            turn(now, h1, 0, "h1_ready", m if now == 0 else None, "h1_turned")
                            inner(now, n, 0)
                        wait_count(pe, S["acc_saved"], n + 1)
                        first = base(pe, t)
                        add_chunk(first, layer * total + first)
                        with pe.If(j > (LAG - 1 - i) // G):
                            outer(now, layer, n)
                        with pe.If(j > (LAG - i) // G):
                            wait_count(pe, S["kv_ready"], n + (T - LAG - 1))
                            project(then, layer + 1, n + (T - LAG - 1), 1)
                        with pe.Fori(first + 1, base(pe, t + 1)) as g:
                            add_chunk(g, layer * total + g)
                m = layer * (T // G) + T // G
                on, ff = layer * T + T, layer * T + LAG
                turn((T - LAG - 1) % G, hs, 1, "hs_ready", on + (T - LAG), "hs_turned")
                for k in range(T - LAG, T - G):
                    turn(k % G, h1, 0, "h1_ready", m - 1, "h1_turned")
                    inner(k % G, ff + k, 0)
                    if k == T - LAG:
                        wait_count(pe, S["kv_ready"], on + (T - LAG - 1))
                        project((T - LAG - 1) % G, layer + 1, on + (T - LAG - 1), 1)
                    outer(k % G, layer, ff + k)
                for k in range(T - LAG, T - G):
                    turn(k % G, hs, 1, "hs_ready", on + (k + 1), "hs_turned")
                    if k > T - LAG:
                        wait_count(pe, S["kv_ready"], on + (k - 1))
                    project(k % G, layer + 1, on + k, (k - T + LAG) % 2)
                wait_count(pe, S["kv_ready"], on + (T - G))
                for i in range(G):
                    if i >= 2:
                        wait_count(pe, S["h1T_ready"], ff + (T - G + i - 1))
                    turn(i, h1, i % 2, "h1_ready", m, "h1_turned")
                for i in range(G):
                    if i >= 2:
                        wait_count(pe, S["g_done"], ff + (T - G + i - 1))
                    inner(i, ff + (T - G + i), i % 2)
                    if i:
                        outer(i - 1, layer, ff + (T - G + i - 1))
                outer(G - 1, layer, ff + (T - 1))
                project_all(layer + 1, on + (T - G))


def kernel(**inputs):
    import numpy as np
    import concourse.bacc as bacc
    from concourse import mybir as mb
    from concourse.bass_utils import run_bass_kernel_spmd as run

    a = {k: np.asarray(v) for k, v in inputs.items()}
    turned = lambda w: np.swapaxes(w, -1, -2)
    given = {
        "x": a["x"], "src": a["src"], "dst": a["dst"],
        "wlr": np.concatenate([a["L0_gnn_Wl"], a["L0_gnn_Wr"]], axis=1),
        "bl": a["L0_gnn_b"],
        "wi": a["L1_gnn_Wi"].T, "bi": a["L1_gnn_bi"][None],
        "wqkvs": np.concatenate([turned(a["L1_gnn_W" + c]) for c in "qkvs"], axis=2),
        "bqkvs": np.concatenate([a["L1_gnn_b" + c] for c in "qkvs"], axis=1),
        "wbeta": a["L1_gnn_Wbeta"][:, 0],
        "lng": a["L1_gnn_ln_g"], "lnb": a["L1_gnn_ln_b"],
        "w1t": turned(a["L1_gnn_W1"]), "b1": a["L1_gnn_b1"],
        "w2t": turned(a["L1_gnn_W2"]), "b2": a["L1_gnn_b2"],
        "wo": a["L1_gnn_Wo"].T, "bo": a["L1_gnn_bo"][None],
    }
    nc = bacc.Bacc("TRN2", target_bir_lowering=False, num_devices=1)
    arrays, t_in = {}, {}
    for name, v in given.items():
        v = np.ascontiguousarray(v)
        arrays["in_" + name] = v
        t_in[name] = nc.dram_tensor("in_" + name, v.shape, mb.dt.from_np(v.dtype), kind="ExternalInput").ap()
    out = nc.dram_tensor("out_0", a["x"].shape, mb.dt.float32, kind="ExternalOutput").ap()
    build(nc, t_in, out)
    r = run(nc, [arrays], core_ids=[0])
    return r.results[0]["out_0"]
```
